# Optimizing a Trainium2 kernel written in Bass

```python
import numpy as np
import jax
import jax.numpy as jnp

def _softmax(x, axis=-1):
    return jax.nn.softmax(x, axis=axis)
def _gelu(x):
    return jax.nn.gelu(x, approximate=True)
def _silu(x):
    return jax.nn.silu(x)
def _sigmoid(x):
    return jax.nn.sigmoid(x)
def _layernorm(x, axis=-1, eps=1e-5):
    m = jnp.mean(x, axis=axis, keepdims=True)
    v = jnp.var(x, axis=axis, keepdims=True)
    return (x - m) / jnp.sqrt(v + eps)
def _scatter_add(tgt, idx, src, axis=0):
    return tgt.at[idx].add(src)
def _segment_sum(src, seg, n):
    return jax.ops.segment_sum(src, seg, n)

kernel_name = 'mk_conv_seq_d2_conv_nchw128_c2167e'

def setup_inputs(seed: int = 0):
    np.random.seed(seed)
    _w = jnp.asarray
    def _rec_inputs():
        import jax
        import jax.numpy as jnp
        _gk = jax.random.key(seed)
        x = 7.22e-05 + 1 * jax.random.normal(jax.random.fold_in(_gk, 1), (4, 128, 128, 128), jnp.float32)
        return x
    x = _rec_inputs()
    def _L0_conv_setup():
        import jax, jax.numpy as jnp
        import numpy as np
        WS = 8
        K = 4
        key = jax.random.key(seed)
        ks = jax.random.split(key, 8)
        B, C, H, W = (4, 128, 128, 128)
        d_in, d_state, dt_rank = (256, 16, 8)
        A_init = jnp.tile(jnp.arange(1, d_state + 1, dtype=jnp.float32), (d_in, 1))
        return {'x': jax.random.normal(ks[0], (B, C, H, W), jnp.float32), 'ln_g': jnp.ones((C,), jnp.float32), 'ln_b': jnp.zeros((C,), jnp.float32), 'W_in': jax.random.normal(ks[1], (C, 2 * d_in), jnp.float32) * C ** (-0.5), 'b_in': jnp.zeros((2 * d_in,), jnp.float32), 'conv_w': jax.random.normal(ks[2], (d_in, K), jnp.float32) * 0.3, 'conv_b': jnp.zeros((d_in,), jnp.float32), 'W_x': jax.random.normal(ks[3], (d_in, dt_rank + 2 * d_state), jnp.float32) * d_in ** (-0.5), 'dt_w': jax.random.normal(ks[4], (dt_rank, d_in), jnp.float32) * dt_rank ** (-0.5), 'dt_b': jnp.full((d_in,), -4.0, jnp.float32), 'A_log': jnp.log(A_init), 'D': jnp.ones((d_in,), jnp.float32), 'W_out': jax.random.normal(ks[5], (d_in, C), jnp.float32) * d_in ** (-0.5), 'b_out': jnp.zeros((C,), jnp.float32)}
    _L0_conv_all = _L0_conv_setup()
    _L0_conv_in = {k: v for k, v in _L0_conv_all.items() if k in ('ln_g', 'ln_b', 'W_in', 'b_in', 'conv_w', 'conv_b', 'W_x', 'dt_w', 'dt_b', 'A_log', 'D', 'W_out', 'b_out', )}
    del _L0_conv_all

    def _L1_conv_setup():
        import jax, jax.numpy as jnp
        import numpy as np
        B, D, GX, GY, L = (4, 128, 128, 128, 16)
        GYR = GY // 2 + 1
        key = jax.random.key(seed)
        ks = jax.random.split(key, 6)
        x = jax.random.normal(ks[0], (B, D, GX, GY), dtype=jnp.float32)
        Phi_f_real = jax.random.normal(ks[1], (L, GX, GYR), dtype=jnp.float32) * 0.1
        Phi_f_imag = jax.random.normal(ks[2], (L, GX, GYR), dtype=jnp.float32) * 0.1
        Theta = jax.random.normal(ks[3], (L, D, D), dtype=jnp.float32) * (1.0 / np.sqrt(D))
        ln_gamma = jnp.ones((D,), dtype=jnp.float32)
        ln_beta = jnp.zeros((D,), dtype=jnp.float32)
        W1 = jax.random.normal(ks[4], (2 * D, D), dtype=jnp.float32) * (1.0 / np.sqrt(D))
        b1 = jnp.zeros((2 * D,), dtype=jnp.float32)
        W2 = jax.random.normal(ks[5], (D, 2 * D), dtype=jnp.float32) * (1.0 / np.sqrt(2 * D))
        b2 = jnp.zeros((D,), dtype=jnp.float32)
        return {'x': x, 'Phi_f_real': Phi_f_real, 'Phi_f_imag': Phi_f_imag, 'Theta': Theta, 'ln_gamma': ln_gamma, 'ln_beta': ln_beta, 'W1': W1, 'b1': b1, 'W2': W2, 'b2': b2}
    _L1_conv_all = _L1_conv_setup()
    _L1_conv_in = {k: v for k, v in _L1_conv_all.items() if k in ('Phi_f_real', 'Phi_f_imag', 'Theta', 'ln_gamma', 'ln_beta', 'W1', 'b1', 'W2', 'b2', )}
    del _L1_conv_all

    return {
        "x": x,
        "L0_conv_ln_g": _L0_conv_in["ln_g"],
        "L0_conv_ln_b": _L0_conv_in["ln_b"],
        "L0_conv_W_in": _L0_conv_in["W_in"],
        "L0_conv_b_in": _L0_conv_in["b_in"],
        "L0_conv_conv_w": _L0_conv_in["conv_w"],
        "L0_conv_conv_b": _L0_conv_in["conv_b"],
        "L0_conv_W_x": _L0_conv_in["W_x"],
        "L0_conv_dt_w": _L0_conv_in["dt_w"],
        "L0_conv_dt_b": _L0_conv_in["dt_b"],
        "L0_conv_A_log": _L0_conv_in["A_log"],
        "L0_conv_D": _L0_conv_in["D"],
        "L0_conv_W_out": _L0_conv_in["W_out"],
        "L0_conv_b_out": _L0_conv_in["b_out"],
        "L1_conv_Phi_f_real": _L1_conv_in["Phi_f_real"],
        "L1_conv_Phi_f_imag": _L1_conv_in["Phi_f_imag"],
        "L1_conv_Theta": _L1_conv_in["Theta"],
        "L1_conv_ln_gamma": _L1_conv_in["ln_gamma"],
        "L1_conv_ln_beta": _L1_conv_in["ln_beta"],
        "L1_conv_W1": _L1_conv_in["W1"],
        "L1_conv_b1": _L1_conv_in["b1"],
        "L1_conv_W2": _L1_conv_in["W2"],
        "L1_conv_b2": _L1_conv_in["b2"],
    }

def reference(x, L0_conv_ln_g, L0_conv_ln_b, L0_conv_W_in, L0_conv_b_in, L0_conv_conv_w, L0_conv_conv_b, L0_conv_W_x, L0_conv_dt_w, L0_conv_dt_b, L0_conv_A_log, L0_conv_D, L0_conv_W_out, L0_conv_b_out, L1_conv_Phi_f_real, L1_conv_Phi_f_imag, L1_conv_Theta, L1_conv_ln_gamma, L1_conv_ln_beta, L1_conv_W1, L1_conv_b1, L1_conv_W2, L1_conv_b2):
    import jax
    import jax.numpy as jnp
    def _L0_conv_ref(x, ln_g, ln_b, W_in, b_in, conv_w, conv_b, W_x, dt_w, dt_b, A_log, D, W_out, b_out):
        import jax, jax.numpy as jnp
        import numpy as np
        WS = 8
        K = 4
        B, C, H, W = x.shape
        nh, nw = (H // WS, W // WS)
        L = WS * WS
        d_in = W_in.shape[1] // 2
        dt_rank = dt_w.shape[0]
        d_state = A_log.shape[1]
        t = x.reshape(B, C, nh, WS, nw, WS).transpose(0, 2, 4, 3, 5, 1).reshape(-1, L, C)
        mu = t.mean(-1, keepdims=True)
        var = t.var(-1, keepdims=True)
        tn = (t - mu) * jax.lax.rsqrt(var + 1e-05) * ln_g + ln_b
        xz = tn @ W_in + b_in
        xi, z = (xz[..., :d_in], xz[..., d_in:])
        xp = jnp.pad(xi, ((0, 0), (K - 1, 0), (0, 0)))
        xc = sum((xp[:, k:k + L, :] * conv_w[:, k] for k in range(K))) + conv_b
        xc = jax.nn.silu(xc)
        dbl = xc @ W_x
        dr = dbl[..., :dt_rank]
        Bm = dbl[..., dt_rank:dt_rank + d_state]
        Cm = dbl[..., dt_rank + d_state:]
        delta = jax.nn.softplus(dr @ dt_w + dt_b)
        A = -jnp.exp(A_log)

        def step(h, inputs):
            d_t, B_t, C_t, x_t = inputs
            dA = jnp.exp(d_t[:, :, None] * A)
            h = dA * h + (d_t * x_t)[:, :, None] * B_t[:, None, :]
            y = jnp.einsum('nds,ns->nd', h, C_t)
            return (h, y)
        n = xc.shape[0]
        h0 = jnp.zeros((n, d_in, d_state), xc.dtype)
        xs = (delta.transpose(1, 0, 2), Bm.transpose(1, 0, 2), Cm.transpose(1, 0, 2), xc.transpose(1, 0, 2))
        _, ys = jax.lax.scan(step, h0, xs)
        y = ys.transpose(1, 0, 2) + xc * D
        y = y * jax.nn.silu(z)
        out = y @ W_out + b_out
        out = out.reshape(B, nh, nw, WS, WS, C).transpose(0, 5, 1, 3, 2, 4).reshape(B, C, H, W)
        return out + x

    def _L1_conv_ref(x, Phi_f_real, Phi_f_imag, Theta, ln_gamma, ln_beta, W1, b1, W2, b2):
        import jax, jax.numpy as jnp
        import numpy as np
        B, D, GX, GY, L = (4, 128, 128, 128, 16)
        GYR = GY // 2 + 1
        gx, gy = (x.shape[-2], x.shape[-1])
        mu = jnp.mean(x, axis=1, keepdims=True)
        var = jnp.var(x, axis=1, keepdims=True)
        z = (x - mu) / jnp.sqrt(var + 1e-05)
        z = z * ln_gamma[None, :, None, None] + ln_beta[None, :, None, None]
        Xf = jnp.fft.rfft2(z, axes=(-2, -1))
        Phi = Phi_f_real + 1j * Phi_f_imag
        Uf = Xf[:, :, None, :, :] * jnp.conj(Phi)[None, None]
        U = jnp.fft.irfft2(Uf, s=(gx, gy), axes=(-2, -1))
        S = jnp.einsum('bdlxy,lhd->bhxy', U, Theta)
        H = jnp.einsum('bdxy,hd->bhxy', S, W1) + b1[None, :, None, None]
        H = jax.nn.gelu(H, approximate=False)
        out = jnp.einsum('bhxy,dh->bdxy', H, W2) + b2[None, :, None, None]
        return x + out

    def _gn(v, G=32, eps=1e-5):
        B_, C_, H_, W_ = v.shape
        g = v.reshape(B_, G, C_ // G, H_, W_)
        m = jnp.mean(g, axis=(2, 3, 4), keepdims=True)
        s = jnp.var(g, axis=(2, 3, 4), keepdims=True)
        return ((g - m) / jnp.sqrt(s + eps)).reshape(v.shape)

    def _ln_c(v, eps=1e-6):
        m = jnp.mean(v, axis=1, keepdims=True)
        s = jnp.var(v, axis=1, keepdims=True)
        return (v - m) / jnp.sqrt(s + eps)

    def _ln_t(v, eps=1e-5):
        m = jnp.mean(v, axis=-1, keepdims=True)
        s = jnp.var(v, axis=-1, keepdims=True)
        return (v - m) / jnp.sqrt(s + eps)

    def _to_tokens(v):
        B_, C_, H_, W_ = v.shape
        return v.reshape(B_, C_, H_ * W_).transpose(0, 2, 1)
    def _from_tokens(t, like):
        B_, C_, H_, W_ = like.shape
        return t.transpose(0, 2, 1).reshape(B_, C_, H_, W_)

    x = _L0_conv_ref(x, L0_conv_ln_g, L0_conv_ln_b, L0_conv_W_in, L0_conv_b_in, L0_conv_conv_w, L0_conv_conv_b, L0_conv_W_x, L0_conv_dt_w, L0_conv_dt_b, L0_conv_A_log, L0_conv_D, L0_conv_W_out, L0_conv_b_out)
    x = _L1_conv_ref(x, L1_conv_Phi_f_real, L1_conv_Phi_f_imag, L1_conv_Theta, L1_conv_ln_gamma, L1_conv_ln_beta, L1_conv_W1, L1_conv_b1, L1_conv_W2, L1_conv_b2)
    return x


_drawn_inputs = setup_inputs


def setup_inputs(seed=0):
    import zlib

    import numpy as np

    out = dict(_drawn_inputs(seed))
    spreads = {'L0_conv_ln_g': (1.0, 0.2),
     'L0_conv_ln_b': (0.0, 0.1),
     'L0_conv_b_in': (0.0, 0.1),
     'L0_conv_conv_b': (0.0, 0.1),
     'L0_conv_dt_b': (-4.0, 0.2),
     'L0_conv_D': (1.0, 0.2),
     'L0_conv_b_out': (0.0, 0.1),
     'L1_conv_ln_gamma': (1.0, 0.2),
     'L1_conv_ln_beta': (0.0, 0.1),
     'L1_conv_b1': (0.0, 0.1),
     'L1_conv_b2': (0.0, 0.1)}
    factors = {}
    for name, (base, spread) in spreads.items():
        noise = np.random.default_rng([zlib.crc32(name.encode()), seed]).standard_normal(out[name].shape)
        drawn = base * np.exp(spread * noise) if base else spread * noise
        out[name] = jnp.asarray(drawn.astype(out[name].dtype))
    for name, factor in factors.items():
        out[name] = (out[name] * factor).astype(out[name].dtype)
    return out
```

```python
from contextlib import ExitStack

import concourse.bass as bass
import numpy as np
from concourse import mybir

ALU = mybir.AluOpType
ACT = mybir.ActivationFunctionType
F32 = mybir.dt.float32
BF16 = mybir.dt.bfloat16

P = 128
B = 4
C = 128
H = W = 128
WS = 8
WT = WS * WS
NW = W // WS
BT = WS * W
KB = H // WS
NM = B * KB
HT = BT // 2
HWN = NW // 2
DI = 256
NS = 16
RANK = 8
K = 4
NSTEP = 32
L = 16
KY = W // 2 + 1
EPS = 1e-5
CLIP = 30.0

JOBS = [(0, "mean0", "front"), (1, "mean1", "front"), (3, "turn10", "back"), (4, "var0", "front"),
        (5, "turn11", "back"), (6, "var1", "front"), (8, "conv00", "front"), (9, "conv10", "front"),
        (10, "conv01", "front"), (11, "conv11", "front"), (12, "z00", "front"), (13, "z10", "front"),
        (14, "z01", "front"), (15, "z11", "front"), (17, "bc", "front"), (18, "dt00", "front"),
        (19, "dt10", "front"), (20, "dt01", "front"), (21, "dt11", "front"), (22, "rows", "front"),
        (23, "out0", "back"), (24, "out1", "back"), (25, "turn00", "scan"), (26, "turn01", "scan"),
        (29, "fy0", "back"), (30, "fy1", "back")]


class Slot:

    def __init__(self, m, front, scan, back, before):
        self.m, self.front, self.scan, self.back = m, front, scan, back
        on = {"front": front, "scan": scan, "back": back}
        mine = [j for j in JOBS if on[j[2]]]
        self.before = {j[1]: before + i for i, j in enumerate(mine)}
        self.at = {j[0]: j[1] for j in mine}
        self.count = len(mine)
        self.start = before


def slots(eng, body, blocks):
    first = Slot(-1, True, False, False, 0)
    body(first, 1)
    second = Slot(0, True, True, False, first.count)
    body(second, 0)
    base = first.count + second.count
    per = len(JOBS)
    with eng.Fori(0, (blocks - 2) // 2) as j:
        for i in range(2):
            body(Slot(j * 2 + 1 + i, True, True, True, j * (2 * per) + base + per * i), 1 - i)
    base += per * (blocks - 2)
    last = Slot(blocks - 1, False, True, True, base)
    body(last, (blocks - 1) % 2)
    body(Slot(blocks, False, False, True, base + last.count), blocks % 2)


def need(eng, sem, value):
    if isinstance(value, int) and value <= 0:
        return
    eng.wait_ge(sem, value)


def conv_seq_program(nc, a, out, blocks=NM, layer1=True):
    x1_dram = nc.dram_tensor("x1_rows", [B * H, W, C], F32).ap()
    y_dram = nc.dram_tensor("row_spectra", [P + 1, H, B, C], F32).ap()
    phi_dram = nc.dram_tensor("filters", [KY, 3 * L * P], F32).ap()
    t_dram = nc.dram_tensor("column_sums", [P + 1, H, B, C], F32).ap()

    with ExitStack() as whole:
        wt = weights(nc, whole)
        setup(nc, a, wt, phi_dram, y_dram)
        layer0(nc, a, wt, x1_dram, y_dram, blocks)
        if layer1:
            spectral(nc, wt, y_dram, phi_dram, t_dram)
            mlp(nc, wt, t_dram, x1_dram, out)


def weights(nc, ctx):
    def sb(name, shape, dt=F32):
        return ctx.enter_context(nc.sbuf_tensor(name, shape, dt))

    return {
        "ident": sb("ident", [P, P]), "identb": sb("identb", [P, P], BF16),
        "mean_w": sb("mean_w", [P, P]),
        "select": sb("select", [96, 2 * NS, P], BF16),
        "tap_w": sb("tap_w", [P, K, DI]),
        "z_w": sb("z_w", [P, DI]), "z_b": sb("z_b", [P, 2]),
        "xc_b": sb("xc_b", [P, 2]), "edge": sb("edge", [P, 2, K - 1]),
        "bc_w": sb("bc_w", [P, 2, 2 * NS]), "dt_w": sb("dt_full_w", [P, 2, DI]),
        "dt_b": sb("dt_bias", [P, 2]), "neg_a": sb("neg_a", [P, 2, NS]),
        "diag_d": sb("diag_d", [P, 2, P]), "out_w": sb("out_w", [P, 2, C]),
        "out_b": sb("out_b_rows", [P, C]), "fy": sb("fy", [P, P]),
        "fx": sb("fx", [P, 4, P]), "ix": sb("ix", [P, 3, P]), "iy": sb("iy", [P, P]),
        "theta": sb("theta_t", [P, L, C]), "gamma": sb("gamma", [P, 1]), "dc": sb("dc", [P, 1]),
        "w1": sb("w1_t", [P, 2, P]), "b1": sb("b1_cols", [P, 2]),
        "w2": sb("w2_t", [P, 2, C]), "b2": sb("b2_col", [P, 1]),
    }


def setup(nc, a, wt, phi_dram, y_dram):
    with ExitStack() as ctx:
        def sb(name, shape, dt=F32):
            return ctx.enter_context(nc.sbuf_tensor(name, shape, dt))

        def sem(name):
            return ctx.enter_context(nc.semaphore(name))

        w_in = sb("w_in", [P, 2 * DI])
        gain = sb("gain", [P, 1])
        shift = sb("shift", [P, 1])
        b_in = sb("b_in", [P, 4])
        conv_w = sb("conv_w", [P, 2, K])
        conv_b = sb("conv_b", [P, 2])
        w_x = sb("w_x", [P, 2, RANK + 2 * NS])
        rank_w = sb("rank_w", [RANK, 2, P])
        dt_low = sb("dt_low", [RANK, DI])
        a_log = sb("a_log", [P, 2, NS])
        d_col = sb("d_col", [P, 2])
        bo_col = sb("bo_col", [P, 1])
        w1_rows = sb("w1_rows", [P, 2, C])
        w2_rows = sb("w2_rows", [P, DI])
        th_rows = sb("th_rows", [P, L, C])
        beta = sb("beta", [P, 1])
        phi = sb("phi", [P, 3, L, KY])
        phi_i = sb("phi_i", [P, L, KY])
        zeros = sb("zeros", [P, B * C])
        phi_t = sb("phi_t", [KY, 3 * L, P])
        b_fold = sb("b_fold", [P, 4])
        tap_sum = sb("tap_sum", [P, 2, K])
        edge0 = sb("edge0", [P, 2])
        ps = [ctx.enter_context(nc.psum_tensor(f"set{i}", [P, 512], F32)) for i in range(2)]

        loads = [
            (w_in[:], a["W_in"]), (gain[:], a["ln_g"].rearrange("(p o) -> p o", o=1)),
            (shift[:], a["ln_b"].rearrange("(p o) -> p o", o=1)),
            (b_in[:], a["b_in"].rearrange("(k p) -> p k", p=P)),
            (conv_w[:], a["conv_w"].rearrange("(k p) t -> p k t", p=P)),
            (conv_b[:], a["conv_b"].rearrange("(k p) -> p k", p=P)),
            (w_x[:], a["W_x"].rearrange("(k p) n -> p k n", p=P)), (dt_low[:], a["dt_w"]),
            (wt["dt_b"][:], a["dt_b"].rearrange("(k p) -> p k", p=P)),
            (a_log[:], a["A_log"].rearrange("(k p) n -> p k n", p=P)),
            (d_col[:], a["D"].rearrange("(k p) -> p k", p=P)),
            (wt["out_w"][:], a["W_out"].rearrange("(k p) n -> p k n", p=P)),
            (bo_col[:], a["b_out"].rearrange("(p o) -> p o", o=1)),
            (w1_rows[:], a["W1"].rearrange("(k p) n -> p k n", p=P)), (w2_rows[:], a["W2"]),
            (th_rows[:], a["Theta"].rearrange("l h d -> h l d")),
            (wt["gamma"][:], a["ln_gamma"].rearrange("(p o) -> p o", o=1)),
            (beta[:], a["ln_beta"].rearrange("(p o) -> p o", o=1)),
            (wt["b1"][:], a["b1"].rearrange("(k p) -> p k", p=P)),
            (wt["b2"][:], a["b2"].rearrange("(p o) -> p o", o=1)),
            (phi[:, 0], a["Phi_f_real"].rearrange("l x y -> x l y")),
            (phi_i[:], a["Phi_f_imag"].rearrange("l x y -> x l y")),
            (wt["fy"][:], a["fy"]), (wt["fx"][:], a["fx"]), (wt["ix"][:], a["ix"]), (wt["iy"][:], a["iy"]),
        ]
        loaded, zeroed, consts = sem("loaded"), sem("zeroed"), sem("consts")
        gained, phi_made, exped = sem("gained"), sem("phi_made"), sem("exped")
        turned, taken, folded, small = sem("turned"), sem("taken"), sem("folded"), sem("small")
        stored = sem("filters_stored")

        turns = []

        def turn(dst, parts):
            turns.append((dst, parts))

        for t in range(K):
            turn(("tap", t), [(k * P, P, P, conv_w[:, k, t:t + 1].to_broadcast([P, P]), wt["ident"][:], True)
                              for k in range(2)])
        turn(("fold",), [(k, 1, P, w_in[:, k * P:(k + 1) * P], shift[:], False) for k in range(4)])
        turn(("bout",), [(0, P, P, bo_col[:, 0:1].to_broadcast([P, P]), wt["ident"][:], True)])
        turn(("rank",), [(k * P, P, RANK, w_x[:, k, 0:RANK], wt["ident"][:], True) for k in range(2)])
        turn(("dt",), [(k * DI, DI, P, rank_w[:, k, :], dt_low[:], False) for k in range(2)])
        turn(("w1",), [(k * P, P, P, w1_rows[:, k, :], wt["ident"][:], True) for k in range(2)])
        turn(("w2",), [(k * P, P, P, w2_rows[:, k * P:(k + 1) * P], wt["ident"][:], True) for k in range(2)])
        for g in range(L // 4):
            turn(("theta", g), [(i * P, P, P, th_rows[:, 4 * g + i, :], wt["ident"][:], True) for i in range(4)])
        for g in range(3 * L // 4):
            turn(("phi", g), [(i * P, P, KY, phi[:, (4 * g + i) // L, (4 * g + i) % L, :], wt["ident"][:], True)
                              for i in range(4)])
        RANKED = [i for i, t in enumerate(turns) if t[0] == ("rank",)][0]

        block = ctx.enter_context(nc.Block())

        @block.sync
        def _(sp):
            for dst, src in loads:
                with nc.allow_non_contiguous_dma(reason="weights, once"):
                    sp.dma_start(dst, src).then_inc(loaded, 16)
            sp.wait_ge(taken, len(turns))
            sp.dma_start(phi_dram, phi_t[:].rearrange("k n x -> k (n x)")).then_inc(stored, 16)
            sp.wait_ge(zeroed, 4)
            sp.dma_start(y_dram[P].rearrange("x b d -> x (b d)"), zeros[:]).then_inc(stored, 16)
            sp.wait_ge(stored, 32)

        @block.gpsimd
        def _(pool):
            pool.memset(wt["ident"][:], 0.0).then_inc(zeroed, 1)
            pool.memset(wt["identb"][:], 0.0).then_inc(zeroed, 1)
            pool.memset(wt["select"][:], 0.0).then_inc(zeroed, 1)
            pool.memset(zeros[:], 0.0).then_inc(zeroed, 1)
            pool.memset(wt["mean_w"][:], 1.0 / C).then_inc(consts, 1)
            pool.wait_ge(zeroed, 3)
            for t in ("ident", "identb"):
                pool.affine_select(out=wt[t][:], in_=wt[t][:], compare_op=ALU.not_equal, fill=1.0, base=0,
                                   pattern=[[-1, P]], channel_multiplier=1).then_inc(consts, 1)
            for part in range(3):
                pool.affine_select(out=wt["select"][:], in_=wt["select"][:], compare_op=ALU.not_equal, fill=1.0,
                                   base=-2 * NS * part, pattern=[[-1, 2 * NS], [0, P]],
                                   channel_multiplier=1).then_inc(consts, 1)
                pool.wait_ge(consts, 4 + part)

        @block.scalar
        def _(act):
            act.wait_ge(loaded, 16 * len(loads))
            act.activation(wt["neg_a"][:], a_log[:], ACT.Exp).then_inc(exped, 1)

        @block.vector
        def _(dve):
            dve.wait_ge(loaded, 16 * len(loads))
            dve.wait_ge(consts, 6)
            dve.tensor_scalar(wt["z_w"][:], w_in[:, DI:2 * DI], gain[:, 0:1], None, ALU.mult)
            dve.tensor_copy(wt["bc_w"][:], w_x[:, :, RANK:])
            dve.tensor_scalar(wt["dc"][:], beta[:], float(H * W), None, ALU.mult)
            for k in range(2):
                dve.tensor_scalar(wt["diag_d"][:, k, :], wt["ident"][:], d_col[:, k:k + 1], None, ALU.mult)
            dve.tensor_tensor(phi[:, 1], phi[:, 0], phi_i[:], ALU.add)
            dve.tensor_tensor(phi[:, 2], phi[:, 0], phi_i[:], ALU.subtract).then_inc(phi_made, 1)
            n = 0
            dve.tensor_copy(tap_sum[:, :, 0], conv_w[:, :, 0]).then_inc(small, 1)
            for t in range(1, K):
                n += 1
                dve.wait_ge(small, n)
                dve.tensor_tensor(tap_sum[:, :, t], tap_sum[:, :, t - 1], conv_w[:, :, t], ALU.add).then_inc(small, 1)
            dve.wait_ge(exped, 1)
            dve.tensor_scalar(wt["neg_a"][:], wt["neg_a"][:], -1.0, None, ALU.mult)
            for i, (dst, _) in enumerate(turns):
                dve.wait_ge(turned, i + 1)
                bank = ps[i % 2]
                if dst[0] == "tap":
                    last = dve.scalar_tensor_tensor(wt["tap_w"][:, dst[1], :], bank[:, 0:DI], gain[:, 0:1],
                                                    w_in[:, 0:DI], ALU.mult, ALU.mult)
                elif dst[0] == "fold":
                    last = dve.tensor_tensor(b_fold[:], bank[:, 0:4], b_in[:], ALU.add)
                elif dst[0] == "bout":
                    last = dve.tensor_copy(wt["out_b"][:], bank[:, 0:P])
                elif dst[0] == "rank":
                    last = dve.tensor_copy(rank_w[:].rearrange("r k p -> r (k p)"), bank[0:RANK, 0:DI])
                elif dst[0] == "dt":
                    last = dve.tensor_copy(wt["dt_w"][:].rearrange("p k n -> p (k n)"), bank[:, :])
                elif dst[0] in ("w1", "w2"):
                    last = dve.tensor_copy(wt[dst[0]][:].rearrange("p k n -> p (k n)"), bank[:, 0:DI])
                elif dst[0] == "theta":
                    g = 4 * dst[1]
                    last = dve.tensor_copy(wt["theta"][:, g:g + 4, :].rearrange("p l h -> p (l h)"), bank[:, :])
                else:
                    g = 4 * dst[1]
                    last = dve.tensor_copy(phi_t[:, g:g + 4, :].rearrange("p l h -> p (l h)"), bank[0:KY, :])
                last.then_inc(taken, 1)
            n += 1
            dve.wait_ge(small, n)
            dve.wait_ge(taken, len(turns))
            dve.tensor_copy(wt["z_b"][:], b_fold[:, 2:4])
            dve.tensor_tensor(edge0[:], tap_sum[:, :, K - 1], b_fold[:, 0:2], ALU.mult).then_inc(small, 1)
            n += 1
            dve.wait_ge(small, n)
            dve.tensor_tensor(wt["xc_b"][:], edge0[:], conv_b[:], ALU.add)
            for t in range(K - 1):
                dve.scalar_tensor_tensor(wt["edge"][:, :, t], tap_sum[:, :, K - 2 - t], -1.0, b_fold[:, 0:2],
                                         ALU.mult, ALU.mult)

        @block.tensor
        def _(pe):
            pe.wait_ge(loaded, 16 * len(loads))
            pe.wait_ge(consts, 6)
            pe.wait_ge(phi_made, 1)
            for i, (_, parts) in enumerate(turns):
                if i >= 2:
                    pe.wait_ge(taken, i - 1)
                if turns[i][0] == ("dt",):
                    pe.wait_ge(taken, RANKED + 1)
                for col, n, rows, lhs, rhs, tr in parts:
                    last = pe.matmul(ps[i % 2][0:rows, col:col + n], lhs, rhs, start=True, stop=True, is_transpose=tr)
                last.then_inc(turned, 1)


def layer0(nc, a, wt, x1_dram, y_dram, blocks):
    with ExitStack() as ctx:
        def sb(name, shape, dt=F32):
            return ctx.enter_context(nc.sbuf_tensor(name, shape, dt))

        def psum(name, shape):
            return ctx.enter_context(nc.psum_tensor(name, shape, F32))

        def sem(name):
            return ctx.enter_context(nc.semaphore(name))

        x_in = sb("x_in", [P, BT])
        x_res = sb("x_res", [P, BT])
        temp = sb("temp", [P, 2 * BT])
        cent, sq = temp[:, 0:BT], temp[:, BT:2 * BT]
        tn = sb("tn", [P, BT])
        xc = [sb(f"xc{i}", [P, 2, BT]) for i in range(2)]
        zs = [sb(f"zs{i}", [P, 2, BT]) for i in range(2)]
        delta = [sb(f"delta{i}", [P, 2, BT]) for i in range(2)]
        du = [sb(f"du{i}", [P, 2, BT]) for i in range(2)]
        bc3 = sb("bc3", [P, BT // P, 96], BF16)
        rest = sb("rest", [P, 2, BT // P, 2 * NS])
        rows = [sb(f"rows{i}", [96, BT], BF16) for i in range(2)]
        b_all = [sb(f"b_all{i}", [P, 2, HT]) for i in range(2)]
        NR = 4
        decay = [sb(f"decay{i}", [P, 2, HWN, WT]) for i in range(NR)]
        drive = [sb(f"drive{i}", [P, 2, HT]) for i in range(2)]
        state = [sb(f"state{i}", [P, 2 * HT]) for i in range(2)]
        prod = [sb(f"prod{i}", [P, 2 * HT]) for i in range(2)]
        y_tok = [sb(f"y_tok{i}", [P, 4, DI]) for i in range(2)]
        gated = sb("gated", [P, 2, BT])
        x1 = sb("x1", [P, WS, C])
        stats = sb("stats", [P, WS, 6])
        mv = sb("mv", [P, WS, 2])
        rstd1 = sb("rstd1", [P, WS])
        z1 = sb("z1", [P, WS, C])
        yo = sb("yo", [P, WS, C])

        c_all = [psum(f"c_all{i}", [P, 2 * HT]) for i in range(2)]
        b_bank = psum("b_bank", [P, HT])
        y_acc = psum("y_acc", [P, 4, DI])
        misc = psum("misc", [P, 512])
        misc_b = misc[:].bitcast(BF16)

        names = """x_ready xres_ready x1_stored yo_stored job_full job_taken sq_done rstd_done tn_done
            edge_done silu_done split_done clip_done softplus_done delta_done du_done c_full b_full b_copied
            decay_done drive_done scan_done prod_done added y_copied stats_done mv_done rstd1_done z1_done
            yo_done zeroed""".split()
        s = {n: sem(n) for n in names}

        def full(eng, S, name):
            need(eng, s["job_full"], S.before[name] + 1)

        def taken(eng, S, name):
            need(eng, s["job_taken"], S.before[name] + 1)

        block = ctx.enter_context(nc.Block())

        xv = a["x"].rearrange("b c (k r) w -> b k c (r w)", r=WS)
        yv = y_dram[0:P].rearrange("f (k r) b d -> k b f r d", r=WS)

        @block.sync
        def _(sp):
            def place(M):
                if isinstance(M, int):
                    return M // KB, M % KB
                return sp.snap(M // KB), sp.snap(M % KB)

            def load_x(dst, at, done):
                sp.dma_start(dst[:], xv[bass.ds(at[0], 1), bass.ds(at[1], 1)]
                             .rearrange("o q c n -> (o q c) n")).then_inc(done, 16)

            def body(m, scan=True, back=True, more=True):
                before, after = place(m - 1), place(m + 2)
                if back:
                    need(sp, s["x1_stored"], m * 16)
                    load_x(x_res, before, s["xres_ready"])
                if more:
                    need(sp, s["sq_done"], (m + 2) * 2)
                    load_x(x_in, after, s["x_ready"])
                if back:
                    need(sp, s["stats_done"], m)
                    sp.dma_start(x1_dram[bass.ds((m - 1) * WS, WS)].rearrange("r w c -> w r c"),
                                 x1[:]).then_inc(s["x1_stored"], 16)
                    need(sp, s["yo_done"], m)
                    sp.dma_start(yv[bass.ds(before[1], 1), bass.ds(before[0], 1)].rearrange("o q f r d -> (o q f) r d"),
                                 yo[:]).then_inc(s["yo_stored"], 16)

            sp.sem_inc(s["x1_stored"], 16)
            sp.sem_inc(s["yo_stored"], 16)
            load_x(x_in, (0, 0), s["x_ready"])
            body(-1, back=False)
            body(0, back=False)
            with sp.Fori(1, blocks - 2) as m:
                body(m)
            body(blocks - 2, more=False)
            body(blocks - 1, more=False)
            body(blocks, more=False)
            sp.wait_ge(s["x1_stored"], 16 * blocks + 16)
            sp.wait_ge(s["yo_stored"], 16 * blocks + 16)

        @block.tensor
        def _(pe):
            def broadcast(M, p, g):
                q, st = g // 8, 2 * (g % 8)
                G = M * 16 + g
                need(pe, s["prod_done"], G * 2 - 2)
                for i in range(2):
                    mm = pe.matmul(c_all[g % 2][:, i * HT:(i + 1) * HT], wt["select"][:, NS + st + i, :],
                                   rows[p][:, q * HT:(q + 1) * HT], start=True, stop=True)
                mm.then_inc(s["c_full"], 1)
                for i in range(2):
                    need(pe, s["b_copied"], G * 2 + i)
                    pe.matmul(b_bank[:], wt["select"][:, st + i, :], rows[p][:, q * HT:(q + 1) * HT],
                              start=True, stop=True).then_inc(s["b_full"], 1)

            def add_states(M, p, n):
                q, hf = n // 16, n % 2
                if n % 16 == 0:
                    need(pe, s["y_copied"], M * 2 + q)
                    need(pe, s["silu_done"], M * 2 + 1)
                    for g in range(4):
                        for k in range(2):
                            pe.matmul(y_acc[:, g, k * P:(k + 1) * P], xc[p][:, k, q * HT + g * P:q * HT + (g + 1) * P],
                                      wt["diag_d"][:, k, :], start=(g % 2 == 0 and k == 0), stop=False,
                                      skip_group_check=True)
                need(pe, s["prod_done"], M * 32 + n + 1)
                for i in range(2):
                    for g in range(4):
                        mm = pe.matmul(y_acc[:, g, hf * P:(hf + 1) * P],
                                       prod[n % 2][:, i * HT + g * P:i * HT + (g + 1) * P], wt["ident"][:],
                                       start=False, stop=False, is_transpose=True, skip_group_check=True)
                mm.then_inc(s["added"], 1)

            def job(S, p, name):
                m, kind, f = S.m, name.rstrip("01"), 1 - p
                need(pe, s["job_taken"], S.before[name])
                if kind == "mean":
                    q = int(name[-1])
                    need(pe, s["x_ready"], (m + 2) * 16)
                    mm = pe.matmul(misc[:].rearrange("p (r c) -> p r c", r=WS), wt["mean_w"][:],
                                   x_in[:].rearrange("p (r q c) -> p r q c", r=WS, q=2)[:, :, q, :],
                                   start=True, stop=True)
                elif kind == "var":
                    q = int(name[-1])
                    need(pe, s["sq_done"], (m + 1) * 2 + q + 1)
                    mm = pe.matmul(misc[:], wt["mean_w"][:], sq[:, q * HT:(q + 1) * HT], start=True, stop=True)
                elif kind == "conv":
                    hf, q = int(name[-2]), int(name[-1])
                    need(pe, s["tn_done"], (m + 1) * 2 + q + 1)
                    o = misc[:].rearrange("p (w t) -> p w t", t=WT)
                    v = tn[:, q * HT:(q + 1) * HT].rearrange("p (w t) -> p w t", t=WT)
                    for k in range(K):
                        mm = pe.matmul(o[:, :, k:WT], wt["tap_w"][:, K - 1 - k, hf * P:(hf + 1) * P],
                                       v[:, :, 0:WT - k], start=(k == 0), stop=(k == K - 1), skip_group_check=True)
                elif kind == "z":
                    hf, q = int(name[-2]), int(name[-1])
                    mm = pe.matmul(misc[:], wt["z_w"][:, hf * P:(hf + 1) * P], tn[:, q * HT:(q + 1) * HT],
                                   start=True, stop=True)
                elif kind == "bc":
                    need(pe, s["silu_done"], (m + 1) * 2 + 1)
                    for g in range(BT // P):
                        for k in range(2):
                            mm = pe.matmul(misc[:, g * 32:(g + 1) * 32], xc[f][:, k, g * P:(g + 1) * P],
                                           wt["bc_w"][:, k, :], start=(g == 0 and k == 0), stop=(k == 1),
                                           skip_group_check=True)
                elif kind == "dt":
                    hf, q = int(name[-2]), int(name[-1])
                    for k in range(2):
                        mm = pe.matmul(misc[:], wt["dt_w"][:, k, hf * P:(hf + 1) * P],
                                       xc[f][:, k, q * HT:(q + 1) * HT], start=(k == 0), stop=(k == 1))
                elif kind == "rows":
                    for g in range(BT // P):
                        mm = pe.matmul(misc_b[0:96, g * P:(g + 1) * P], bc3[:, g, :], wt["identb"][:],
                                       start=True, stop=True, is_transpose=True)
                elif kind == "turn":
                    q, hf = int(name[-2]), int(name[-1])
                    M = m if q == 0 else m - 1
                    need(pe, s["y_copied"], M * 2 + q + 1)
                    for g in range(4):
                        mm = pe.matmul(misc[:, g * P:(g + 1) * P], y_tok[q][:, g, hf * P:(hf + 1) * P], wt["ident"][:],
                                       start=True, stop=True, is_transpose=True)
                elif kind == "out":
                    q = int(name[-1])
                    need(pe, s["xres_ready"], m * 16)
                    for r in range(4):
                        row = 4 * q + r
                        o = misc[:, r * P:(r + 1) * P]
                        for k in range(2):
                            pe.matmul(o, gated[:, k, row * W:(row + 1) * W], wt["out_w"][:, k, :], start=(r == 0 and k == 0), stop=False, skip_group_check=True)
                        mm = pe.matmul(o, x_res[:, row * W:(row + 1) * W], wt["ident"][:], start=False, stop=(r == 3),
                                       is_transpose=True, skip_group_check=True)
                elif kind == "fy":
                    q = int(name[-1])
                    need(pe, s["z1_done"], m)
                    mm = pe.matmul(misc[:], wt["fy"][:], z1[:, 4 * q:4 * q + 4, :].rearrange("p r c -> p (r c)"),
                                   start=True, stop=True)
                mm.then_inc(s["job_full"], 1)

            def body(S, p):
                for n in range(NSTEP):
                    if n % 2 == 0 and n < NSTEP - 2 and S.scan:
                        broadcast(S.m, p, n // 2 + 1)
                    if n == NSTEP - 2 and S.front:
                        taken(pe, S, "rows")
                        broadcast(S.m + 1, 1 - p, 0)
                    if n >= 2 and S.scan:
                        add_states(S.m, p, n - 2)
                    if n < 2 and S.back:
                        add_states(S.m - 1, 1 - p, NSTEP - 2 + n)
                    if n in S.at:
                        job(S, p, S.at[n])

            slots(pe, body, blocks)

        @block.scalar
        def _(act):
            def copy_b(M, g):
                G = M * 16 + g
                need(act, s["drive_done"], G * 2 - 2)
                for i in range(2):
                    need(act, s["b_full"], G * 2 + i + 1)
                    act.activation(b_all[g % 2][:, i, :], b_bank[:], ACT.Copy).then_inc(s["b_copied"], 1)

            def decays(M, p, n):
                q, st, hf = n // 16, 2 * ((n % 16) // 2), n % 2
                need(act, s["zeroed"], 1)
                need(act, s["delta_done"], M + 1)
                need(act, s["scan_done"], M * 32 + n + 1 - NR)
                for i in range(2):
                    last = act.activation(
                        decay[n % NR][:, i, :, 1:WT],
                        delta[p][:, hf, q * HT:(q + 1) * HT].rearrange("p (w t) -> p w t", t=WT)[:, :, 1:WT],
                        ACT.Exp, scale=wt["neg_a"][:, hf, st + i:st + i + 1])
                last.then_inc(s["decay_done"], 1)

            def chain(S, n, m, f):
                if n in (2, 3):
                    q = n - 2
                    taken(act, S, f"mean{q}")
                    act.activation(sq[:, q * HT:(q + 1) * HT], cent[:, q * HT:(q + 1) * HT],
                                   ACT.Square).then_inc(s["sq_done"], 1)
                elif n in (5, 7):
                    q = (n - 5) // 2
                    full(act, S, f"var{q}")
                    act.activation(sq[:, q * HT:(q + 1) * HT], misc[:], ACT.Ln,
                                   bias=EPS).then_inc(s["job_taken"], 1)
                elif n in (6, 8):
                    q = (n - 6) // 2
                    taken(act, S, f"var{q}")
                    act.activation(sq[:, q * HT:(q + 1) * HT], sq[:, q * HT:(q + 1) * HT], ACT.Exp,
                                   scale=-0.5).then_inc(s["rstd_done"], 1)
                elif 9 <= n < 17:
                    hf, q, kind = (n - 9) % 2, ((n - 9) // 2) % 2, "z" if n >= 13 else "conv"
                    dst, bias = (zs, wt["z_b"]) if kind == "z" else (xc, wt["xc_b"])
                    full(act, S, f"{kind}{hf}{q}")
                    act.activation(dst[f][:, hf, q * HT:(q + 1) * HT], misc[:], ACT.Identity,
                                   bias=bias[:, hf:hf + 1]).then_inc(s["job_taken"], 1)
                elif n == 17:
                    need(act, s["edge_done"], m + 2)
                    act.activation(xc[f][:], xc[f][:], ACT.Silu).then_inc(s["silu_done"], 1)
                    taken(act, S, "z11")
                    act.activation(zs[f][:], zs[f][:], ACT.Silu).then_inc(s["silu_done"], 1)
                elif 19 <= n < 23:
                    hf, q = (n - 19) % 2, (n - 19) // 2
                    full(act, S, f"dt{hf}{q}")
                    act.activation(delta[f][:, hf, q * HT:(q + 1) * HT], misc[:], ACT.Identity,
                                   bias=wt["dt_b"][:, hf:hf + 1]).then_inc(s["job_taken"], 1)
                elif n == 24:
                    need(act, s["clip_done"], m + 2)
                    act.activation(temp[:], temp[:], ACT.Exp).then_inc(s["softplus_done"], 1)
                    need(act, s["softplus_done"], (m + 1) * 2 + 1)
                    act.activation(temp[:], temp[:], ACT.Ln, bias=1.0).then_inc(s["softplus_done"], 1)

            def body(S, p):
                m, f = S.m, 1 - p
                for n in range(NSTEP):
                    if n % 2 == 0 and n < NSTEP - 2 and S.scan:
                        copy_b(m, n // 2 + 1)
                    if n == NSTEP - 2 and S.front:
                        copy_b(m + 1, 0)
                    if n < NSTEP - 1 and S.scan:
                        decays(m, p, n + 1)
                    if n == NSTEP - 1 and S.front:
                        decays(m + 1, f, 0)
                    if S.front:
                        chain(S, n, m, f)
                    if (n == 2 and S.back) or (n == 18 and S.scan):
                        q, M = (1, m - 1) if n == 2 else (0, m)
                        need(act, s["job_taken"], S.start)
                        need(act, s["added"], M * 32 + 16 * q + 16)
                        act.activation(y_tok[q][:].rearrange("p g d -> p (g d)"),
                                       y_acc[:].rearrange("p g d -> p (g d)"), ACT.Copy).then_inc(s["y_copied"], 1)
                    if n == 27 and S.back:
                        need(act, s["mv_done"], m)
                        act.activation(rstd1[:], mv[:, :, 1], ACT.Ln, bias=EPS).then_inc(s["rstd1_done"], 1)
                        need(act, s["rstd1_done"], (m - 1) * 2 + 1)
                        act.activation(rstd1[:], rstd1[:], ACT.Exp, scale=-0.5).then_inc(s["rstd1_done"], 1)
                    if n in (30, 31) and S.back:
                        q = n - 30
                        need(act, s["yo_stored"], m * 16)
                        full(act, S, f"fy{q}")
                        act.activation(yo[:, 4 * q:4 * q + 4, :].rearrange("p r c -> p (r c)"), misc[:],
                                       ACT.Copy).then_inc(s["job_taken"], 1)
                        if q == 1:
                            need(act, s["job_taken"], S.start + S.count)
                            act.sem_inc(s["yo_done"], 1)

            slots(act, body, blocks)

        @block.vector
        def _(dve):
            def scan(M, p, n):
                need(dve, s["decay_done"], M * 32 + n + 1)
                need(dve, s["drive_done"], M * 32 + n + 1)
                need(dve, s["prod_done"], M * 32 + n - 1)
                dve.tensor_tensor_scan(state[n % 2][:], decay[n % NR][:].rearrange("p i w t -> p (i w t)"),
                                       drive[n % 2][:].rearrange("p i t -> p (i t)"), 0.0, ALU.mult,
                                       ALU.add).then_inc(s["scan_done"], 1)

            def times_c(M, p, n):
                g = n // 2
                need(dve, s["scan_done"], M * 32 + n + 1)
                need(dve, s["c_full"], M * 16 + g + 1)
                need(dve, s["added"], M * 32 + n - 1)
                dve.tensor_tensor(prod[n % 2][:], state[n % 2][:], c_all[g % 2][:],
                                  ALU.mult).then_inc(s["prod_done"], 1)

            def chain(S, n, m, f):
                if n in (1, 2):
                    q = n - 1
                    full(dve, S, f"mean{q}")
                    need(dve, s["delta_done"], m + 1)
                    dve.tensor_tensor(
                        cent[:, q * HT:(q + 1) * HT].rearrange("p (n r c) -> p r n c", n=HWN, r=WS),
                        x_in[:].rearrange("p (r q n c) -> p r q n c", r=WS, q=2, n=HWN)[:, :, q],
                        misc[:].rearrange("p (r n c) -> p r n c", r=WS, n=HWN),
                        ALU.subtract).then_inc(s["job_taken"], 1)
                elif n in (7, 9):
                    q = (n - 7) // 2
                    need(dve, s["rstd_done"], (m + 1) * 2 + q + 1)
                    dve.tensor_tensor(tn[:, q * HT:(q + 1) * HT], cent[:, q * HT:(q + 1) * HT],
                                      sq[:, q * HT:(q + 1) * HT], ALU.mult).then_inc(s["tn_done"], 1)
                elif n == 18:
                    full(dve, S, "bc")
                    v = misc[:, 0:256].rearrange("p (g i) -> p g i", i=2 * NS)
                    steps = [
                        lambda: dve.tensor_copy(bc3[:, :, 0:32], v),
                        lambda: dve.tensor_tensor(rest[:, 0], v, bc3[:, :, 0:32], ALU.subtract),
                        lambda: dve.tensor_copy(bc3[:, :, 32:64], rest[:, 0]),
                        lambda: dve.tensor_tensor(rest[:, 1], rest[:, 0], bc3[:, :, 32:64], ALU.subtract),
                    ]
                    for i, step in enumerate(steps):
                        step().then_inc(s["split_done"], 1)
                        need(dve, s["split_done"], (m + 1) * 4 + i + 1)
                    dve.tensor_copy(bc3[:, :, 64:96], rest[:, 1]).then_inc(s["job_taken"], 1)
                elif n == 23:
                    full(dve, S, "rows")
                    dve.tensor_copy(rows[f][:], misc_b[0:96, :]).then_inc(s["job_taken"], 1)
                    dve.tensor_scalar(temp[:].rearrange("p (k t) -> p k t", k=2), delta[f][:], CLIP, None,
                                      ALU.min).then_inc(s["clip_done"], 1)
                elif n == 25:
                    need(dve, s["softplus_done"], (m + 1) * 2 + 2)
                    dve.tensor_tensor(delta[f][:], delta[f][:], temp[:].rearrange("p (k t) -> p k t", k=2),
                                      ALU.max).then_inc(s["delta_done"], 1)

            def gate(S, q, hf, par):
                full(dve, S, f"turn{q}{hf}")
                by_window = "p (n r c) -> p n r c"
                dve.tensor_tensor(
                    gated[:, hf, :].rearrange("p (r q n c) -> p q n r c", r=WS, q=2, n=HWN)[:, q],
                    misc[:].rearrange(by_window, n=HWN, r=WS),
                    zs[par][:, hf, q * HT:(q + 1) * HT].rearrange(by_window, n=HWN, r=WS),
                    ALU.mult).then_inc(s["job_taken"], 1)

            def behind(S, n, m, f):
                if n in (4, 6):
                    gate(S, 1, (n - 4) // 2, f)
                elif n in (24, 25):
                    q = n - 24
                    full(dve, S, f"out{q}")
                    need(dve, s["x1_stored"], m * 16)
                    dve.tensor_tensor(x1[:, 4 * q:4 * q + 4, :], misc[:].rearrange("p (r c) -> p r c", r=4),
                                      wt["out_b"][:].unsqueeze(1).to_broadcast([P, 4, C]),
                                      ALU.add).then_inc(s["job_taken"], 1)
                    if q == 1:
                        taken(dve, S, "out1")
                        for r in range(WS):
                            last = dve.bn_stats(stats[:, r, :], x1[:, r, :])
                        last.then_inc(s["stats_done"], 1)
                elif n == 26:
                    for r in range(WS):
                        last = dve.bn_aggr(mv[:, r, :], stats[:, r, :])
                    last.then_inc(s["mv_done"], 1)
                elif n == 28:
                    need(dve, s["rstd1_done"], m * 2)
                    for r in range(WS):
                        last = dve.tensor_scalar(z1[:, r, :], x1[:, r, :], mv[:, r, 0:1], rstd1[:, r:r + 1],
                                                 ALU.subtract, ALU.mult)
                    last.then_inc(s["z1_done"], 1)

            def body(S, p):
                for n in range(NSTEP):
                    if S.scan:
                        scan(S.m, p, n)
                    if n == 0 and S.back:
                        times_c(S.m - 1, 1 - p, NSTEP - 1)
                    if n >= 1 and S.scan:
                        times_c(S.m, p, n - 1)
                    if S.front:
                        chain(S, n, S.m, 1 - p)
                    if S.back and n == 26:
                        need(dve, s["stats_done"], S.m)
                    if S.scan and n in (26, 27):
                        gate(S, 0, n - 26, p)
                    if S.back:
                        behind(S, n, S.m, 1 - p)

            for i in range(NR):
                last = dve.memset(decay[i][:].rearrange("p i w t -> p (i w t)"), 0.0)
            last.then_inc(s["zeroed"], 1)
            slots(dve, body, blocks)

        @block.gpsimd
        def _(pool):
            def drives(M, p, n):
                q, g, hf = n // 16, n // 2, n % 2
                need(pool, s["du_done"], M * 2 + 1 + q)
                need(pool, s["b_copied"], M * 32 + 2 * g + 2)
                need(pool, s["scan_done"], M * 32 + n - 1)
                pool.tensor_tensor(drive[n % 2][:], du[p][:, hf:hf + 1, q * HT:(q + 1) * HT].to_broadcast([P, 2, HT]),
                                   b_all[g % 2][:], ALU.mult).then_inc(s["drive_done"], 1)

            def body(S, p):
                m, f = S.m, 1 - p
                for n in range(NSTEP):
                    if n < NSTEP - 1 and S.scan:
                        drives(m, p, n + 1)
                    if n == 13 and S.front:
                        taken(pool, S, "conv11")
                        v = xc[f][:].rearrange("p k (w t) -> p k w t", t=WT)[:, :, :, 0:K - 1]
                        pool.tensor_tensor(v, v, wt["edge"][:].unsqueeze(2).to_broadcast([P, 2, NW, K - 1]),
                                           ALU.add).then_inc(s["edge_done"], 1)
                    if n in (26, 28) and S.front:
                        q = (n - 26) // 2
                        need(pool, s["delta_done"], m + 2)
                        pool.tensor_tensor(du[f][:, :, q * HT:(q + 1) * HT], delta[f][:, :, q * HT:(q + 1) * HT],
                                           xc[f][:, :, q * HT:(q + 1) * HT], ALU.mult).then_inc(s["du_done"], 1)
                    if n == NSTEP - 1 and S.front:
                        drives(m + 1, f, 0)

            slots(pool, body, blocks)


def spectral(nc, wt, y_dram, phi_dram, t_dram):
    with ExitStack() as ctx:
        def sb(name, shape):
            return ctx.enter_context(nc.sbuf_tensor(name, shape, F32))

        def psum(name, shape):
            return ctx.enter_context(nc.psum_tensor(name, shape, F32))

        def sem(name):
            return ctx.enter_context(nc.semaphore(name))

        N = B * P
        LG = 4
        NG = L // LG
        ys = [sb(f"ys{i}", [P, 2, B, C]) for i in range(2)]
        filt = [sb(f"filt{i}", [P, 3, L, P]) for i in range(2)]
        spec = [sb(f"spec{i}", [P, 3, B, P]) for i in range(2)]
        u1 = sb("u1", [P, LG, B, P])
        u2 = [sb(f"u2_{i}", [P, LG, B, P]) for i in range(2)]
        u3 = [sb(f"u3_{i}", [P, LG, B, P]) for i in range(2)]
        mixed = sb("mixed", [P, 2, N])
        turned_s = sb("turned_s", [P, 2, N])
        tt = [sb(f"tt{i}", [P, 2, N]) for i in range(2)]

        x_bank = psum("x_bank", [P, 4, 2, P])
        s_bank = [psum(f"s_bank{i}", [P, 2, N]) for i in range(2)]
        way = psum("way", [P, 2, N])

        names = """cols_done spec_done sum_done u1_done u2_by_dve u2_by_pool u3_done im_done re_done
            theta_done mixed_done turn_done turned_done inv_done tt_done dc_done""".split()
        s = {n: sem(n) for n in names}
        ys_ready, filt_ready, tt_stored = ([sem(f"{n}{i}") for i in range(2)] for n in
                                           ("ys_ready", "filt_ready", "tt_stored"))

        def rounds(eng, body):
            body(-1, -1, 1, True, False, False)
            body(0, 0, 0, True, True, False)
            body(1, 0, 1, True, True, True)
            with eng.Fori(1, (KY - 1) // 2) as j:
                for i in range(2):
                    body(j * 2 + i, j, i, True, True, True)
            body(KY - 1, (KY - 1) // 2, 0, False, True, True)
            body(KY, KY // 2, 1, False, False, True)

        block = ctx.enter_context(nc.Block())

        @block.sync
        def _(sp):
            def load_ys(k, half, p, im_row=None):
                need(sp, s["cols_done"], k - 1)
                for i, row in enumerate((k, k + KY - 1 if im_row is None else im_row)):
                    sp.dma_start(ys[p][:, i].rearrange("x b d -> x (b d)"),
                                 y_dram[bass.ds(row, 1)].rearrange("o x b d -> (o x) (b d)")).then_inc(ys_ready[p], 16)

            def load_filt(k, p):
                need(sp, s["theta_done"], (k - 1) * NG)
                sp.dma_start(filt[p][:].rearrange("p t l x -> p (t l x)"),
                             phi_dram[bass.ds(k, 1)].to_broadcast([P, 3 * L * P])).then_inc(filt_ready[p], 16)

            def body(k, half, p, columns, products, back, more=True):
                if columns:
                    load_filt(k + 1, 1 - p)
                    if more:
                        load_ys(k + 2, half + 1, p)
                if back:
                    need(sp, s["tt_done"], k * 2)
                    for i, row in enumerate((k - 1, KY - 1 + (k - 1) if not (isinstance(k, int) and k == 1) else P)):
                        sp.dma_start(t_dram[bass.ds(row, 1)].rearrange("o x b d -> (o x) (b d)"),
                                     tt[1 - p][:, i]).then_inc(tt_stored[1 - p], 16)

            for i in range(2):
                sp.sem_inc(tt_stored[i], 32)
            load_ys(0, 0, 0, im_row=P)
            body(-1, -1, 1, True, False, False)
            body(0, 0, 0, True, True, False)
            body(1, 0, 1, True, True, True)
            with sp.Fori(1, (KY - 3) // 2) as j:
                for i in range(2):
                    body(j * 2 + i, j, i, True, True, True)
            body(KY - 3, (KY - 3) // 2, 0, True, True, True)
            body(KY - 2, (KY - 3) // 2, 1, True, True, True, more=False)
            body(KY - 1, 0, 0, False, True, True)
            body(KY, 0, 1, False, False, True)
            sp.wait_ge(tt_stored[0], 32 * ((KY + 1) // 2) + 32)
            sp.wait_ge(tt_stored[1], 32 * (KY // 2) + 32)

        @block.tensor
        def _(pe):
            def columns(k, half, p):
                pe.wait_ge(ys_ready[p], (half + 1) * 32)
                need(pe, s["spec_done"], k * 2)
                for b in range(B):
                    for i in range(2):
                        mm = pe.matmul(x_bank[:, b].rearrange("p c x -> p (c x)"), ys[p][:, i, b, :],
                                       wt["fx"][:, 2 * i:2 * i + 2, :].rearrange("p c x -> p (c x)"),
                                       start=(b % 2 == 0 and i == 0), stop=(i == 1), skip_group_check=True)
                mm.then_inc(s["cols_done"], 1)

            def theta(k, p, g):
                if g == 0:
                    need(pe, s["mixed_done"], (k - 1) * 2)
                for part, done, src in ((0, "re_done", u3), (1, "im_done", u2)):
                    need(pe, s[done], k * NG + g + 1)
                    for i in range(LG):
                        l = LG * g + i
                        mm = pe.matmul(s_bank[p][:, part, :], wt["theta"][:, l, :],
                                       src[g % 2][:, i].rearrange("p b x -> p (b x)"),
                                       start=(l == 0), stop=(l == L - 1))
                mm.then_inc(s["theta_done"], 1)

            def turn(k):
                need(pe, s["mixed_done"], k * 2 + 2)
                need(pe, s["tt_done"], k * 2)
                for part in range(2):
                    for b in range(B):
                        mm = pe.matmul(way[:, part, b * P:(b + 1) * P], mixed[:, part, b * P:(b + 1) * P],
                                       wt["ident"][:], start=True, stop=True, is_transpose=True)
                mm.then_inc(s["turn_done"], 1)

            def inverse(k):
                need(pe, s["turned_done"], k * 2 + 2)
                for part in range(2):
                    pe.matmul(way[:, part, :], wt["ix"][:, part, :], turned_s[:, 0, :], start=True, stop=False)
                    mm = pe.matmul(way[:, part, :], wt["ix"][:, 2 if part == 0 else 0, :], turned_s[:, 1, :],
                                   start=False, stop=True)
                mm.then_inc(s["inv_done"], 1)

            def body(k, half, p, col, products, back):
                if col:
                    columns(k + 1, half + p, 1 - p)
                for g in range(NG):
                    if products:
                        theta(k, p, g)
                    if back and g == 0:
                        turn(k - 1)
                    if back and g == 2:
                        inverse(k - 1)

            rounds(pe, body)

        @block.scalar
        def _(act):
            def take_spec(k, p):
                need(act, s["cols_done"], k + 1)
                need(act, s["theta_done"], (k - 1) * NG)
                for i in range(2):
                    act.activation(spec[p][:, 0:2, 2 * i:2 * i + 2, :],
                                   x_bank[:, 2 * i:2 * i + 2].rearrange("p b c x -> p c b x"), ACT.Copy,
                                   scale=wt["gamma"][:, 0:1]).then_inc(s["spec_done"], 1)

            def copy2(dst, src, done):
                for i in range(2):
                    act.activation(dst[:, i, :], src[:, i, :], ACT.Copy).then_inc(s[done], 1)

            def body(k, half, p, columns, products, back):
                if columns:
                    take_spec(k + 1, 1 - p)
                if back:
                    need(act, s["turn_done"], k)
                    copy2(turned_s, way, "turned_done")
                    need(act, s["inv_done"], k)
                    need(act, tt_stored[1 - p], (half + p) * 32)
                    copy2(tt[1 - p], way, "tt_done")
                if products:
                    need(act, s["theta_done"], k * NG + NG)
                    need(act, s["turn_done"], k)
                    copy2(mixed, s_bank[p], "mixed_done")

            rounds(act, body)

        def times(eng, dst, src, kind, g, k, p):
            return eng.tensor_tensor(
                dst[:], spec[p][:, kind[0]].unsqueeze(1).to_broadcast([P, LG, B, P]),
                filt[p][:, kind[1], LG * g:LG * g + LG, :].unsqueeze(2).to_broadcast([P, LG, B, P]), ALU.mult)

        @block.vector
        def _(dve):
            def total(k, p):
                need(dve, s["spec_done"], k * 2 + 2)
                need(dve, s["u1_done"], (k - 1) * NG)
                if isinstance(k, int) and k == 0:
                    dc = spec[p][:, 0, :, 0]
                    dve.tensor_scalar(dc, dc, wt["dc"][:, 0:1], None, ALU.add).then_inc(s["dc_done"], 1)
                    dve.wait_ge(s["dc_done"], 1)
                dve.tensor_tensor(spec[p][:, 2], spec[p][:, 0], spec[p][:, 1], ALU.add).then_inc(s["sum_done"], 1)

            def body(k, half, p, columns, products, back):
                if products:
                    dve.wait_ge(filt_ready[p], (half + 1) * 16)
                    for g in range(NG):
                        n = k * NG + g
                        need(dve, s["sum_done"], k + 1)
                        need(dve, s["im_done"], n)
                        need(dve, s["re_done"], n)
                        times(dve, u1, spec, (2, 0), g, k, p).then_inc(s["u1_done"], 1)
                        if g % 2 == 0:
                            need(dve, s["theta_done"], n - 1)
                            times(dve, u2[0], spec, (0, 1), g, k, p).then_inc(s["u2_by_dve"], 1)
                        need(dve, s["u3_done"], n + 1)
                        need(dve, s["u1_done"], n + 1)
                        dve.tensor_tensor(u3[g % 2][:], u1[:], u3[g % 2][:], ALU.subtract).then_inc(s["re_done"], 1)
                        if g % 2 == 0:
                            need(dve, s["u2_by_dve"], k * 2 + g // 2 + 1)
                        else:
                            need(dve, s["u2_by_pool"], k * 2 + g // 2 + 1)
                        dve.tensor_tensor(u2[g % 2][:], u1[:], u2[g % 2][:], ALU.subtract).then_inc(s["im_done"], 1)
                        if g == 1 and columns:
                            total(k + 1, 1 - p)
                elif columns:
                    total(k + 1, 1 - p)

            rounds(dve, body)

        @block.gpsimd
        def _(pool):
            def body(k, half, p, columns, products, back):
                if products:
                    pool.wait_ge(filt_ready[p], (half + 1) * 16)
                    need(pool, s["sum_done"], k + 1)
                    for g in range(NG):
                        n = k * NG + g
                        need(pool, s["theta_done"], n - 1)
                        times(pool, u3[g % 2], spec, (1, 2), g, k, p).then_inc(s["u3_done"], 1)
                        if g % 2 == 1:
                            times(pool, u2[1], spec, (0, 1), g, k, p).then_inc(s["u2_by_pool"], 1)

            rounds(pool, body)


def mlp(nc, wt, t_dram, x1_dram, out):
    with ExitStack() as ctx:
        def sb(name, shape):
            return ctx.enter_context(nc.sbuf_tensor(name, shape, F32))

        def psum(name, shape):
            return ctx.enter_context(nc.psum_tensor(name, shape, F32))

        def sem(name):
            return ctx.enter_context(nc.semaphore(name))

        R = 4
        T = R * W
        NGR = H // R
        tk = [sb(f"tk{i}", [P, R, B, C]) for i in range(2)]
        x1t = [sb(f"x1t{i}", [P, B, R, C]) for i in range(2)]
        mix = [sb(f"mix{i}", [P, T]) for i in range(2)]
        hid = [sb(f"hid{i}", [P, 2, T]) for i in range(2)]
        res = [sb(f"res{i}", [P, T]) for i in range(2)]
        mix_bank = [psum(f"mix_bank{i}", [P, T]) for i in range(2)]
        hid_bank = [psum(f"hid_bank{i}", [P, 2, T]) for i in range(2)]
        res_bank = [psum(f"res_bank{i}", [P, T]) for i in range(2)]

        names = "rows_done mix_done up_done hid_done down_done res_done".split()
        s = {n: sem(n) for n in names}
        tk_ready, x1_ready, res_stored = ([sem(f"{n}{i}") for i in range(2)] for n in
                                          ("tk_ready", "x1_ready", "res_stored"))

        def steps(eng, body):
            body(-2, -1, 6, True, False, False)
            body(-1, -1, 7, True, True, False)
            for i in range(2 * B):
                body(i, 0, i, True, True, True)
            with eng.Fori(1, NGR // 2 - 1) as j:
                for i in range(2 * B):
                    body(j * (2 * B) + i, j, i, True, True, True)
            last = NGR // 2 - 1
            for i in range(2 * B):
                body(last * 2 * B + i, last, i, i < 2 * B - 2, i < 2 * B - 1, True)

        block = ctx.enter_context(nc.Block())
        x1v = x1_dram.rearrange("(b x) y c -> b y x c", b=B)
        ov = out.rearrange("b d x y -> b d (x y)")

        @block.sync
        def _(sp):
            def load(g, p):
                need(sp, s["rows_done"], (g - 1) * B)
                sp.dma_start(tk[p][:].rearrange("p x b h -> p (x b h)"),
                             t_dram[0:P, bass.ds(g * R, R)].rearrange("f x b h -> f (x b h)")).then_inc(tk_ready[p], 16)
                need(sp, s["down_done"], (g - 1) * B)
                for b in range(B):
                    sp.dma_start(x1t[p][:, b], x1v[b, :, bass.ds(g * R, R), :]).then_inc(x1_ready[p], 16)

            def body(g, p, more):
                if more:
                    load(g + 1, 1 - p)
                for b in range(B):
                    need(sp, s["res_done"], g * B + b + 1)
                    sp.dma_start(ov[b, :, bass.ds(g * T, T)], res[b % 2][:]).then_inc(res_stored[b % 2], 16)

            load(0, 0)
            body(0, 0, True)
            body(1, 1, True)
            with sp.Fori(1, NGR // 2 - 1) as j:
                for i in range(2):
                    body(j * 2 + i, i, True)
            body(NGR - 2, 0, True)
            body(NGR - 1, 1, False)
            for i in range(2):
                sp.wait_ge(res_stored[i], 16 * NGR * B // 2)

        @block.tensor
        def _(pe):
            def rows(u, j, i):
                p, b = i // B, i % B
                pe.wait_ge(tk_ready[p], (j + 1) * 16)
                need(pe, s["mix_done"], u - 1)
                for r in range(R):
                    mm = pe.matmul(mix_bank[i % 2][:, r * W:(r + 1) * W], tk[p][:, r, b, :], wt["iy"][:],
                                   start=True, stop=True)
                mm.then_inc(s["rows_done"], 1)

            def up(u, i):
                need(pe, s["mix_done"], u + 1)
                need(pe, s["hid_done"], (u - 1) * 2)
                for k in range(2):
                    mm = pe.matmul(hid_bank[i % 2][:, k, :], wt["w1"][:, k, :], mix[i % 2][:], start=True, stop=True)
                mm.then_inc(s["up_done"], 1)

            def down(u, j, i):
                p, b = i // B, i % B
                need(pe, s["hid_done"], u * 2 + 2)
                need(pe, s["res_done"], u - 1)
                pe.wait_ge(x1_ready[p], (j + 1) * 16 * B)
                for k in range(2):
                    pe.matmul(res_bank[i % 2][:], wt["w2"][:, k, :], hid[i % 2][:, k, :], start=(k == 0), stop=False,
                              skip_group_check=True)
                for r in range(R):
                    mm = pe.matmul(res_bank[i % 2][:, r * W:(r + 1) * W], x1t[p][:, b, r, :], wt["ident"][:],
                                   start=False, stop=(r == R - 1), is_transpose=True, skip_group_check=True)
                mm.then_inc(s["down_done"], 1)

            def body(u, j, i, has_rows, has_up, has_down):
                if has_rows:
                    rows(u + 2, j + (i + 2) // (2 * B), (i + 2) % (2 * B))
                if has_up:
                    up(u + 1, (i + 1) % (2 * B))
                if has_down:
                    down(u, j, i)

            steps(pe, body)

        @block.scalar
        def _(act):
            def body(u, j, i, has_rows, has_up, has_down):
                if has_up:
                    v, i = u + 1, (i + 1) % (2 * B)
                    need(act, s["up_done"], v + 1)
                    need(act, s["down_done"], v - 1)
                    for k in range(2):
                        act.activation(hid[i % 2][:, k, :], hid_bank[i % 2][:, k, :], ACT.Gelu,
                                       bias=wt["b1"][:, k:k + 1]).then_inc(s["hid_done"], 1)

            steps(act, body)

        @block.vector
        def _(dve):
            def body(u, j, i, has_rows, has_up, has_down):
                if has_rows:
                    v, iv = u + 2, (i + 2) % (2 * B)
                    need(dve, s["rows_done"], v + 1)
                    need(dve, s["up_done"], v - 1)
                    dve.tensor_copy(mix[iv % 2][:], mix_bank[iv % 2][:]).then_inc(s["mix_done"], 1)
                if has_down:
                    need(dve, s["down_done"], u + 1)
                    need(dve, res_stored[i % 2], (j * B + i // 2) * 16)
                    dve.tensor_scalar(res[i % 2][:], res_bank[i % 2][:], wt["b2"][:, 0:1], None,
                                      ALU.add).then_inc(s["res_done"], 1)

            steps(dve, body)


_INS = {
    "x": "x", "ln_g": "L0_conv_ln_g", "ln_b": "L0_conv_ln_b", "W_in": "L0_conv_W_in", "b_in": "L0_conv_b_in",
    "conv_w": "L0_conv_conv_w", "conv_b": "L0_conv_conv_b", "W_x": "L0_conv_W_x", "dt_w": "L0_conv_dt_w",
    "dt_b": "L0_conv_dt_b", "A_log": "L0_conv_A_log", "D": "L0_conv_D", "W_out": "L0_conv_W_out",
    "b_out": "L0_conv_b_out", "Phi_f_real": "L1_conv_Phi_f_real", "Phi_f_imag": "L1_conv_Phi_f_imag",
    "Theta": "L1_conv_Theta", "ln_gamma": "L1_conv_ln_gamma", "ln_beta": "L1_conv_ln_beta",
    "W1": "L1_conv_W1", "b1": "L1_conv_b1", "W2": "L1_conv_W2", "b2": "L1_conv_b2",
}


def transforms():
    n = np.arange(P)
    angle = 2 * np.pi * (np.outer(n, n) % P) / P
    c, s = np.cos(angle), np.sin(angle)
    fy = np.concatenate([c[:, :KY], -s[:, 1:KY - 1]], axis=1)
    fx = np.stack([c, -s, s, c], axis=1)
    ix = np.stack([c, s, -s], axis=1)
    once = np.where((n[:KY] == 0) | (n[:KY] == KY - 1), 1.0, 2.0)[:, None]
    iy = np.concatenate([once * c[:KY], -2 * s[1:KY - 1]], axis=0) / (H * W)
    return {k: np.ascontiguousarray(v, dtype=np.float32) for k, v in dict(fy=fy, fx=fx, ix=ix, iy=iy).items()}


def kernel(**inputs):
    import concourse.bacc as _bacc
    from concourse.bass_utils import run_bass_kernel_spmd as _run

    nc = _bacc.Bacc("TRN2", target_bir_lowering=False, num_devices=1)
    arrays, args = {}, {}
    given = {k: np.ascontiguousarray(inputs[v]) for k, v in _INS.items()}
    for name, v in {**given, **transforms()}.items():
        arrays[f"in_{name}_dram"] = v
        args[name] = nc.dram_tensor(f"in_{name}_dram", v.shape, mybir.dt.from_np(v.dtype), kind="ExternalInput").ap()
    out = nc.dram_tensor("out_0_dram", (B, C, H, W), F32, kind="ExternalOutput").ap()
    conv_seq_program(nc, args, out)
    r = _run(nc, [arrays], core_ids=[0])
    return r.results[0]["out_0_dram"]
```

```python
from contextlib import ExitStack

import concourse.bass as bass
import numpy as np
from concourse import mybir

ALU = mybir.AluOpType
ACT = mybir.ActivationFunctionType
F32 = mybir.dt.float32
BF16 = mybir.dt.bfloat16

P = 128
B = 4
C = 128
H = W = 128
WS = 8
WT = WS * WS
NW = W // WS
BT = WS * W
KB = H // WS
NM = B * KB
HT = BT // 2
HWN = NW // 2
DI = 256
NS = 16
RANK = 8
K = 4
NSTEP = 2 * NS
L = 16
KY = W // 2 + 1
EPS = 1e-5
TABLES = "natural_log_exp_and_others"
B_AHEAD, A_AHEAD, D_AHEAD = 5, 3, 2
CLIP = 30.0

JOBS = [(0, "mean0", "front"), (0, "mean1", "front"), (2, "turn10", "back"), (3, "turn11", "back"),
        (4, "var0", "front"), (5, "var1", "front"), (7, "conv00", "front"), (9, "z00", "front"),
        (10, "conv10", "front"), (12, "z10", "front"), (13, "conv01", "front"), (15, "z01", "front"),
        (16, "conv11", "front"), (18, "z11", "front"), (19, "out0", "back"), (20, "out1", "back"),
        (21, "bc", "front"), (22, "dt00", "front"), (23, "dt10", "front"), (24, "rows", "front"),
        (24, "dt01", "front"), (25, "dt11", "front"), (26, "turn00", "scan"), (27, "turn01", "scan"),
        (28, "fy0", "back"), (29, "fy1", "back")]
SKIP_AT = {2: 0, 3: 1, 4: 2, 6: 3, 26: 0, 27: 1, 28: 2, 29: 3}


class Slot:

    def __init__(self, m, front, scan, back, rounds):
        self.m, self.front, self.scan, self.back = m, front, scan, back
        on = {"front": front, "scan": scan, "back": back}
        mine = [j for j in JOBS if on[j[2]]]
        self.bank = {j[1]: i % 2 for i, j in enumerate(mine)}
        self.before = {j[1]: rounds + i // 2 for i, j in enumerate(mine)}
        self.rounds = len(mine) // 2
        self.names = {j[1] for j in mine}

    def at(self, n):
        return [name for step, name, _ in JOBS if step == n and name in self.names]

    def step(self, n, p):
        if n >= NSTEP:
            return (self.m + 1, 1 - p, n - NSTEP) if self.front else None
        if n < 0:
            return (self.m - 1, 1 - p, n + NSTEP) if self.back else None
        return (self.m, p, n) if self.scan else None


def slots(eng, body, blocks):
    first = Slot(-1, True, False, False, 0)
    body(first, 1)
    second = Slot(0, True, True, False, first.rounds)
    body(second, 0)
    base = first.rounds + second.rounds
    per = len(JOBS) // 2
    with eng.Fori(0, (blocks - 2) // 2) as j:
        for i in range(2):
            body(Slot(j * 2 + 1 + i, True, True, True, j * (2 * per) + base + per * i), 1 - i)
    base += per * (blocks - 2)
    last = Slot(blocks - 1, False, True, True, base)
    body(last, (blocks - 1) % 2)
    body(Slot(blocks, False, False, True, base + last.rounds), blocks % 2)


def since(n, ring):
    return next(d for d in range(1, NSTEP) if (n - d) % NSTEP % ring == n % ring)


def need(eng, sem, value):
    if isinstance(value, int) and value <= 0:
        return
    eng.wait_ge(sem, value)


def conv_seq_program(nc, a, out, blocks=NM, layer1=True):
    x1_dram = nc.dram_tensor("x1_rows", [B * H, W, C], F32).ap()
    y_dram = nc.dram_tensor("row_spectra", [P + 1, H, B, C], F32).ap()
    phi_dram = nc.dram_tensor("filters", [KY, 3 * L * P], F32).ap()
    t_dram = nc.dram_tensor("column_sums", [P + 1, H, B, C], F32).ap()

    with ExitStack() as whole:
        wt = weights(nc, whole)
        setup(nc, a, wt, phi_dram, y_dram)
        layer0(nc, a, wt, x1_dram, y_dram, blocks)
        if layer1:
            spectral(nc, wt, y_dram, phi_dram, t_dram)
            mlp(nc, wt, t_dram, x1_dram, out)


def weights(nc, ctx):
    def sb(name, shape, dt=F32):
        return ctx.enter_context(nc.sbuf_tensor(name, shape, dt))

    return {
        "ident": sb("ident", [P, P]), "identb": sb("identb", [P, P], BF16),
        "mean_w": sb("mean_w", [P, P]),
        "select": sb("select", [96, 2 * NS, P], BF16),
        "tap_w": sb("tap_w", [P, K, DI]),
        "z_w": sb("z_w", [P, DI]), "z_b": sb("z_b", [P, 2]),
        "xc_b": sb("xc_b", [P, 2]), "edge": sb("edge", [P, 2, K - 1]),
        "bc_w": sb("bc_w", [P, 2, 2 * NS]), "dt_w": sb("dt_full_w", [P, 2, DI]),
        "dt_b": sb("dt_bias", [P, 2]), "neg_a": sb("neg_a", [P, 2, NS]),
        "diag_d": sb("diag_d", [P, 2, P]), "out_w": sb("out_w", [P, 2, C]),
        "out_b": sb("out_b_rows", [P, C]), "fy": sb("fy", [P, P]),
        "fx": sb("fx", [P, 4, P]), "ix": sb("ix", [P, 3, P]), "iy": sb("iy", [P, P]),
        "theta": sb("theta_t", [P, L, C]), "gamma": sb("gamma", [P, 1]), "dc": sb("dc", [P, 1]),
        "w1": sb("w1_t", [P, 2, P]), "b1": sb("b1_cols", [P, 2]),
        "w2": sb("w2_t", [P, 2, C]), "b2": sb("b2_col", [P, 1]),
    }


def setup(nc, a, wt, phi_dram, y_dram):
    with ExitStack() as ctx:
        def sb(name, shape, dt=F32):
            return ctx.enter_context(nc.sbuf_tensor(name, shape, dt))

        def sem(name):
            return ctx.enter_context(nc.semaphore(name))

        w_in = sb("w_in", [P, 2 * DI])
        gain = sb("gain", [P, 1])
        shift = sb("shift", [P, 1])
        b_in = sb("b_in", [P, 4])
        conv_w = sb("conv_w", [P, 2, K])
        conv_b = sb("conv_b", [P, 2])
        w_x = sb("w_x", [P, 2, RANK + 2 * NS])
        rank_w = sb("rank_w", [RANK, 2, P])
        dt_low = sb("dt_low", [RANK, DI])
        a_log = sb("a_log", [P, 2, NS])
        d_col = sb("d_col", [P, 2])
        bo_col = sb("bo_col", [P, 1])
        w1_rows = sb("w1_rows", [P, 2, C])
        w2_rows = sb("w2_rows", [P, DI])
        th_rows = sb("th_rows", [P, L, C])
        beta = sb("beta", [P, 1])
        phi = sb("phi", [P, 3, L, KY])
        phi_i = sb("phi_i", [P, L, KY])
        zeros = sb("zeros", [P, B * C])
        phi_t = sb("phi_t", [KY, 3 * L, P])
        b_fold = sb("b_fold", [P, 4])
        tap_sum = sb("tap_sum", [P, 2, K])
        edge0 = sb("edge0", [P, 2])
        ps = [ctx.enter_context(nc.psum_tensor(f"set{i}", [P, 512], F32)) for i in range(2)]

        loads = [
            (w_in[:], a["W_in"]), (gain[:], a["ln_g"].rearrange("(p o) -> p o", o=1)),
            (shift[:], a["ln_b"].rearrange("(p o) -> p o", o=1)),
            (b_in[:], a["b_in"].rearrange("(k p) -> p k", p=P)),
            (conv_w[:], a["conv_w"].rearrange("(k p) t -> p k t", p=P)),
            (conv_b[:], a["conv_b"].rearrange("(k p) -> p k", p=P)),
            (w_x[:], a["W_x"].rearrange("(k p) n -> p k n", p=P)), (dt_low[:], a["dt_w"]),
            (wt["dt_b"][:], a["dt_b"].rearrange("(k p) -> p k", p=P)),
            (a_log[:], a["A_log"].rearrange("(k p) n -> p k n", p=P)),
            (d_col[:], a["D"].rearrange("(k p) -> p k", p=P)),
            (wt["out_w"][:], a["W_out"].rearrange("(k p) n -> p k n", p=P)),
            (bo_col[:], a["b_out"].rearrange("(p o) -> p o", o=1)),
            (w1_rows[:], a["W1"].rearrange("(k p) n -> p k n", p=P)), (w2_rows[:], a["W2"]),
            (th_rows[:], a["Theta"].rearrange("l h d -> h l d")),
            (wt["gamma"][:], a["ln_gamma"].rearrange("(p o) -> p o", o=1)),
            (beta[:], a["ln_beta"].rearrange("(p o) -> p o", o=1)),
            (wt["b1"][:], a["b1"].rearrange("(k p) -> p k", p=P)),
            (wt["b2"][:], a["b2"].rearrange("(p o) -> p o", o=1)),
            (phi[:, 0], a["Phi_f_real"].rearrange("l x y -> x l y")),
            (phi_i[:], a["Phi_f_imag"].rearrange("l x y -> x l y")),
            (wt["fy"][:], a["fy"]), (wt["fx"][:], a["fx"]), (wt["ix"][:], a["ix"]), (wt["iy"][:], a["iy"]),
        ]
        loaded, zeroed, consts = sem("loaded"), sem("zeroed"), sem("consts")
        gained, phi_made, exped = sem("gained"), sem("phi_made"), sem("exped")
        turned, taken, folded, small = sem("turned"), sem("taken"), sem("folded"), sem("small")
        stored = sem("filters_stored")

        turns = []

        def turn(dst, parts):
            turns.append((dst, parts))

        for t in range(K):
            turn(("tap", t), [(k * P, P, P, conv_w[:, k, t:t + 1].to_broadcast([P, P]), wt["ident"][:], True)
                              for k in range(2)])
        turn(("fold",), [(k, 1, P, w_in[:, k * P:(k + 1) * P], shift[:], False) for k in range(4)])
        turn(("bout",), [(0, P, P, bo_col[:, 0:1].to_broadcast([P, P]), wt["ident"][:], True)])
        turn(("rank",), [(k * P, P, RANK, w_x[:, k, 0:RANK], wt["ident"][:], True) for k in range(2)])
        turn(("dt",), [(k * DI, DI, P, rank_w[:, k, :], dt_low[:], False) for k in range(2)])
        turn(("w1",), [(k * P, P, P, w1_rows[:, k, :], wt["ident"][:], True) for k in range(2)])
        turn(("w2",), [(k * P, P, P, w2_rows[:, k * P:(k + 1) * P], wt["ident"][:], True) for k in range(2)])
        for g in range(L // 4):
            turn(("theta", g), [(i * P, P, P, th_rows[:, 4 * g + i, :], wt["ident"][:], True) for i in range(4)])
        for g in range(3 * L // 4):
            turn(("phi", g), [(i * P, P, KY, phi[:, (4 * g + i) // L, (4 * g + i) % L, :], wt["ident"][:], True)
                              for i in range(4)])
        RANKED = [i for i, t in enumerate(turns) if t[0] == ("rank",)][0]

        block = ctx.enter_context(nc.Block())

        @block.sync
        def _(sp):
            for dst, src in loads:
                with nc.allow_non_contiguous_dma(reason="weights, once"):
                    sp.dma_start(dst, src).then_inc(loaded, 16)
            sp.wait_ge(taken, len(turns))
            sp.dma_start(phi_dram, phi_t[:].rearrange("k n x -> k (n x)")).then_inc(stored, 16)
            sp.wait_ge(zeroed, 4)
            sp.dma_start(y_dram[P].rearrange("x b d -> x (b d)"), zeros[:]).then_inc(stored, 16)
            sp.wait_ge(stored, 32)

        @block.gpsimd
        def _(pool):
            pool.memset(wt["ident"][:], 0.0).then_inc(zeroed, 1)
            pool.memset(wt["identb"][:], 0.0).then_inc(zeroed, 1)
            pool.memset(wt["select"][:], 0.0).then_inc(zeroed, 1)
            pool.memset(zeros[:], 0.0).then_inc(zeroed, 1)
            pool.memset(wt["mean_w"][:], 1.0 / C).then_inc(consts, 1)
            pool.wait_ge(zeroed, 3)
            for t in ("ident", "identb"):
                pool.affine_select(out=wt[t][:], in_=wt[t][:], compare_op=ALU.not_equal, fill=1.0, base=0,
                                   pattern=[[-1, P]], channel_multiplier=1).then_inc(consts, 1)
            for part in range(3):
                pool.affine_select(out=wt["select"][:], in_=wt["select"][:], compare_op=ALU.not_equal, fill=1.0,
                                   base=-2 * NS * part, pattern=[[-1, 2 * NS], [0, P]],
                                   channel_multiplier=1).then_inc(consts, 1)
                pool.wait_ge(consts, 4 + part)

        @block.scalar
        def _(act):
            act.wait_ge(loaded, 16 * len(loads))
            act.activation(wt["neg_a"][:], a_log[:], ACT.Exp).then_inc(exped, 1)

        @block.vector
        def _(dve):
            dve.wait_ge(loaded, 16 * len(loads))
            dve.wait_ge(consts, 6)
            dve.tensor_scalar(wt["z_w"][:], w_in[:, DI:2 * DI], gain[:, 0:1], None, ALU.mult)
            dve.tensor_copy(wt["bc_w"][:], w_x[:, :, RANK:])
            dve.tensor_scalar(wt["dc"][:], beta[:], float(H * W), None, ALU.mult)
            for k in range(2):
                dve.tensor_scalar(wt["diag_d"][:, k, :], wt["ident"][:], d_col[:, k:k + 1], None, ALU.mult)
            dve.tensor_tensor(phi[:, 1], phi[:, 0], phi_i[:], ALU.add)
            dve.tensor_tensor(phi[:, 2], phi[:, 0], phi_i[:], ALU.subtract).then_inc(phi_made, 1)
            n = 0
            dve.tensor_copy(tap_sum[:, :, 0], conv_w[:, :, 0]).then_inc(small, 1)
            for t in range(1, K):
                n += 1
                dve.wait_ge(small, n)
                dve.tensor_tensor(tap_sum[:, :, t], tap_sum[:, :, t - 1], conv_w[:, :, t], ALU.add).then_inc(small, 1)
            dve.wait_ge(exped, 1)
            dve.tensor_scalar(wt["neg_a"][:], wt["neg_a"][:], -1.0, None, ALU.mult)
            for i, (dst, _) in enumerate(turns):
                dve.wait_ge(turned, i + 1)
                bank = ps[i % 2]
                if dst[0] == "tap":
                    last = dve.scalar_tensor_tensor(wt["tap_w"][:, dst[1], :], bank[:, 0:DI], gain[:, 0:1],
                                                    w_in[:, 0:DI], ALU.mult, ALU.mult)
                elif dst[0] == "fold":
                    last = dve.tensor_tensor(b_fold[:], bank[:, 0:4], b_in[:], ALU.add)
                elif dst[0] == "bout":
                    last = dve.tensor_copy(wt["out_b"][:], bank[:, 0:P])
                elif dst[0] == "rank":
                    last = dve.tensor_copy(rank_w[:].rearrange("r k p -> r (k p)"), bank[0:RANK, 0:DI])
                elif dst[0] == "dt":
                    last = dve.tensor_copy(wt["dt_w"][:].rearrange("p k n -> p (k n)"), bank[:, :])
                elif dst[0] in ("w1", "w2"):
                    last = dve.tensor_copy(wt[dst[0]][:].rearrange("p k n -> p (k n)"), bank[:, 0:DI])
                elif dst[0] == "theta":
                    g = 4 * dst[1]
                    last = dve.tensor_copy(wt["theta"][:, g:g + 4, :].rearrange("p l h -> p (l h)"), bank[:, :])
                else:
                    g = 4 * dst[1]
                    last = dve.tensor_copy(phi_t[:, g:g + 4, :].rearrange("p l h -> p (l h)"), bank[0:KY, :])
                last.then_inc(taken, 1)
            n += 1
            dve.wait_ge(small, n)
            dve.wait_ge(taken, len(turns))
            dve.tensor_copy(wt["z_b"][:], b_fold[:, 2:4])
            dve.tensor_tensor(edge0[:], tap_sum[:, :, K - 1], b_fold[:, 0:2], ALU.mult).then_inc(small, 1)
            n += 1
            dve.wait_ge(small, n)
            dve.tensor_tensor(wt["xc_b"][:], edge0[:], conv_b[:], ALU.add)
            for t in range(K - 1):
                dve.scalar_tensor_tensor(wt["edge"][:, :, t], tap_sum[:, :, K - 2 - t], -1.0, b_fold[:, 0:2],
                                         ALU.mult, ALU.mult)

        @block.tensor
        def _(pe):
            pe.wait_ge(loaded, 16 * len(loads))
            pe.wait_ge(consts, 6)
            pe.wait_ge(phi_made, 1)
            for i, (_, parts) in enumerate(turns):
                if i >= 2:
                    pe.wait_ge(taken, i - 1)
                if turns[i][0] == ("dt",):
                    pe.wait_ge(taken, RANKED + 1)
                for col, n, rows, lhs, rhs, tr in parts:
                    last = pe.matmul(ps[i % 2][0:rows, col:col + n], lhs, rhs, start=True, stop=True, is_transpose=tr)
                last.then_inc(turned, 1)


def layer0(nc, a, wt, x1_dram, y_dram, blocks):
    with ExitStack() as ctx:
        def sb(name, shape, dt=F32):
            return ctx.enter_context(nc.sbuf_tensor(name, shape, dt))

        def psum(name, shape):
            return ctx.enter_context(nc.psum_tensor(name, shape, F32))

        def sem(name):
            return ctx.enter_context(nc.semaphore(name))

        x_in = sb("x_in", [P, BT])
        x_res = sb("x_res", [P, BT])
        temp = sb("temp", [P, 2 * BT])
        cent, sq = temp[:, 0:BT], temp[:, BT:2 * BT]
        tn = sb("tn", [P, BT])
        xc = [sb(f"xc{i}", [P, 2, BT]) for i in range(2)]
        zs = [sb(f"zs{i}", [P, 2, BT]) for i in range(2)]
        delta = [sb(f"delta{i}", [P, 2, BT]) for i in range(2)]
        du = sb("du", [P, 2, BT])
        bc3 = sb("bc3", [P, BT // P, 96], BF16)
        rest = sb("rest", [P, 2, BT // P, 2 * NS])
        rows = [sb(f"rows{i}", [96, BT], BF16) for i in range(2)]
        NB, NA, ND, NP = 4, 4, 3, 3
        b_all = [sb(f"b_all{i}", [P, HT]) for i in range(NB)]
        decay = [sb(f"decay{i}", [P, 2, HWN, WT]) for i in range(NA)]
        drive = [sb(f"drive{i}", [P, 2, HT]) for i in range(ND)]
        state = [sb(f"state{i}", [P, 2, HT]) for i in range(NP)]
        prod = [sb(f"prod{i}", [P, 2, HT]) for i in range(NP)]
        y_tok = [sb(f"y_tok{i}", [P, 4, DI]) for i in range(2)]
        gated = sb("gated", [P, 2, BT])
        x1 = sb("x1", [P, WS, C])
        stats = sb("stats", [P, WS, 6])
        mv = sb("mv", [P, WS, 2])
        rstd1 = sb("rstd1", [P, WS])
        z1 = sb("z1", [P, WS, C])
        yo = z1

        c_bank = [psum(f"c_bank{i}", [P, HT]) for i in range(2)]
        b_bank = [psum(f"b_bank{i}", [P, HT]) for i in range(2)]
        y_acc = psum("y_acc", [P, 4, DI])
        job_bank = [psum(f"job_bank{i}", [P, 512]) for i in range(2)]

        names = """x_ready xres_ready x1_stored yo_stored sq_done rstd_done tn_done
            edge_done silu_done split_done clip_done softplus_done delta_done du_done c_full b_full b_copied
            decay_done drive_done scan_done prod_done added y_copied stats_done mv_done rstd1_done z1_done
            yo_done zeroed""".split()
        s = {n: sem(n) for n in names}

        job_full = [sem(f"job_full{i}") for i in range(2)]
        job_taken = [sem(f"job_taken{i}") for i in range(2)]

        def full(eng, S, name):
            need(eng, job_full[S.bank[name]], S.before[name] + 1)
            return job_bank[S.bank[name]]

        def taken(eng, S, name):
            need(eng, job_taken[S.bank[name]], S.before[name] + 1)

        def take(S, name):
            return job_taken[S.bank[name]]

        block = ctx.enter_context(nc.Block())

        xv = a["x"].rearrange("b c (k r) w -> b k c (r w)", r=WS)
        yv = y_dram[0:P].rearrange("f (k r) b d -> k b f r d", r=WS)

        @block.sync
        def _(sp):
            def place(M):
                if isinstance(M, int):
                    return M // KB, M % KB
                return sp.snap(M // KB), sp.snap(M % KB)

            def load_x(dst, at, done):
                sp.dma_start(dst[:], xv[bass.ds(at[0], 1), bass.ds(at[1], 1)]
                             .rearrange("o q c n -> (o q c) n")).then_inc(done, 16)

            def body(m, scan=True, back=True, more=True):
                before, after = place(m - 1), place(m + 2)
                if back:
                    need(sp, s["x1_stored"], m * 16)
                    load_x(x_res, before, s["xres_ready"])
                if more:
                    need(sp, s["sq_done"], (m + 2) * 2)
                    load_x(x_in, after, s["x_ready"])
                if back:
                    need(sp, s["stats_done"], m)
                    sp.dma_start(x1_dram[bass.ds((m - 1) * WS, WS)].rearrange("r w c -> w r c"),
                                 x1[:]).then_inc(s["x1_stored"], 16)
                    need(sp, s["yo_done"], m)
                    sp.dma_start(yv[bass.ds(before[1], 1), bass.ds(before[0], 1)].rearrange("o q f r d -> (o q f) r d"),
                                 yo[:]).then_inc(s["yo_stored"], 16)

            sp.sem_inc(s["x1_stored"], 16)
            sp.sem_inc(s["yo_stored"], 16)
            load_x(x_in, (0, 0), s["x_ready"])
            body(-1, back=False)
            body(0, back=False)
            with sp.Fori(1, blocks - 2) as m:
                body(m)
            body(blocks - 2, more=False)
            body(blocks - 1, more=False)
            body(blocks, more=False)
            sp.wait_ge(s["x1_stored"], 16 * blocks + 16)
            sp.wait_ge(s["yo_stored"], 16 * blocks + 16)

        @block.tensor
        def _(pe):
            def broadcast(bank, step, row, done):
                M, p, n = step
                q = n // NS
                pe.matmul(bank[n % 2][:], wt["select"][:, row + n % NS, :], rows[p][:, q * HT:(q + 1) * HT],
                          start=True, stop=True).then_inc(done, 1)

            def broadcast_b(step):
                M, p, n = step
                need(pe, s["b_copied"], M * NSTEP + n - 1)
                broadcast(b_bank, step, 0, s["b_full"])

            def broadcast_c(step):
                M, p, n = step
                need(pe, s["prod_done"], M * NSTEP + n - 1)
                broadcast(c_bank, step, NS, s["c_full"])

            def add_state(step):
                M, p, n = step
                if n % NS == 0:
                    need(pe, s["y_copied"], M * 2 + n // NS)
                need(pe, s["prod_done"], M * NSTEP + n + 1)
                for hf in range(2):
                    for g in range(4):
                        mm = pe.matmul(y_acc[:, g, hf * P:(hf + 1) * P], prod[n % NP][:, hf, g * P:(g + 1) * P],
                                       wt["ident"][:], start=(n % NS == 0 and hf == 0 and g % 2 == 0), stop=False,
                                       is_transpose=True, skip_group_check=True)
                mm.then_inc(s["added"], 1)

            def add_skip(p, q, g):
                for k in range(2):
                    pe.matmul(y_acc[:, g, k * P:(k + 1) * P], xc[p][:, k, q * HT + g * P:q * HT + (g + 1) * P],
                              wt["diag_d"][:, k, :], start=False, stop=False, skip_group_check=True)

            def job(S, p, name, part=0):
                m, kind, f = S.m, name.rstrip("01"), 1 - p
                misc = job_bank[S.bank[name]]
                if part == 0:
                    need(pe, job_taken[S.bank[name]], S.before[name])
                if kind == "mean":
                    q = int(name[-1])
                    need(pe, s["x_ready"], (m + 2) * 16)
                    mm = pe.matmul(misc[:].rearrange("p (r c) -> p r c", r=WS), wt["mean_w"][:],
                                   x_in[:].rearrange("p (r q c) -> p r q c", r=WS, q=2)[:, :, q, :],
                                   start=True, stop=True)
                elif kind == "var":
                    q = int(name[-1])
                    need(pe, s["sq_done"], (m + 1) * 2 + q + 1)
                    mm = pe.matmul(misc[:], wt["mean_w"][:], sq[:, q * HT:(q + 1) * HT], start=True, stop=True)
                elif kind == "conv":
                    hf, q = int(name[-2]), int(name[-1])
                    if part == 0:
                        need(pe, s["tn_done"], (m + 1) * 2 + q + 1)
                    o = misc[:].rearrange("p (w t) -> p w t", t=WT)
                    v = tn[:, q * HT:(q + 1) * HT].rearrange("p (w t) -> p w t", t=WT)
                    for k in range(2 * part, 2 * part + 2):
                        mm = pe.matmul(o[:, :, k:WT], wt["tap_w"][:, K - 1 - k, hf * P:(hf + 1) * P],
                                       v[:, :, 0:WT - k], start=(k == 0), stop=(k == K - 1), skip_group_check=True)
                elif kind == "z":
                    hf, q = int(name[-2]), int(name[-1])
                    mm = pe.matmul(misc[:], wt["z_w"][:, hf * P:(hf + 1) * P], tn[:, q * HT:(q + 1) * HT],
                                   start=True, stop=True)
                elif kind == "bc":
                    need(pe, s["silu_done"], (m + 1) * 2 + 2)
                    for g in range(BT // P):
                        for k in range(2):
                            mm = pe.matmul(misc[:, g * 32:(g + 1) * 32], xc[f][:, k, g * P:(g + 1) * P],
                                           wt["bc_w"][:, k, :], start=(g == 0 and k == 0), stop=(k == 1),
                                           skip_group_check=True)
                elif kind == "dt":
                    hf, q = int(name[-2]), int(name[-1])
                    for k in range(2):
                        mm = pe.matmul(misc[:], wt["dt_w"][:, k, hf * P:(hf + 1) * P],
                                       xc[f][:, k, q * HT:(q + 1) * HT], start=(k == 0), stop=(k == 1))
                elif kind == "rows":
                    taken(pe, S, "bc")
                    for g in range(BT // P):
                        mm = pe.matmul(misc[:].bitcast(BF16)[0:96, g * P:(g + 1) * P], bc3[:, g, :], wt["identb"][:],
                                       start=True, stop=True, is_transpose=True)
                elif kind == "turn":
                    q, hf = int(name[-2]), int(name[-1])
                    M = m if q == 0 else m - 1
                    need(pe, s["y_copied"], M * 2 + q + 1)
                    for g in range(4):
                        mm = pe.matmul(misc[:, g * P:(g + 1) * P], y_tok[q][:, g, hf * P:(hf + 1) * P], wt["ident"][:],
                                       start=True, stop=True, is_transpose=True)
                elif kind == "out":
                    q = int(name[-1])
                    taken(pe, S, "turn10")
                    taken(pe, S, "turn11")
                    need(pe, s["xres_ready"], m * 16)
                    for r in range(4):
                        row = 4 * q + r
                        o = misc[:, r * P:(r + 1) * P]
                        for k in range(2):
                            pe.matmul(o, gated[:, k, row * W:(row + 1) * W], wt["out_w"][:, k, :], start=(r == 0 and k == 0), stop=False, skip_group_check=True)
                        mm = pe.matmul(o, x_res[:, row * W:(row + 1) * W], wt["ident"][:], start=False, stop=(r == 3),
                                       is_transpose=True, skip_group_check=True)
                elif kind == "fy":
                    q = int(name[-1])
                    need(pe, s["z1_done"], m)
                    mm = pe.matmul(misc[:], wt["fy"][:], z1[:, 4 * q:4 * q + 4, :].rearrange("p r c -> p (r c)"),
                                   start=True, stop=True)
                if kind != "conv" or part == 1:
                    mm.then_inc(job_full[S.bank[name]], 1)

            def body(S, p):
                def jobs(n):
                    for name in S.at(n):
                        job(S, p, name)
                    for name in S.at(n - 1):
                        if name.startswith("conv"):
                            job(S, p, name, 1)

                for n in range(NSTEP):
                    if n == NSTEP - B_AHEAD and S.front:
                        taken(pe, S, "rows")
                    if S.step(n + B_AHEAD, p):
                        broadcast_b(S.step(n + B_AHEAD, p))
                    if S.step(n + 1, p):
                        broadcast_c(S.step(n + 1, p))
                    late = n % NS == 1
                    if late:
                        jobs(n)
                    if S.step(n - 1, p):
                        add_state(S.step(n - 1, p))
                    if not late:
                        jobs(n)
                    if n in SKIP_AT and S.scan:
                        add_skip(p, n // NS, SKIP_AT[n])

            slots(pe, body, blocks)

        @block.scalar
        def _(act):
            def copy_b(step):
                M, p, n = step
                need(act, s["drive_done"], M * NSTEP + n + 1 - since(n, NB))
                need(act, s["b_full"], M * NSTEP + n + 1)
                act.activation(b_all[n % NB][:], b_bank[n % 2][:], ACT.Copy).then_inc(s["b_copied"], 1)

            def decays(step):
                M, p, n = step
                q, st = n // NS, n % NS
                need(act, s["zeroed"], 1)
                need(act, s["delta_done"], M + 1)
                need(act, s["scan_done"], M * NSTEP + n + 1 - since(n, NA))
                for hf in range(2):
                    last = act.activation(
                        decay[n % NA][:, hf, :, 1:WT],
                        delta[p][:, hf, q * HT:(q + 1) * HT].rearrange("p (w t) -> p w t", t=WT)[:, :, 1:WT],
                        ACT.Exp, scale=wt["neg_a"][:, hf, st:st + 1])
                last.then_inc(s["decay_done"], 1)

            def chain(S, n, m, f):
                if n in (2, 3):
                    q = n - 2
                    taken(act, S, f"mean{q}")
                    act.activation(sq[:, q * HT:(q + 1) * HT], cent[:, q * HT:(q + 1) * HT],
                                   ACT.Square).then_inc(s["sq_done"], 1)
                elif n in (5, 6):
                    q = n - 5
                    misc = full(act, S, f"var{q}")
                    act.activation(sq[:, q * HT:(q + 1) * HT], misc[:], ACT.Ln,
                                   bias=EPS).then_inc(take(S, f"var{q}"), 1)
                    taken(act, S, f"var{q}")
                    act.activation(sq[:, q * HT:(q + 1) * HT], sq[:, q * HT:(q + 1) * HT], ACT.Exp,
                                   scale=-0.5).then_inc(s["rstd_done"], 1)
                elif n == 20:
                    taken(act, S, "z11")
                    act.activation(zs[f][:], zs[f][:], ACT.Silu).then_inc(s["silu_done"], 1)
                    need(act, s["edge_done"], m + 2)
                    act.activation(xc[f][:], xc[f][:], ACT.Silu).then_inc(s["silu_done"], 1)
                    act.preload_act_table_set(TABLES)
                elif n == 27:
                    need(act, s["clip_done"], m + 2)
                    act.activation(temp[:], temp[:], ACT.Exp).then_inc(s["softplus_done"], 1)
                    need(act, s["softplus_done"], (m + 1) * 2 + 1)
                    act.activation(temp[:], temp[:], ACT.Ln, bias=1.0).then_inc(s["softplus_done"], 1)
                moved = {"conv": (xc, wt["xc_b"]), "z": (zs, wt["z_b"]), "dt": (delta, wt["dt_b"])}
                for name in S.at(n - 1) + S.at(n - 2):
                    kind = name.rstrip("01")
                    if kind not in moved or (name in S.at(n - 1)) != (kind != "conv"):
                        continue
                    hf, q = int(name[-2]), int(name[-1])
                    dst, bias = moved[kind]
                    misc = full(act, S, name)
                    act.activation(dst[f][:, hf, q * HT:(q + 1) * HT], misc[:], ACT.Identity,
                                   bias=bias[:, hf:hf + 1]).then_inc(take(S, name), 1)

            def copy_y(M, q):
                need(act, s["added"], M * NSTEP + NS * (q + 1))
                act.activation(y_tok[q][:].rearrange("p g d -> p (g d)"),
                               y_acc[:].rearrange("p g d -> p (g d)"), ACT.Copy).then_inc(s["y_copied"], 1)

            def body(S, p):
                m, f = S.m, 1 - p
                for n in range(NSTEP):
                    if n == 1 and S.back:
                        copy_y(m - 1, 1)
                    if n == NS + 1 and S.scan:
                        copy_y(m, 0)
                    if S.step(n + B_AHEAD - 1, p):
                        copy_b(S.step(n + B_AHEAD - 1, p))
                    if S.step(n + A_AHEAD, p):
                        decays(S.step(n + A_AHEAD, p))
                    if S.front:
                        chain(S, n, m, f)
                    if n == 24 and S.back:
                        need(act, s["mv_done"], m)
                        act.activation(rstd1[:], mv[:, :, 1], ACT.Ln, bias=EPS).then_inc(s["rstd1_done"], 1)
                        need(act, s["rstd1_done"], (m - 1) * 2 + 1)
                        act.activation(rstd1[:], rstd1[:], ACT.Exp, scale=-0.5).then_inc(s["rstd1_done"], 1)
                    if n in (29, 30) and S.back:
                        q = n - 29
                        misc = full(act, S, f"fy{q}")
                        act.activation(yo[:, 4 * q:4 * q + 4, :].rearrange("p r c -> p (r c)"), misc[:],
                                       ACT.Copy).then_inc(take(S, f"fy{q}"), 1)
                        if q == 1:
                            taken(act, S, "fy0")
                            taken(act, S, "fy1")
                            act.sem_inc(s["yo_done"], 1)

            act.preload_act_table_set(TABLES)
            slots(act, body, blocks)

        @block.vector
        def _(dve):
            def scan(step):
                M, p, n = step
                need(dve, s["decay_done"], M * NSTEP + n + 1)
                need(dve, s["drive_done"], M * NSTEP + n + 1)
                need(dve, s["prod_done"], M * NSTEP + n + 1 - since(n, NP))
                dve.tensor_tensor_scan(state[n % NP][:].rearrange("p h t -> p (h t)"),
                                       decay[n % NA][:].rearrange("p h w t -> p (h w t)"),
                                       drive[n % ND][:].rearrange("p h t -> p (h t)"), 0.0, ALU.mult,
                                       ALU.add).then_inc(s["scan_done"], 1)

            def times_c(step):
                M, p, n = step
                need(dve, s["scan_done"], M * NSTEP + n + 1)
                need(dve, s["c_full"], M * NSTEP + n + 1)
                need(dve, s["added"], M * NSTEP + n + 1 - since(n, NP))
                dve.tensor_tensor(prod[n % NP][:], state[n % NP][:],
                                  c_bank[n % 2][:].unsqueeze(1).to_broadcast([P, 2, HT]),
                                  ALU.mult).then_inc(s["prod_done"], 1)

            def chain(S, n, m, f):
                if n in (1, 2):
                    q = n - 1
                    misc = full(dve, S, f"mean{q}")
                    need(dve, s["delta_done"], m + 1)
                    dve.tensor_tensor(
                        cent[:, q * HT:(q + 1) * HT].rearrange("p (n r c) -> p r n c", n=HWN, r=WS),
                        x_in[:].rearrange("p (r q n c) -> p r q n c", r=WS, q=2, n=HWN)[:, :, q],
                        misc[:].rearrange("p (r n c) -> p r n c", r=WS, n=HWN),
                        ALU.subtract).then_inc(take(S, f"mean{q}"), 1)
                elif n in (6, 7):
                    q = n - 6
                    need(dve, s["rstd_done"], (m + 1) * 2 + q + 1)
                    dve.tensor_tensor(tn[:, q * HT:(q + 1) * HT], cent[:, q * HT:(q + 1) * HT],
                                      sq[:, q * HT:(q + 1) * HT], ALU.mult).then_inc(s["tn_done"], 1)
                elif n == 22:
                    misc = full(dve, S, "bc")
                    v = misc[:, 0:256].rearrange("p (g i) -> p g i", i=2 * NS)
                    steps = [
                        lambda: dve.tensor_copy(bc3[:, :, 0:32], v),
                        lambda: dve.tensor_tensor(rest[:, 0], v, bc3[:, :, 0:32], ALU.subtract),
                        lambda: dve.tensor_copy(bc3[:, :, 32:64], rest[:, 0]),
                        lambda: dve.tensor_tensor(rest[:, 1], rest[:, 0], bc3[:, :, 32:64], ALU.subtract),
                    ]
                    for i, step in enumerate(steps):
                        step().then_inc(s["split_done"], 1)
                        need(dve, s["split_done"], (m + 1) * 4 + i + 1)
                    dve.tensor_copy(bc3[:, :, 64:96], rest[:, 1]).then_inc(take(S, "bc"), 1)
                elif n == 25:
                    misc = full(dve, S, "rows")
                    dve.tensor_copy(rows[f][:], misc[:].bitcast(BF16)[0:96, :]).then_inc(take(S, "rows"), 1)
                elif n == 26:
                    taken(dve, S, "dt01")
                    taken(dve, S, "dt11")
                    dve.tensor_scalar(temp[:].rearrange("p (k t) -> p k t", k=2), delta[f][:], CLIP, None,
                                      ALU.min).then_inc(s["clip_done"], 1)
                elif n == 28:
                    need(dve, s["softplus_done"], (m + 1) * 2 + 2)
                    dve.tensor_tensor(delta[f][:], delta[f][:], temp[:].rearrange("p (k t) -> p k t", k=2),
                                      ALU.max).then_inc(s["delta_done"], 1)

            def gate(S, q, hf, par):
                misc = full(dve, S, f"turn{q}{hf}")
                by_window = "p (n r c) -> p n r c"
                dve.tensor_tensor(
                    gated[:, hf, :].rearrange("p (r q n c) -> p q n r c", r=WS, q=2, n=HWN)[:, q],
                    misc[:].rearrange(by_window, n=HWN, r=WS),
                    zs[par][:, hf, q * HT:(q + 1) * HT].rearrange(by_window, n=HWN, r=WS),
                    ALU.mult).then_inc(take(S, f"turn{q}{hf}"), 1)

            def behind(S, n, m, f):
                if n in (3, 4):
                    gate(S, 1, n - 3, f)
                elif n in (20, 21):
                    q = n - 20
                    misc = full(dve, S, f"out{q}")
                    need(dve, s["x1_stored"], m * 16)
                    dve.tensor_tensor(x1[:, 4 * q:4 * q + 4, :], misc[:].rearrange("p (r c) -> p r c", r=4),
                                      wt["out_b"][:].unsqueeze(1).to_broadcast([P, 4, C]),
                                      ALU.add).then_inc(take(S, f"out{q}"), 1)
                elif n == 22:
                        taken(dve, S, "out0")
                        taken(dve, S, "out1")
                        for r in range(WS):
                            last = dve.bn_stats(stats[:, r, :], x1[:, r, :])
                        last.then_inc(s["stats_done"], 1)
                elif n == 23:
                    for r in range(WS):
                        last = dve.bn_aggr(mv[:, r, :], stats[:, r, :])
                    last.then_inc(s["mv_done"], 1)
                elif n == 25:
                    need(dve, s["yo_stored"], m * 16)
                    need(dve, s["rstd1_done"], m * 2)
                    for r in range(WS):
                        last = dve.tensor_scalar(z1[:, r, :], x1[:, r, :], mv[:, r, 0:1], rstd1[:, r:r + 1],
                                                 ALU.subtract, ALU.mult)
                    last.then_inc(s["z1_done"], 1)

            def body(S, p):
                for n in range(NSTEP):
                    if S.back and n == 23:
                        need(dve, s["stats_done"], S.m)
                    if S.step(n, p):
                        scan(S.step(n, p))
                    if S.step(n - 1, p):
                        times_c(S.step(n - 1, p))
                    if S.front:
                        chain(S, n, S.m, 1 - p)
                    if S.scan and n in (27, 28):
                        gate(S, 0, n - 27, p)
                    if S.back:
                        behind(S, n, S.m, 1 - p)

            for i in range(NA):
                last = dve.memset(decay[i][:].rearrange("p i w t -> p (i w t)"), 0.0)
            last.then_inc(s["zeroed"], 1)
            slots(dve, body, blocks)

        @block.gpsimd
        def _(pool):
            def drives(step):
                M, p, n = step
                q = n // NS
                need(pool, s["du_done"], M * 2 + 1 + q)
                need(pool, s["b_copied"], M * NSTEP + n + 1)
                need(pool, s["scan_done"], M * NSTEP + n + 1 - since(n, ND))
                pool.tensor_tensor(drive[n % ND][:], du[:, :, q * HT:(q + 1) * HT],
                                   b_all[n % NB][:].unsqueeze(1).to_broadcast([P, 2, HT]),
                                   ALU.mult).then_inc(s["drive_done"], 1)

            def make_du(S, q, f):
                need(pool, s["delta_done"], S.m + 2)
                need(pool, s["drive_done"], S.m * NSTEP + NS * (q + 1))
                pool.tensor_tensor(du[:, :, q * HT:(q + 1) * HT], delta[f][:, :, q * HT:(q + 1) * HT],
                                   xc[f][:, :, q * HT:(q + 1) * HT], ALU.mult).then_inc(s["du_done"], 1)

            def body(S, p):
                m, f = S.m, 1 - p
                for n in range(NSTEP):
                    if n == NSTEP - D_AHEAD and S.front:
                        make_du(S, 0, f)
                    if S.step(n + D_AHEAD, p):
                        drives(S.step(n + D_AHEAD, p))
                    if n == 19 and S.front:
                        taken(pool, S, "conv01")
                        taken(pool, S, "conv11")
                        v = xc[f][:].rearrange("p k (w t) -> p k w t", t=WT)[:, :, :, 0:K - 1]
                        pool.tensor_tensor(v, v, wt["edge"][:].unsqueeze(2).to_broadcast([P, 2, NW, K - 1]),
                                           ALU.add).then_inc(s["edge_done"], 1)
                    if n == NSTEP - 1 and S.front:
                        make_du(S, 1, f)

            slots(pool, body, blocks)


def spectral(nc, wt, y_dram, phi_dram, t_dram):
    with ExitStack() as ctx:
        def sb(name, shape):
            return ctx.enter_context(nc.sbuf_tensor(name, shape, F32))

        def psum(name, shape):
            return ctx.enter_context(nc.psum_tensor(name, shape, F32))

        def sem(name):
            return ctx.enter_context(nc.semaphore(name))

        N = B * P
        LG = 4
        NG = L // LG
        ys = [sb(f"ys{i}", [P, 2, B, C]) for i in range(2)]
        filt = [sb(f"filt{i}", [P, 3, L, P]) for i in range(2)]
        spec = [sb(f"spec{i}", [P, 3, B, P]) for i in range(2)]
        u1 = sb("u1", [P, LG, B, P])
        u2 = [sb(f"u2_{i}", [P, LG, B, P]) for i in range(2)]
        u3 = [sb(f"u3_{i}", [P, LG, B, P]) for i in range(2)]
        mixed = sb("mixed", [P, 2, N])
        turned_s = sb("turned_s", [P, 2, N])
        tt = [sb(f"tt{i}", [P, 2, N]) for i in range(2)]

        x_bank = psum("x_bank", [P, 4, 2, P])
        s_bank = [psum(f"s_bank{i}", [P, 2, N]) for i in range(2)]
        way = psum("way", [P, 2, N])

        names = """cols_done spec_done sum_done u1_done u2_by_dve u2_by_pool u3_done im_done re_done
            theta_done mixed_done turn_done turned_done inv_done tt_done dc_done""".split()
        s = {n: sem(n) for n in names}
        ys_ready, filt_ready, tt_stored = ([sem(f"{n}{i}") for i in range(2)] for n in
                                           ("ys_ready", "filt_ready", "tt_stored"))

        def rounds(eng, body):
            body(-1, -1, 1, True, False, False)
            body(0, 0, 0, True, True, False)
            body(1, 0, 1, True, True, True)
            with eng.Fori(1, (KY - 1) // 2) as j:
                for i in range(2):
                    body(j * 2 + i, j, i, True, True, True)
            body(KY - 1, (KY - 1) // 2, 0, False, True, True)
            body(KY, KY // 2, 1, False, False, True)

        block = ctx.enter_context(nc.Block())

        @block.sync
        def _(sp):
            def load_ys(k, half, p, im_row=None):
                need(sp, s["cols_done"], k - 1)
                for i, row in enumerate((k, k + KY - 1 if im_row is None else im_row)):
                    sp.dma_start(ys[p][:, i].rearrange("x b d -> x (b d)"),
                                 y_dram[bass.ds(row, 1)].rearrange("o x b d -> (o x) (b d)")).then_inc(ys_ready[p], 16)

            def load_filt(k, p):
                need(sp, s["theta_done"], (k - 1) * NG)
                sp.dma_start(filt[p][:].rearrange("p t l x -> p (t l x)"),
                             phi_dram[bass.ds(k, 1)].to_broadcast([P, 3 * L * P])).then_inc(filt_ready[p], 16)

            def body(k, half, p, columns, products, back, more=True):
                if columns:
                    load_filt(k + 1, 1 - p)
                    if more:
                        load_ys(k + 2, half + 1, p)
                if back:
                    need(sp, s["tt_done"], k * 2)
                    for i, row in enumerate((k - 1, KY - 1 + (k - 1) if not (isinstance(k, int) and k == 1) else P)):
                        sp.dma_start(t_dram[bass.ds(row, 1)].rearrange("o x b d -> (o x) (b d)"),
                                     tt[1 - p][:, i]).then_inc(tt_stored[1 - p], 16)

            for i in range(2):
                sp.sem_inc(tt_stored[i], 32)
            load_ys(0, 0, 0, im_row=P)
            body(-1, -1, 1, True, False, False)
            body(0, 0, 0, True, True, False)
            body(1, 0, 1, True, True, True)
            with sp.Fori(1, (KY - 3) // 2) as j:
                for i in range(2):
                    body(j * 2 + i, j, i, True, True, True)
            body(KY - 3, (KY - 3) // 2, 0, True, True, True)
            body(KY - 2, (KY - 3) // 2, 1, True, True, True, more=False)
            body(KY - 1, 0, 0, False, True, True)
            body(KY, 0, 1, False, False, True)
            sp.wait_ge(tt_stored[0], 32 * ((KY + 1) // 2) + 32)
            sp.wait_ge(tt_stored[1], 32 * (KY // 2) + 32)

        @block.tensor
        def _(pe):
            def columns(k, half, p):
                pe.wait_ge(ys_ready[p], (half + 1) * 32)
                need(pe, s["spec_done"], k * 2)
                for b in range(B):
                    for i in range(2):
                        mm = pe.matmul(x_bank[:, b].rearrange("p c x -> p (c x)"), ys[p][:, i, b, :],
                                       wt["fx"][:, 2 * i:2 * i + 2, :].rearrange("p c x -> p (c x)"),
                                       start=(b % 2 == 0 and i == 0), stop=(i == 1), skip_group_check=True)
                mm.then_inc(s["cols_done"], 1)

            def theta(k, p, g):
                if g == 0:
                    need(pe, s["mixed_done"], (k - 1) * 2)
                for part, done, src in ((0, "re_done", u3), (1, "im_done", u2)):
                    need(pe, s[done], k * NG + g + 1)
                    for i in range(LG):
                        l = LG * g + i
                        mm = pe.matmul(s_bank[p][:, part, :], wt["theta"][:, l, :],
                                       src[g % 2][:, i].rearrange("p b x -> p (b x)"),
                                       start=(l == 0), stop=(l == L - 1))
                mm.then_inc(s["theta_done"], 1)

            def turn(k):
                need(pe, s["mixed_done"], k * 2 + 2)
                need(pe, s["tt_done"], k * 2)
                for part in range(2):
                    for b in range(B):
                        mm = pe.matmul(way[:, part, b * P:(b + 1) * P], mixed[:, part, b * P:(b + 1) * P],
                                       wt["ident"][:], start=True, stop=True, is_transpose=True)
                mm.then_inc(s["turn_done"], 1)

            def inverse(k):
                need(pe, s["turned_done"], k * 2 + 2)
                for part in range(2):
                    pe.matmul(way[:, part, :], wt["ix"][:, part, :], turned_s[:, 0, :], start=True, stop=False)
                    mm = pe.matmul(way[:, part, :], wt["ix"][:, 2 if part == 0 else 0, :], turned_s[:, 1, :],
                                   start=False, stop=True)
                mm.then_inc(s["inv_done"], 1)

            def body(k, half, p, col, products, back):
                if col:
                    columns(k + 1, half + p, 1 - p)
                for g in range(NG):
                    if products:
                        theta(k, p, g)
                    if back and g == 0:
                        turn(k - 1)
                    if back and g == 2:
                        inverse(k - 1)

            rounds(pe, body)

        @block.scalar
        def _(act):
            def take_spec(k, p):
                need(act, s["cols_done"], k + 1)
                need(act, s["theta_done"], (k - 1) * NG)
                for i in range(2):
                    act.activation(spec[p][:, 0:2, 2 * i:2 * i + 2, :],
                                   x_bank[:, 2 * i:2 * i + 2].rearrange("p b c x -> p c b x"), ACT.Copy,
                                   scale=wt["gamma"][:, 0:1]).then_inc(s["spec_done"], 1)

            def copy2(dst, src, done):
                for i in range(2):
                    act.activation(dst[:, i, :], src[:, i, :], ACT.Copy).then_inc(s[done], 1)

            def body(k, half, p, columns, products, back):
                if columns:
                    take_spec(k + 1, 1 - p)
                if back:
                    need(act, s["turn_done"], k)
                    copy2(turned_s, way, "turned_done")
                    need(act, s["inv_done"], k)
                    need(act, tt_stored[1 - p], (half + p) * 32)
                    copy2(tt[1 - p], way, "tt_done")
                if products:
                    need(act, s["theta_done"], k * NG + NG)
                    need(act, s["turn_done"], k)
                    copy2(mixed, s_bank[p], "mixed_done")

            rounds(act, body)

        def times(eng, dst, src, kind, g, k, p):
            return eng.tensor_tensor(
                dst[:], spec[p][:, kind[0]].unsqueeze(1).to_broadcast([P, LG, B, P]),
                filt[p][:, kind[1], LG * g:LG * g + LG, :].unsqueeze(2).to_broadcast([P, LG, B, P]), ALU.mult)

        @block.vector
        def _(dve):
            def total(k, p):
                need(dve, s["spec_done"], k * 2 + 2)
                need(dve, s["u1_done"], (k - 1) * NG)
                if isinstance(k, int) and k == 0:
                    dc = spec[p][:, 0, :, 0]
                    dve.tensor_scalar(dc, dc, wt["dc"][:, 0:1], None, ALU.add).then_inc(s["dc_done"], 1)
                    dve.wait_ge(s["dc_done"], 1)
                dve.tensor_tensor(spec[p][:, 2], spec[p][:, 0], spec[p][:, 1], ALU.add).then_inc(s["sum_done"], 1)

            def body(k, half, p, columns, products, back):
                if products:
                    dve.wait_ge(filt_ready[p], (half + 1) * 16)
                    for g in range(NG):
                        n = k * NG + g
                        need(dve, s["sum_done"], k + 1)
                        need(dve, s["im_done"], n)
                        need(dve, s["re_done"], n)
                        times(dve, u1, spec, (2, 0), g, k, p).then_inc(s["u1_done"], 1)
                        if g % 2 == 0:
                            need(dve, s["theta_done"], n - 1)
                            times(dve, u2[0], spec, (0, 1), g, k, p).then_inc(s["u2_by_dve"], 1)
                        need(dve, s["u3_done"], n + 1)
                        need(dve, s["u1_done"], n + 1)
                        dve.tensor_tensor(u3[g % 2][:], u1[:], u3[g % 2][:], ALU.subtract).then_inc(s["re_done"], 1)
                        if g % 2 == 0:
                            need(dve, s["u2_by_dve"], k * 2 + g // 2 + 1)
                        else:
                            need(dve, s["u2_by_pool"], k * 2 + g // 2 + 1)
                        dve.tensor_tensor(u2[g % 2][:], u1[:], u2[g % 2][:], ALU.subtract).then_inc(s["im_done"], 1)
                        if g == 1 and columns:
                            total(k + 1, 1 - p)
                elif columns:
                    total(k + 1, 1 - p)

            rounds(dve, body)

        @block.gpsimd
        def _(pool):
            def body(k, half, p, columns, products, back):
                if products:
                    pool.wait_ge(filt_ready[p], (half + 1) * 16)
                    need(pool, s["sum_done"], k + 1)
                    for g in range(NG):
                        n = k * NG + g
                        need(pool, s["theta_done"], n - 1)
                        times(pool, u3[g % 2], spec, (1, 2), g, k, p).then_inc(s["u3_done"], 1)
                        if g % 2 == 1:
                            times(pool, u2[1], spec, (0, 1), g, k, p).then_inc(s["u2_by_pool"], 1)

            rounds(pool, body)


def mlp(nc, wt, t_dram, x1_dram, out):
    with ExitStack() as ctx:
        def sb(name, shape):
            return ctx.enter_context(nc.sbuf_tensor(name, shape, F32))

        def psum(name, shape):
            return ctx.enter_context(nc.psum_tensor(name, shape, F32))

        def sem(name):
            return ctx.enter_context(nc.semaphore(name))

        R = 4
        T = R * W
        NGR = H // R
        tk = [sb(f"tk{i}", [P, R, B, C]) for i in range(2)]
        x1t = [sb(f"x1t{i}", [P, B, R, C]) for i in range(2)]
        mix = [sb(f"mix{i}", [P, T]) for i in range(2)]
        hid = [sb(f"hid{i}", [P, 2, T]) for i in range(2)]
        res = [sb(f"res{i}", [P, T]) for i in range(2)]
        mix_bank = [psum(f"mix_bank{i}", [P, T]) for i in range(2)]
        hid_bank = [psum(f"hid_bank{i}", [P, 2, T]) for i in range(2)]
        res_bank = [psum(f"res_bank{i}", [P, T]) for i in range(2)]

        names = "rows_done mix_done up_done hid_done down_done res_done".split()
        s = {n: sem(n) for n in names}
        tk_ready, x1_ready, res_stored = ([sem(f"{n}{i}") for i in range(2)] for n in
                                          ("tk_ready", "x1_ready", "res_stored"))

        def steps(eng, body):
            body(-2, -1, 6, True, False, False)
            body(-1, -1, 7, True, True, False)
            for i in range(2 * B):
                body(i, 0, i, True, True, True)
            with eng.Fori(1, NGR // 2 - 1) as j:
                for i in range(2 * B):
                    body(j * (2 * B) + i, j, i, True, True, True)
            last = NGR // 2 - 1
            for i in range(2 * B):
                body(last * 2 * B + i, last, i, i < 2 * B - 2, i < 2 * B - 1, True)

        block = ctx.enter_context(nc.Block())
        x1v = x1_dram.rearrange("(b x) y c -> b y x c", b=B)
        ov = out.rearrange("b d x y -> b d (x y)")

        @block.sync
        def _(sp):
            def load(g, p):
                need(sp, s["rows_done"], (g - 1) * B)
                sp.dma_start(tk[p][:].rearrange("p x b h -> p (x b h)"),
                             t_dram[0:P, bass.ds(g * R, R)].rearrange("f x b h -> f (x b h)")).then_inc(tk_ready[p], 16)
                need(sp, s["down_done"], (g - 1) * B)
                for b in range(B):
                    sp.dma_start(x1t[p][:, b], x1v[b, :, bass.ds(g * R, R), :]).then_inc(x1_ready[p], 16)

            def body(g, p, more):
                if more:
                    load(g + 1, 1 - p)
                for b in range(B):
                    need(sp, s["res_done"], g * B + b + 1)
                    sp.dma_start(ov[b, :, bass.ds(g * T, T)], res[b % 2][:]).then_inc(res_stored[b % 2], 16)

            load(0, 0)
            body(0, 0, True)
            body(1, 1, True)
            with sp.Fori(1, NGR // 2 - 1) as j:
                for i in range(2):
                    body(j * 2 + i, i, True)
            body(NGR - 2, 0, True)
            body(NGR - 1, 1, False)
            for i in range(2):
                sp.wait_ge(res_stored[i], 16 * NGR * B // 2)

        @block.tensor
        def _(pe):
            def rows(u, j, i):
                p, b = i // B, i % B
                pe.wait_ge(tk_ready[p], (j + 1) * 16)
                need(pe, s["mix_done"], u - 1)
                for r in range(R):
                    mm = pe.matmul(mix_bank[i % 2][:, r * W:(r + 1) * W], tk[p][:, r, b, :], wt["iy"][:],
                                   start=True, stop=True)
                mm.then_inc(s["rows_done"], 1)

            def up(u, i):
                need(pe, s["mix_done"], u + 1)
                need(pe, s["hid_done"], (u - 1) * 2)
                for k in range(2):
                    mm = pe.matmul(hid_bank[i % 2][:, k, :], wt["w1"][:, k, :], mix[i % 2][:], start=True, stop=True)
                mm.then_inc(s["up_done"], 1)

            def down(u, j, i):
                p, b = i // B, i % B
                need(pe, s["hid_done"], u * 2 + 2)
                need(pe, s["res_done"], u - 1)
                pe.wait_ge(x1_ready[p], (j + 1) * 16 * B)
                for k in range(2):
                    pe.matmul(res_bank[i % 2][:], wt["w2"][:, k, :], hid[i % 2][:, k, :], start=(k == 0), stop=False,
                              skip_group_check=True)
                for r in range(R):
                    mm = pe.matmul(res_bank[i % 2][:, r * W:(r + 1) * W], x1t[p][:, b, r, :], wt["ident"][:],
                                   start=False, stop=(r == R - 1), is_transpose=True, skip_group_check=True)
                mm.then_inc(s["down_done"], 1)

            def body(u, j, i, has_rows, has_up, has_down):
                if has_rows:
                    rows(u + 2, j + (i + 2) // (2 * B), (i + 2) % (2 * B))
                if has_up:
                    up(u + 1, (i + 1) % (2 * B))
                if has_down:
                    down(u, j, i)

            steps(pe, body)

        @block.scalar
        def _(act):
            def body(u, j, i, has_rows, has_up, has_down):
                if has_up:
                    v, i = u + 1, (i + 1) % (2 * B)
                    need(act, s["up_done"], v + 1)
                    need(act, s["down_done"], v - 1)
                    for k in range(2):
                        act.activation(hid[i % 2][:, k, :], hid_bank[i % 2][:, k, :], ACT.Gelu,
                                       bias=wt["b1"][:, k:k + 1]).then_inc(s["hid_done"], 1)

            steps(act, body)

        @block.vector
        def _(dve):
            def body(u, j, i, has_rows, has_up, has_down):
                if has_rows:
                    v, iv = u + 2, (i + 2) % (2 * B)
                    need(dve, s["rows_done"], v + 1)
                    need(dve, s["up_done"], v - 1)
                    dve.tensor_copy(mix[iv % 2][:], mix_bank[iv % 2][:]).then_inc(s["mix_done"], 1)
                if has_down:
                    need(dve, s["down_done"], u + 1)
                    need(dve, res_stored[i % 2], (j * B + i // 2) * 16)
                    dve.tensor_scalar(res[i % 2][:], res_bank[i % 2][:], wt["b2"][:, 0:1], None,
                                      ALU.add).then_inc(s["res_done"], 1)

            steps(dve, body)


_INS = {
    "x": "x", "ln_g": "L0_conv_ln_g", "ln_b": "L0_conv_ln_b", "W_in": "L0_conv_W_in", "b_in": "L0_conv_b_in",
    "conv_w": "L0_conv_conv_w", "conv_b": "L0_conv_conv_b", "W_x": "L0_conv_W_x", "dt_w": "L0_conv_dt_w",
    "dt_b": "L0_conv_dt_b", "A_log": "L0_conv_A_log", "D": "L0_conv_D", "W_out": "L0_conv_W_out",
    "b_out": "L0_conv_b_out", "Phi_f_real": "L1_conv_Phi_f_real", "Phi_f_imag": "L1_conv_Phi_f_imag",
    "Theta": "L1_conv_Theta", "ln_gamma": "L1_conv_ln_gamma", "ln_beta": "L1_conv_ln_beta",
    "W1": "L1_conv_W1", "b1": "L1_conv_b1", "W2": "L1_conv_W2", "b2": "L1_conv_b2",
}


def transforms():
    n = np.arange(P)
    angle = 2 * np.pi * (np.outer(n, n) % P) / P
    c, s = np.cos(angle), np.sin(angle)
    fy = np.concatenate([c[:, :KY], -s[:, 1:KY - 1]], axis=1)
    fx = np.stack([c, -s, s, c], axis=1)
    ix = np.stack([c, s, -s], axis=1)
    once = np.where((n[:KY] == 0) | (n[:KY] == KY - 1), 1.0, 2.0)[:, None]
    iy = np.concatenate([once * c[:KY], -2 * s[1:KY - 1]], axis=0) / (H * W)
    return {k: np.ascontiguousarray(v, dtype=np.float32) for k, v in dict(fy=fy, fx=fx, ix=ix, iy=iy).items()}


def kernel(**inputs):
    import concourse.bacc as _bacc
    from concourse.bass_utils import run_bass_kernel_spmd as _run

    nc = _bacc.Bacc("TRN2", target_bir_lowering=False, num_devices=1)
    arrays, args = {}, {}
    given = {k: np.ascontiguousarray(inputs[v]) for k, v in _INS.items()}
    for name, v in {**given, **transforms()}.items():
        arrays[f"in_{name}_dram"] = v
        args[name] = nc.dram_tensor(f"in_{name}_dram", v.shape, mybir.dt.from_np(v.dtype), kind="ExternalInput").ap()
    out = nc.dram_tensor("out_0_dram", (B, C, H, W), F32, kind="ExternalOutput").ap()
    conv_seq_program(nc, args, out)
    r = _run(nc, [arrays], core_ids=[0])
    return r.results[0]["out_0_dram"]
```

```python
from contextlib import ExitStack

import concourse.bass as bass
import numpy as np
from concourse import mybir

ALU = mybir.AluOpType
ACT = mybir.ActivationFunctionType
F32 = mybir.dt.float32
BF16 = mybir.dt.bfloat16
F32R = mybir.dt.float32r

P = 128
B = 4
C = 128
H = W = 128
WS = 8
WT = WS * WS
NW = W // WS
BT = WS * W
KB = H // WS
NM = B * KB
HT = BT // 2
HWN = NW // 2
DI = 256
NS = 16
RANK = 8
XP = RANK + 2 * NS
K = 4
NSTEP = 2 * NS
L = 16
KY = W // 2 + 1
UNITS = L
BY_POOL = (1, 3, 6, 9, 12, 14)
BY_DVE = [u for u in range(UNITS) if u not in BY_POOL]
COLUMNS = {5: 0, 11: 1}
BACK = {8: 0, 14: 1}
MIX_AFTER, SPLIT_AFTER = 2, 8
EPS = 1e-5
RINGS = (5, 6, 4, 3, 3)
TABLES = "natural_log_exp_and_others"
B_AHEAD, COPY_AHEAD, A_AHEAD, D_AHEAD = (7, 4), (5, 4), (3, 3), (2, 1)

JOBS = [
    (0, "conv00", "front"), (0, "turn10", "back"), (2, "turn11", "back"), (2, "dt01", "scan"),
    (5, "z00", "front"), (6, "dt11", "scan"), (7, "conv10", "front"), (9, "z10", "front"),
    (10, "conv01", "front"), (10, "z01", "front"), (12, "out0", "back"), (14, "conv11", "front"),
    (16, "out1", "back"), (16, "turn00", "scan"), (17, "z11", "front"), (19, "xproj", "front"),
    (19, "turn01", "scan"), (21, "mean0", "ahead"), (21, "rows", "front"), (23, "mean1", "ahead"),
    (24, "dt00", "front"), (24, "var0", "ahead"), (25, "dt10", "front"), (27, "var1", "ahead"),
    (28, "fy0", "back"), (29, "fy1", "back"),
]
SKIP_AT = {3: 0, 4: 1, 15: 2, 6: 3, 26: 0, 21: 1, 22: 2, 30: 3}
AT = {
    "square": (25, 26), "deviation": (27, 28), "take_conv": 2, "take_z": 1, "silu": 18, "take_rows": 24,
    "take_dt0": (26, 27), "softplus0": 27, "take_dt1": (4, 7), "softplus1": 8, "copy_y": (18, 1),
    "deviation1": 22, "z1_by_act": 23, "yo": (29, 30),
    "centre": (23, 24), "split": 21, "add_soft0": 28, "add_soft1": 13, "gate0": (19, 22), "gate1": (3, 5),
    "x1": (15, 18), "stats": 18, "mean_var": 19, "z1_by_dve": 22,
    "tn": (30, 31), "edge": 17, "du1": 13,
}


class Slot:

    def __init__(self, m, ahead, front, scan, back, rounds):
        self.m, self.ahead, self.front, self.scan, self.back = m, ahead, front, scan, back
        on = {"ahead": ahead, "front": front, "scan": scan, "back": back}
        mine = [j for j in JOBS if on[j[2]]]
        self.bank = {j[1]: i % 2 for i, j in enumerate(mine)}
        self.before = {j[1]: rounds + i // 2 for i, j in enumerate(mine)}
        self.rounds = len(mine) // 2
        self.names = {j[1] for j in mine}

    def at(self, n):
        return [name for step, name, _ in JOBS if step == n and name in self.names]

    def step(self, n, p):
        if n >= NSTEP:
            return (self.m + 1, 1 - p, n - NSTEP) if self.front else None
        if n < 0:
            return (self.m - 1, 1 - p, n + NSTEP) if self.back else None
        return (self.m, p, n) if self.scan else None

    def due(self, n, p, ahead):
        by, start = ahead
        first = NSTEP if n == NSTEP - start else n + by
        if NSTEP <= n + by and n < NSTEP - start:
            return []
        return [self.step(k, p) for k in range(first, n + by + 1) if self.step(k, p)]


def slots(eng, body, blocks):
    rounds = 0
    for m in range(-2, 2):
        slot = Slot(m, True, m >= -1, m >= 0, m >= 1, rounds)
        body(slot, m % 2)
        rounds += slot.rounds
    per = len(JOBS) // 2
    with eng.Fori(0, (blocks - 4) // 2) as j:
        for i in range(2):
            body(Slot(j * 2 + 2 + i, True, True, True, True, j * (2 * per) + rounds + per * i), i)
    rounds += per * (blocks - 4)
    for m in range(blocks - 2, blocks + 1):
        slot = Slot(m, False, m < blocks - 1, m < blocks, True, rounds)
        body(slot, m % 2)
        rounds += slot.rounds


def since(n, ring):
    return next(d for d in range(1, NSTEP) if (n - d) % NSTEP % ring == n % ring)


def need(eng, sem, value):
    if isinstance(value, int) and value <= 0:
        return
    eng.wait_ge(sem, value)


def conv_seq_program(nc, a, out, blocks=NM, layer1=True):
    x1_dram = nc.dram_tensor("x1_rows", [B * H, W, C], F32).ap()
    y_dram = nc.dram_tensor("row_spectra", [P + 1, H, B, C], F32).ap()
    phi_dram = nc.dram_tensor("filters", [KY, P, 3 * L], F32).ap()
    t_dram = nc.dram_tensor("column_sums", [P + 1, H, B, C], F32).ap()

    with ExitStack() as whole:
        wt = weights(nc, whole)
        setup(nc, a, wt, phi_dram, y_dram)
        layer0(nc, a, wt, x1_dram, y_dram, blocks)
        if layer1:
            spectral(nc, wt, y_dram, phi_dram, t_dram)
            mlp(nc, wt, t_dram, x1_dram, out)


def weights(nc, ctx):
    def sb(name, shape, dt=F32):
        return ctx.enter_context(nc.sbuf_tensor(name, shape, dt))

    return {
        "ident": sb("ident", [P, P]), "identb": sb("identb", [P, P], BF16),
        "mean_w": sb("mean_w", [P, P]),
        "select": sb("select", [3 * XP, 2 * NS, P], BF16),
        "tap_w": sb("tap_w", [P, K, DI]),
        "z_w": sb("z_w", [P, DI]), "z_b": sb("z_b", [P, 2]),
        "xc_b": sb("xc_b", [P, 2]), "edge": sb("edge", [P, 2, K - 1]),
        "xp_w": sb("xp_w", [P, 2, XP]),
        "dt_parts": sb("dt_parts", [3 * XP, 3, DI], BF16),
        "dt_b": sb("dt_bias", [P, 2]), "neg_a": sb("neg_a", [P, 2, NS]),
        "diag_d": sb("diag_d", [P, 2, P]), "out_w": sb("out_w", [P, 2, C]),
        "out_b": sb("out_b_rows", [P, C]), "fy": sb("fy", [P, P]),
        "fx": sb("fx", [P, 4, P]), "ix": sb("ix", [P, 3, P]), "iy": sb("iy", [P, P]),
        "theta": sb("theta_t", [P, L, C]), "gamma": sb("gamma", [P, 1]), "dc": sb("dc", [P, 1]),
        "w1": sb("w1_t", [P, 2, P]), "b1": sb("b1_cols", [P, 2]),
        "w2": sb("w2_t", [P, 2, C]), "b2": sb("b2_col", [P, 1]),
    }


def setup(nc, a, wt, phi_dram, y_dram):
    with ExitStack() as ctx:
        def sb(name, shape, dt=F32):
            return ctx.enter_context(nc.sbuf_tensor(name, shape, dt))

        def sem(name):
            return ctx.enter_context(nc.semaphore(name))

        w_in = sb("w_in", [P, 2 * DI])
        gain = sb("gain", [P, 1])
        shift = sb("shift", [P, 1])
        b_in = sb("b_in", [P, 4])
        conv_w = sb("conv_w", [P, 2, K])
        conv_b = sb("conv_b", [P, 2])
        dt_rows = sb("dt_rows", [3 * XP, DI])
        dt_rest = sb("dt_rest", [3 * XP, 2, DI])
        a_log = sb("a_log", [P, 2, NS])
        d_col = sb("d_col", [P, 2])
        bo_col = sb("bo_col", [P, 1])
        w1_rows = sb("w1_rows", [P, 2, C])
        w2_rows = sb("w2_rows", [P, DI])
        th_rows = sb("th_rows", [P, L, C])
        beta = sb("beta", [P, 1])
        phi = sb("phi", [P, 2, L, KY])
        zeros = sb("zeros", [P, B * C])
        phi_t = sb("phi_t", [P, KY, 3, L])
        b_fold = sb("b_fold", [P, 4])
        tap_sum = sb("tap_sum", [P, 2, K])
        edge0 = sb("edge0", [P, 2])
        ps = [ctx.enter_context(nc.psum_tensor(f"set{i}", [P, 512], F32)) for i in range(2)]

        loads = [
            (w_in[:], a["W_in"]), (gain[:], a["ln_g"].rearrange("(p o) -> p o", o=1)),
            (shift[:], a["ln_b"].rearrange("(p o) -> p o", o=1)),
            (b_in[:], a["b_in"].rearrange("(k p) -> p k", p=P)),
            (conv_w[:], a["conv_w"].rearrange("(k p) t -> p k t", p=P)),
            (conv_b[:], a["conv_b"].rearrange("(k p) -> p k", p=P)),
            (wt["xp_w"][:], a["W_x"].rearrange("(k p) n -> p k n", p=P)),
            (wt["dt_b"][:], a["dt_b"].rearrange("(k p) -> p k", p=P)),
            (a_log[:], a["A_log"].rearrange("(k p) n -> p k n", p=P)),
            (d_col[:], a["D"].rearrange("(k p) -> p k", p=P)),
            (wt["out_w"][:], a["W_out"].rearrange("(k p) n -> p k n", p=P)),
            (bo_col[:], a["b_out"].rearrange("(p o) -> p o", o=1)),
            (w1_rows[:], a["W1"].rearrange("(k p) n -> p k n", p=P)), (w2_rows[:], a["W2"]),
            (th_rows[:], a["Theta"].rearrange("l h d -> h l d")),
            (wt["gamma"][:], a["ln_gamma"].rearrange("(p o) -> p o", o=1)),
            (beta[:], a["ln_beta"].rearrange("(p o) -> p o", o=1)),
            (wt["b1"][:], a["b1"].rearrange("(k p) -> p k", p=P)),
            (wt["b2"][:], a["b2"].rearrange("(p o) -> p o", o=1)),
            (phi[:, 0], a["Phi_f_real"].rearrange("l x y -> x l y")),
            (phi[:, 1], a["Phi_f_imag"].rearrange("l x y -> x l y")),
            (wt["fy"][:], a["fy"]), (wt["fx"][:], a["fx"]), (wt["ix"][:], a["ix"]), (wt["iy"][:], a["iy"]),
        ] + [(dt_rows[part * XP:part * XP + RANK], a["dt_w"]) for part in range(3)]
        loaded, zeroed, consts = sem("loaded"), sem("zeroed"), sem("consts")
        phi_made, exped = sem("phi_made"), sem("exped")
        turned, taken, small = sem("turned"), sem("taken"), sem("small")
        stored, blank, parted = sem("filters_stored"), sem("blank"), sem("parted")

        turns = []

        def turn(dst, parts):
            turns.append((dst, parts))

        for t in range(K):
            turn(("tap", t), [(k * P, P, P, conv_w[:, k, t:t + 1].to_broadcast([P, P]), wt["ident"][:], True)
                              for k in range(2)])
        turn(("fold",), [(k, 1, P, w_in[:, k * P:(k + 1) * P], shift[:], False) for k in range(4)])
        turn(("bout",), [(0, P, P, bo_col[:, 0:1].to_broadcast([P, P]), wt["ident"][:], True)])
        turn(("w1",), [(k * P, P, P, w1_rows[:, k, :], wt["ident"][:], True) for k in range(2)])
        turn(("w2",), [(k * P, P, P, w2_rows[:, k * P:(k + 1) * P], wt["ident"][:], True) for k in range(2)])
        for g in range(L // 4):
            turn(("theta", g), [(i * P, P, P, th_rows[:, 4 * g + i, :], wt["ident"][:], True) for i in range(4)])

        block = ctx.enter_context(nc.Block())

        @block.sync
        def _(sp):
            sp.wait_ge(blank, 1)
            for dst, src in loads:
                with nc.allow_non_contiguous_dma(reason="weights, once"):
                    sp.dma_start(dst, src).then_inc(loaded, 16)
            sp.wait_ge(phi_made, 1)
            with nc.allow_non_contiguous_dma(reason="filters, once"):
                sp.dma_start(phi_dram.rearrange("k x n -> x k n"),
                             phi_t[:].rearrange("p k t l -> p k (t l)")).then_inc(stored, 16)
            sp.wait_ge(zeroed, 4)
            sp.dma_start(y_dram[P].rearrange("x b d -> x (b d)"), zeros[:]).then_inc(stored, 16)
            sp.wait_ge(stored, 32)

        @block.gpsimd
        def _(pool):
            pool.memset(dt_rows[:], 0.0).then_inc(blank, 1)
            pool.memset(wt["ident"][:], 0.0).then_inc(zeroed, 1)
            pool.memset(wt["identb"][:], 0.0).then_inc(zeroed, 1)
            pool.memset(wt["select"][:], 0.0).then_inc(zeroed, 1)
            pool.memset(zeros[:], 0.0).then_inc(zeroed, 1)
            pool.memset(wt["mean_w"][:], 1.0 / C).then_inc(consts, 1)
            pool.wait_ge(zeroed, 3)
            for t in ("ident", "identb"):
                pool.affine_select(out=wt[t][:], in_=wt[t][:], compare_op=ALU.not_equal, fill=1.0, base=0,
                                   pattern=[[-1, P]], channel_multiplier=1).then_inc(consts, 1)
            for part in range(3):
                pool.affine_select(out=wt["select"][:], in_=wt["select"][:], compare_op=ALU.not_equal, fill=1.0,
                                   base=-(XP * part + RANK), pattern=[[-1, 2 * NS], [0, P]],
                                   channel_multiplier=1).then_inc(consts, 1)
                pool.wait_ge(consts, 4 + part)

        @block.scalar
        def _(act):
            act.wait_ge(loaded, 16 * len(loads))
            act.activation(wt["neg_a"][:], a_log[:], ACT.Exp).then_inc(exped, 1)

        @block.vector
        def _(dve):
            dve.wait_ge(loaded, 16 * len(loads))
            dve.wait_ge(consts, 6)
            dve.tensor_scalar(wt["z_w"][:], w_in[:, DI:2 * DI], gain[:, 0:1], None, ALU.mult)
            src = dt_rows[:]
            for part in range(3):
                dve.tensor_copy(wt["dt_parts"][:, part, :], src).then_inc(parted, 1)
                if part < 2:
                    dve.wait_ge(parted, 2 * part + 1)
                    dve.tensor_tensor(dt_rest[:, part, :], src, wt["dt_parts"][:, part, :],
                                      ALU.subtract).then_inc(parted, 1)
                    dve.wait_ge(parted, 2 * part + 2)
                    src = dt_rest[:, part, :]
            dve.tensor_scalar(wt["dc"][:], beta[:], float(H * W), None, ALU.mult)
            for k in range(2):
                dve.tensor_scalar(wt["diag_d"][:, k, :], wt["ident"][:], d_col[:, k:k + 1], None, ALU.mult)
            for t, (part, sign) in enumerate(((0, 1.0), (1, 1.0), (1, -1.0))):
                last = dve.tensor_scalar(phi_t[:, :, t, :], phi[:, part].rearrange("p l k -> p k l"), sign, None,
                                         ALU.mult)
            last.then_inc(phi_made, 1)
            n = 0
            dve.tensor_copy(tap_sum[:, :, 0], conv_w[:, :, 0]).then_inc(small, 1)
            for t in range(1, K):
                n += 1
                dve.wait_ge(small, n)
                dve.tensor_tensor(tap_sum[:, :, t], tap_sum[:, :, t - 1], conv_w[:, :, t], ALU.add).then_inc(small, 1)
            dve.wait_ge(exped, 1)
            dve.tensor_scalar(wt["neg_a"][:], wt["neg_a"][:], -1.0, None, ALU.mult)
            for i, (dst, _) in enumerate(turns):
                dve.wait_ge(turned, i + 1)
                bank = ps[i % 2]
                if dst[0] == "tap":
                    last = dve.scalar_tensor_tensor(wt["tap_w"][:, dst[1], :], bank[:, 0:DI], gain[:, 0:1],
                                                    w_in[:, 0:DI], ALU.mult, ALU.mult)
                elif dst[0] == "fold":
                    last = dve.tensor_tensor(b_fold[:], bank[:, 0:4], b_in[:], ALU.add)
                elif dst[0] == "bout":
                    last = dve.tensor_copy(wt["out_b"][:], bank[:, 0:P])
                elif dst[0] in ("w1", "w2"):
                    last = dve.tensor_copy(wt[dst[0]][:].rearrange("p k n -> p (k n)"), bank[:, 0:DI])
                else:
                    g = 4 * dst[1]
                    last = dve.tensor_copy(wt["theta"][:, g:g + 4, :].rearrange("p l h -> p (l h)"), bank[:, :])
                last.then_inc(taken, 1)
            n += 1
            dve.wait_ge(small, n)
            dve.wait_ge(taken, len(turns))
            dve.tensor_copy(wt["z_b"][:], b_fold[:, 2:4])
            dve.tensor_tensor(edge0[:], tap_sum[:, :, K - 1], b_fold[:, 0:2], ALU.mult).then_inc(small, 1)
            n += 1
            dve.wait_ge(small, n)
            dve.tensor_tensor(wt["xc_b"][:], edge0[:], conv_b[:], ALU.add)
            for t in range(K - 1):
                dve.scalar_tensor_tensor(wt["edge"][:, :, t], tap_sum[:, :, K - 2 - t], -1.0, b_fold[:, 0:2],
                                         ALU.mult, ALU.mult)

        @block.tensor
        def _(pe):
            pe.wait_ge(loaded, 16 * len(loads))
            pe.wait_ge(consts, 6)
            for i, (_, parts) in enumerate(turns):
                if i >= 2:
                    pe.wait_ge(taken, i - 1)
                for col, n, rows, lhs, rhs, tr in parts:
                    last = pe.matmul(ps[i % 2][0:rows, col:col + n], lhs, rhs, start=True, stop=True, is_transpose=tr)
                last.then_inc(turned, 1)


def layer0(nc, a, wt, x1_dram, y_dram, blocks):
    with ExitStack() as ctx:
        def sb(name, shape, dt=F32):
            return ctx.enter_context(nc.sbuf_tensor(name, shape, dt))

        def psum(name, shape):
            return ctx.enter_context(nc.psum_tensor(name, shape, F32))

        def sem(name):
            return ctx.enter_context(nc.semaphore(name))

        x_in = sb("x_in", [P, BT])
        x_res = sb("x_res", [P, BT])
        cent = sb("cent", [P, BT])
        sq = sb("sq", [P, BT])
        tn = x_in
        soft = sb("soft", [P, 2, HT])
        xc = [sb(f"xc{i}", [P, 2, BT]) for i in range(2)]
        zs = [sb(f"zs{i}", [P, 2, BT]) for i in range(2)]
        delta = sb("delta", [P, 2, BT])
        du = sb("du", [P, 2, BT])
        parts = sb("parts", [P, BT // P, 3, XP], BF16)
        rest = cent[:, 0:2 * BT // P * XP].rearrange("p (i g n) -> p i g n", i=2, g=BT // P)
        rows = [sb(f"rows{i}", [3 * XP, BT], BF16) for i in range(2)]
        NB, NA, ND, NT, NP = RINGS
        b_all = [sb(f"b_all{i}", [P, HT]) for i in range(NB)]
        decay = [sb(f"decay{i}", [P, 2, HWN, WT]) for i in range(NA)]
        drive = [sb(f"drive{i}", [P, 2, HT]) for i in range(ND)]
        state = [sb(f"state{i}", [P, 2, HT]) for i in range(NT)]
        prod = [sb(f"prod{i}", [P, 2, HT]) for i in range(NP)]
        y_tok = sb("y_tok", [P, 4, DI])
        gated = sb("gated", [P, 2, BT])
        x1 = sb("x1", [P, WS, C])
        stats = sb("stats", [P, WS, 6])
        mv = sb("mv", [P, WS, 2])
        rstd1 = sb("rstd1", [P, WS])
        shift1 = sb("shift1", [P, WS])
        z1 = sb("z1", [P, WS, C])
        yo = z1

        c_bank = [psum(f"c_bank{i}", [P, HT]) for i in range(2)]
        b_bank = [psum(f"b_bank{i}", [P, HT]) for i in range(2)]
        y_acc = psum("y_acc", [P, 4, DI])
        job_bank = [psum(f"job_bank{i}", [P, 512]) for i in range(2)]

        names = """x_ready xres_ready x1_stored yo_stored sq_done rstd_done tn_done
            edge_done silu_done split_done softplus_done delta_done du_done c_full b_full b_copied
            decay_done drive_done scan_done prod_done added y_copied stats_done mv_done rstd1_done
            shift1_done z1_by_act z1_by_dve yo_done zeroed""".split()
        s = {n: sem(n) for n in names}

        job_full = [sem(f"job_full{i}") for i in range(2)]
        job_taken = [sem(f"job_taken{i}") for i in range(2)]

        def full(eng, S, name):
            need(eng, job_full[S.bank[name]], S.before[name] + 1)
            return job_bank[S.bank[name]]

        def taken(eng, S, *names):
            for bank in range(2):
                last = [n for _, n, _ in JOBS if n in names and S.bank[n] == bank][-1:]
                for name in last:
                    need(eng, job_taken[bank], S.before[name] + 1)

        def take(S, name):
            return job_taken[S.bank[name]]

        block = ctx.enter_context(nc.Block())

        xv = a["x"].rearrange("b c (k r) w -> b k c (r w)", r=WS)
        yv = y_dram[0:P].rearrange("f (k r) b d -> k b f r d", r=WS)

        @block.sync
        def _(sp):
            def place(M):
                if isinstance(M, int):
                    return M // KB, M % KB
                return sp.snap(M // KB), sp.snap(M % KB)

            def load_x(dst, at, done):
                sp.dma_start(dst[:], xv[bass.ds(at[0], 1), bass.ds(at[1], 1)]
                             .rearrange("o q c n -> (o q c) n")).then_inc(done, 16)

            def body(S, p):
                m = S.m
                before, now, after = (place(m + i) if on else None for i, on in
                                      ((-1, S.back), (0, S.scan), (2, S.ahead)))
                if S.ahead:
                    if S.front:
                        full(sp, S, "z11")
                    load_x(x_in, after, s["x_ready"])
                if S.back:
                    need(sp, s["stats_done"], m)
                    sp.dma_start(x1_dram[bass.ds((m - 1) * WS, WS)].rearrange("r w c -> w r c"),
                                 x1[:]).then_inc(s["x1_stored"], 16)
                if S.scan:
                    need(sp, s["x1_stored"], (m + 1) * 16)
                    load_x(x_res, now, s["xres_ready"])
                if S.back:
                    need(sp, s["yo_done"], m)
                    sp.dma_start(yv[bass.ds(before[1], 1), bass.ds(before[0], 1)].rearrange("o q f r d -> (o q f) r d"),
                                 yo[:]).then_inc(s["yo_stored"], 16)

            sp.sem_inc(s["x1_stored"], 16)
            sp.sem_inc(s["yo_stored"], 16)
            slots(sp, body, blocks)
            sp.wait_ge(s["x1_stored"], 16 * blocks + 16)
            sp.wait_ge(s["yo_stored"], 16 * blocks + 16)

        @block.tensor
        def _(pe):
            def broadcast(bank, step, row, done):
                M, p, n = step
                q = n // NS
                pe.matmul(bank[n % 2][:], wt["select"][:, row + n % NS, :], rows[p][:, q * HT:(q + 1) * HT],
                          start=True, stop=True).then_inc(done, 1)

            def broadcast_b(step):
                M, p, n = step
                need(pe, s["b_copied"], M * NSTEP + n - 1)
                broadcast(b_bank, step, 0, s["b_full"])

            def broadcast_c(step):
                M, p, n = step
                need(pe, s["prod_done"], M * NSTEP + n - 1)
                broadcast(c_bank, step, NS, s["c_full"])

            def add_state(step):
                M, p, n = step
                if n % NS == 0:
                    need(pe, s["y_copied"], M * 2 + n // NS)
                need(pe, s["prod_done"], M * NSTEP + n + 1)
                for hf in range(2):
                    for g in range(4):
                        mm = pe.matmul(y_acc[:, g, hf * P:(hf + 1) * P], prod[n % NP][:, hf, g * P:(g + 1) * P],
                                       wt["ident"][:], start=(n % NS == 0 and hf == 0 and g % 2 == 0), stop=False,
                                       is_transpose=True, skip_group_check=True)
                mm.then_inc(s["added"], 1)

            def add_skip(p, q, g):
                for k in range(2):
                    pe.matmul(y_acc[:, g, k * P:(k + 1) * P], xc[p][:, k, q * HT + g * P:q * HT + (g + 1) * P],
                              wt["diag_d"][:, k, :], start=False, stop=False, skip_group_check=True)

            def job(S, p, name, part=0):
                m, kind, f = S.m, name.rstrip("01"), 1 - p
                misc = job_bank[S.bank[name]]
                if part == 0:
                    need(pe, job_taken[S.bank[name]], S.before[name])
                if kind == "mean":
                    q = int(name[-1])
                    need(pe, s["x_ready"], (m + 3) * 16)
                    mm = pe.matmul(misc[:].rearrange("p (r c) -> p r c", r=WS), wt["mean_w"][:],
                                   x_in[:].rearrange("p (r q c) -> p r q c", r=WS, q=2)[:, :, q, :],
                                   start=True, stop=True)
                elif kind == "var":
                    q = int(name[-1])
                    need(pe, s["sq_done"], (m + 2) * 2 + q + 1)
                    mm = pe.matmul(misc[:], wt["mean_w"][:], sq[:, q * HT:(q + 1) * HT], start=True, stop=True)
                elif kind == "conv":
                    hf, q = int(name[-2]), int(name[-1])
                    if part == 0:
                        need(pe, s["tn_done"], (m + 1) * 2 + q + 1)
                    o = misc[:].rearrange("p (w t) -> p w t", t=WT)
                    v = tn[:, q * HT:(q + 1) * HT].rearrange("p (w t) -> p w t", t=WT)
                    for k in range(2 * part, 2 * part + 2):
                        mm = pe.matmul(o[:, :, k:WT], wt["tap_w"][:, K - 1 - k, hf * P:(hf + 1) * P],
                                       v[:, :, 0:WT - k], start=(k == 0), stop=(k == K - 1), skip_group_check=True)
                elif kind == "z":
                    hf, q = int(name[-2]), int(name[-1])
                    mm = pe.matmul(misc[:], wt["z_w"][:, hf * P:(hf + 1) * P], tn[:, q * HT:(q + 1) * HT],
                                   start=True, stop=True)
                elif kind == "xproj":
                    need(pe, s["silu_done"], (m + 1) * 2 + 2)
                    for g in range(BT // P):
                        for k in range(2):
                            mm = pe.matmul(misc[:, g * XP:(g + 1) * XP], xc[f][:, k, g * P:(g + 1) * P],
                                           wt["xp_w"][:, k, :], start=(g == 0 and k == 0), stop=(k == 1),
                                           skip_group_check=True)
                elif kind == "dt":
                    hf, q = int(name[-2]), int(name[-1])
                    if q == 0:
                        taken(pe, S, "rows")
                    for part in range(3):
                        mm = pe.matmul(misc[:], wt["dt_parts"][:, part, hf * P:(hf + 1) * P],
                                       rows[1 - p if q == 0 else p][:, q * HT:(q + 1) * HT],
                                       start=(part == 0), stop=(part == 2))
                elif kind == "rows":
                    taken(pe, S, "xproj")
                    for g in range(BT // P):
                        mm = pe.matmul(misc[:].bitcast(BF16)[0:3 * XP, g * P:(g + 1) * P],
                                       parts[:, g].rearrange("p t n -> p (t n)"), wt["identb"][:],
                                       start=True, stop=True, is_transpose=True)
                elif kind == "turn":
                    q, hf = int(name[-2]), int(name[-1])
                    M = m if q == 0 else m - 1
                    need(pe, s["y_copied"], M * 2 + q + 1)
                    for g in range(4):
                        mm = pe.matmul(misc[:, g * P:(g + 1) * P], y_tok[:, g, hf * P:(hf + 1) * P], wt["ident"][:],
                                       start=True, stop=True, is_transpose=True)
                elif kind == "out":
                    q = int(name[-1])
                    taken(pe, S, "turn10", "turn11")
                    need(pe, s["xres_ready"], m * 16)
                    for r in range(4):
                        row = 4 * q + r
                        o = misc[:, r * P:(r + 1) * P]
                        for k in range(2):
                            pe.matmul(o, gated[:, k, row * W:(row + 1) * W], wt["out_w"][:, k, :],
                                      start=(r == 0 and k == 0), stop=False, skip_group_check=True)
                        mm = pe.matmul(o, x_res[:, row * W:(row + 1) * W], wt["ident"][:], start=False, stop=(r == 3),
                                       is_transpose=True, skip_group_check=True)
                elif kind == "fy":
                    q = int(name[-1])
                    need(pe, s["z1_by_dve" if q else "z1_by_act"], m)
                    mm = pe.matmul(misc[:], wt["fy"][:], z1[:, 4 * q:4 * q + 4, :].rearrange("p r c -> p (r c)"),
                                   start=True, stop=True)
                if kind != "conv" or part == 1:
                    mm.then_inc(job_full[S.bank[name]], 1)

            def body(S, p):
                def jobs(n):
                    for name in S.at(n):
                        job(S, p, name)
                    for name in S.at(n - 1):
                        if name.startswith("conv"):
                            job(S, p, name, 1)

                for n in range(NSTEP):
                    if n == NSTEP - B_AHEAD[1] and S.front:
                        taken(pe, S, "rows")
                    for step in S.due(n, p, B_AHEAD):
                        broadcast_b(step)
                    if S.step(n + 1, p):
                        broadcast_c(S.step(n + 1, p))
                    late = n % NS == 1
                    if late:
                        jobs(n)
                    if S.step(n - 1, p):
                        add_state(S.step(n - 1, p))
                    if not late:
                        jobs(n)
                    if n in SKIP_AT and S.scan:
                        add_skip(p, n // NS, SKIP_AT[n])

            slots(pe, body, blocks)

        @block.scalar
        def _(act):
            def copy_b(step):
                M, p, n = step
                need(act, s["drive_done"], M * NSTEP + n + 1 - since(n, NB))
                need(act, s["b_full"], M * NSTEP + n + 1)
                act.activation(b_all[n % NB][:], b_bank[n % 2][:], ACT.Copy).then_inc(s["b_copied"], 1)

            def decays(step):
                M, p, n = step
                q, st = n // NS, n % NS
                need(act, s["zeroed"], 1)
                need(act, s["delta_done"], M * 2 + q + 1)
                need(act, s["scan_done"], M * NSTEP + n + 1 - since(n, NA))
                for hf in range(2):
                    last = act.activation(
                        decay[n % NA][:, hf, :, 1:WT],
                        delta[:, hf, q * HT:(q + 1) * HT].rearrange("p (w t) -> p w t", t=WT)[:, :, 1:WT],
                        ACT.Exp, scale=wt["neg_a"][:, hf, st:st + 1])
                last.then_inc(s["decay_done"], 1)

            def ahead(S, n, m):
                if n in AT["square"]:
                    q = AT["square"].index(n)
                    taken(act, S, f"mean{q}")
                    act.activation(sq[:, q * HT:(q + 1) * HT], cent[:, q * HT:(q + 1) * HT],
                                   ACT.Square).then_inc(s["sq_done"], 1)
                if n in AT["deviation"]:
                    q = AT["deviation"].index(n)
                    misc = full(act, S, f"var{q}")
                    act.activation(sq[:, q * HT:(q + 1) * HT], misc[:], ACT.Ln,
                                   bias=EPS).then_inc(take(S, f"var{q}"), 1)
                    taken(act, S, f"var{q}")
                    act.activation(sq[:, q * HT:(q + 1) * HT], sq[:, q * HT:(q + 1) * HT], ACT.Exp,
                                   scale=-0.5).then_inc(s["rstd_done"], 1)

            def chain(S, n, m, f):
                if n == AT["silu"]:
                    need(act, s["edge_done"], m + 2)
                    act.activation(xc[f][:], xc[f][:], ACT.Silu).then_inc(s["silu_done"], 1)
                if n == AT["silu"] + 1:
                    taken(act, S, "z01", "z11")
                    act.activation(zs[f][:], zs[f][:], ACT.Silu).then_inc(s["silu_done"], 1)
                    act.preload_act_table_set(TABLES)
                if n == AT["take_rows"]:
                    act.activation(rows[f][:], full(act, S, "rows")[:].bitcast(BF16)[0:3 * XP, :],
                                   ACT.Copy).then_inc(take(S, "rows"), 1)
                moved = {"conv": (xc, wt["xc_b"]), "z": (zs, wt["z_b"])}
                for name in S.at(n - AT["take_z"]) + S.at(n - AT["take_conv"]):
                    kind = name.rstrip("01")
                    if kind not in moved or name not in S.at(n - AT["take_" + kind]):
                        continue
                    hf, q = int(name[-2]), int(name[-1])
                    dst, bias = moved[kind]
                    misc = full(act, S, name)
                    act.activation(dst[f][:, hf, q * HT:(q + 1) * HT], misc[:], ACT.Identity,
                                   bias=bias[:, hf:hf + 1]).then_inc(take(S, name), 1)

            def take_dt(S, hf, q):
                M = S.m + 1 if q == 0 else S.m
                misc = full(act, S, f"dt{hf}{q}")
                need(act, s["delta_done"], M * 2 - 1 + q)
                need(act, s["decay_done"], M * NSTEP - NS * (1 - q))
                need(act, s["du_done"], M * 2 - 1 + q)
                act.activation(soft[:, hf, :], misc[:], ACT.Abs, bias=wt["dt_b"][:, hf:hf + 1])
                act.activation(delta[:, hf, q * HT:(q + 1) * HT], misc[:], ACT.Relu,
                               bias=wt["dt_b"][:, hf:hf + 1]).then_inc(take(S, f"dt{hf}{q}"), 1)

            def softplus(S, M, q):
                taken(act, S, f"dt0{q}", f"dt1{q}")
                n = M * 4 + 2 * q
                act.activation(soft[:], soft[:], ACT.Exp, scale=-1.0).then_inc(s["softplus_done"], 1)
                need(act, s["softplus_done"], n + 1)
                act.activation(soft[:], soft[:], ACT.Ln, bias=1.0).then_inc(s["softplus_done"], 1)

            def copy_y(M, q):
                need(act, s["added"], M * NSTEP + NS * (q + 1))
                act.activation(y_tok[:].rearrange("p g d -> p (g d)"),
                               y_acc[:].rearrange("p g d -> p (g d)"), ACT.Copy).then_inc(s["y_copied"], 1)

            def body(S, p):
                m, f = S.m, 1 - p
                for n in range(NSTEP):
                    if n == AT["copy_y"][1] and S.back:
                        copy_y(m - 1, 1)
                    if n == AT["copy_y"][0] and S.scan:
                        copy_y(m, 0)
                    for step in S.due(n, p, COPY_AHEAD):
                        copy_b(step)
                    silu = AT["silu"]
                    if n == silu + 1 and S.front:
                        chain(S, n, m, f)
                    if n != silu:
                        for step in (S.due(silu, p, A_AHEAD) if n == silu + 1 else []) + S.due(n, p, A_AHEAD):
                            decays(step)
                    if n != silu + 1 and S.front:
                        chain(S, n, m, f)
                    if S.ahead:
                        ahead(S, n, m)
                    for hf in range(2):
                        if n == AT["take_dt1"][hf] and S.scan:
                            take_dt(S, hf, 1)
                        if n == AT["take_dt0"][hf] and S.front:
                            take_dt(S, hf, 0)
                    if n == AT["softplus1"] and S.scan:
                        softplus(S, m, 1)
                    if n == AT["softplus0"] and S.front:
                        softplus(S, m + 1, 0)
                    if n == AT["deviation1"] and S.back:
                        need(act, s["mv_done"], m)
                        act.activation(rstd1[:], mv[:, :, 1], ACT.Ln, bias=EPS).then_inc(s["rstd1_done"], 1)
                        need(act, s["rstd1_done"], (m - 1) * 2 + 1)
                        act.activation(rstd1[:], rstd1[:], ACT.Exp, scale=-0.5).then_inc(s["rstd1_done"], 1)
                    if n == AT["z1_by_act"] and S.back:
                        need(act, s["yo_stored"], m * 16)
                        need(act, s["shift1_done"], m)
                        for r in range(WS // 2):
                            last = act.activation(z1[:, r, :], x1[:, r, :], ACT.Identity,
                                                  scale=rstd1[:, r:r + 1], bias=shift1[:, r:r + 1])
                        last.then_inc(s["z1_by_act"], 1)
                    if n in AT["yo"] and S.back:
                        q = AT["yo"].index(n)
                        misc = full(act, S, f"fy{q}")
                        act.activation(yo[:, 4 * q:4 * q + 4, :].rearrange("p r c -> p (r c)"), misc[:],
                                       ACT.Copy).then_inc(take(S, f"fy{q}"), 1)
                        if q == 1:
                            taken(act, S, "fy0", "fy1")
                            act.sem_inc(s["yo_done"], 1)

            act.preload_act_table_set(TABLES)
            slots(act, body, blocks)

        @block.vector
        def _(dve):
            def scan(step):
                M, p, n = step
                need(dve, s["decay_done"], M * NSTEP + n + 1)
                need(dve, s["drive_done"], M * NSTEP + n + 1)
                need(dve, s["prod_done"], M * NSTEP + n + 1 - since(n, NT))
                dve.tensor_tensor_scan(state[n % NT][:].rearrange("p h t -> p (h t)"),
                                       decay[n % NA][:].rearrange("p h w t -> p (h w t)"),
                                       drive[n % ND][:].rearrange("p h t -> p (h t)"), 0.0, ALU.mult,
                                       ALU.add).then_inc(s["scan_done"], 1)

            def times_c(step):
                M, p, n = step
                need(dve, s["scan_done"], M * NSTEP + n + 1)
                need(dve, s["c_full"], M * NSTEP + n + 1)
                need(dve, s["added"], M * NSTEP + n + 1 - since(n, NP))
                dve.tensor_tensor(prod[n % NP][:], state[n % NT][:],
                                  c_bank[n % 2][:].unsqueeze(1).to_broadcast([P, 2, HT]),
                                  ALU.mult).then_inc(s["prod_done"], 1)

            def ahead(S, n, m):
                if n in AT["centre"]:
                    q = AT["centre"].index(n)
                    misc = full(dve, S, f"mean{q}")
                    if S.front:
                        taken(dve, S, "xproj")
                    dve.tensor_tensor(
                        cent[:, q * HT:(q + 1) * HT].rearrange("p (n r c) -> p r n c", n=HWN, r=WS),
                        x_in[:].rearrange("p (r q n c) -> p r q n c", r=WS, q=2, n=HWN)[:, :, q],
                        misc[:].rearrange("p (r n c) -> p r n c", r=WS, n=HWN),
                        ALU.subtract).then_inc(take(S, f"mean{q}"), 1)

            def chain(S, n, m):
                if n == AT["split"]:
                    misc = full(dve, S, "xproj")
                    v = misc[:, 0:BT // P * XP].rearrange("p (g i) -> p g i", i=XP)
                    steps = [
                        lambda: dve.tensor_copy(parts[:, :, 0, :], v),
                        lambda: dve.tensor_tensor(rest[:, 0], v, parts[:, :, 0, :], ALU.subtract),
                        lambda: dve.tensor_copy(parts[:, :, 1, :], rest[:, 0]),
                        lambda: dve.tensor_tensor(rest[:, 1], rest[:, 0], parts[:, :, 1, :], ALU.subtract),
                    ]
                    for i, step in enumerate(steps):
                        step().then_inc(s["split_done"], 1)
                        need(dve, s["split_done"], (m + 1) * 4 + i + 1)
                    dve.tensor_copy(parts[:, :, 2, :], rest[:, 1]).then_inc(take(S, "xproj"), 1)

            def add_soft(M, q):
                need(dve, s["softplus_done"], M * 4 + 2 * q + 2)
                d = delta[:, :, q * HT:(q + 1) * HT]
                dve.tensor_tensor(d, d, soft[:], ALU.add).then_inc(s["delta_done"], 1)

            def gate(S, q, hf, par):
                misc = full(dve, S, f"turn{q}{hf}")
                by_window = "p (n r c) -> p n r c"
                dve.tensor_tensor(
                    gated[:, hf, :].rearrange("p (r q n c) -> p q n r c", r=WS, q=2, n=HWN)[:, q],
                    misc[:].rearrange(by_window, n=HWN, r=WS),
                    zs[par][:, hf, q * HT:(q + 1) * HT].rearrange(by_window, n=HWN, r=WS),
                    ALU.mult).then_inc(take(S, f"turn{q}{hf}"), 1)

            def behind(S, n, m, f):
                if n in AT["gate1"]:
                    gate(S, 1, AT["gate1"].index(n), f)
                if n in AT["x1"]:
                    q = AT["x1"].index(n)
                    misc = full(dve, S, f"out{q}")
                    need(dve, s["x1_stored"], m * 16)
                    dve.tensor_tensor(x1[:, 4 * q:4 * q + 4, :], misc[:].rearrange("p (r c) -> p r c", r=4),
                                      wt["out_b"][:].unsqueeze(1).to_broadcast([P, 4, C]),
                                      ALU.add).then_inc(take(S, f"out{q}"), 1)
                if n == AT["stats"]:
                    taken(dve, S, "out0", "out1")
                    for r in range(WS):
                        last = dve.bn_stats(stats[:, r, :], x1[:, r, :])
                    last.then_inc(s["stats_done"], 1)
                if n == AT["mean_var"]:
                    for r in range(WS):
                        last = dve.bn_aggr(mv[:, r, :], stats[:, r, :])
                    last.then_inc(s["mv_done"], 1)
                if n == AT["z1_by_dve"]:
                    need(dve, s["rstd1_done"], m * 2)
                    need(dve, s["z1_by_act"], m - 1)
                    dve.scalar_tensor_tensor(shift1[:], mv[:, :, 0], -1.0, rstd1[:], ALU.mult,
                                             ALU.mult).then_inc(s["shift1_done"], 1)
                    need(dve, s["yo_stored"], m * 16)
                    for r in range(WS // 2, WS):
                        last = dve.tensor_scalar(z1[:, r, :], x1[:, r, :], mv[:, r, 0:1], rstd1[:, r:r + 1],
                                                 ALU.subtract, ALU.mult)
                    last.then_inc(s["z1_by_dve"], 1)

            def body(S, p):
                for n in range(NSTEP):
                    if S.back and n == AT["mean_var"]:
                        need(dve, s["stats_done"], S.m)
                    if S.step(n, p):
                        scan(S.step(n, p))
                    if S.step(n - 1, p):
                        times_c(S.step(n - 1, p))
                    if S.front:
                        chain(S, n, S.m)
                    if S.ahead:
                        ahead(S, n, S.m)
                    if n == AT["add_soft1"] and S.scan:
                        add_soft(S.m, 1)
                    if n == AT["add_soft0"] and S.front:
                        add_soft(S.m + 1, 0)
                    if S.scan and n in AT["gate0"]:
                        gate(S, 0, AT["gate0"].index(n), p)
                    if S.back:
                        behind(S, n, S.m, 1 - p)

            for i in range(NA):
                last = dve.memset(decay[i][:].rearrange("p i w t -> p (i w t)"), 0.0)
            last.then_inc(s["zeroed"], 1)
            slots(dve, body, blocks)

        @block.gpsimd
        def _(pool):
            def drives(step):
                M, p, n = step
                q = n // NS
                need(pool, s["du_done"], M * 2 + 1 + q)
                need(pool, s["b_copied"], M * NSTEP + n + 1)
                need(pool, s["scan_done"], M * NSTEP + n + 1 - since(n, ND))
                pool.tensor_tensor(drive[n % ND][:], du[:, :, q * HT:(q + 1) * HT],
                                   b_all[n % NB][:].unsqueeze(1).to_broadcast([P, 2, HT]),
                                   ALU.mult).then_inc(s["drive_done"], 1)

            def make_du(M, q, p):
                need(pool, s["delta_done"], M * 2 + q + 1)
                need(pool, s["drive_done"], (M - 1) * NSTEP + NS * (q + 1))
                pool.tensor_tensor(du[:, :, q * HT:(q + 1) * HT], delta[:, :, q * HT:(q + 1) * HT],
                                   xc[p][:, :, q * HT:(q + 1) * HT], ALU.mult).then_inc(s["du_done"], 1)

            def body(S, p):
                m, f = S.m, 1 - p
                for n in range(NSTEP):
                    if n == NSTEP - D_AHEAD[1] and S.front:
                        make_du(m + 1, 0, f)
                    for step in S.due(n, p, D_AHEAD):
                        drives(step)
                    if n in AT["tn"] and S.ahead:
                        q = AT["tn"].index(n)
                        need(pool, s["rstd_done"], (m + 2) * 2 + q + 1)
                        pool.tensor_tensor(tn[:, q * HT:(q + 1) * HT], cent[:, q * HT:(q + 1) * HT],
                                           sq[:, q * HT:(q + 1) * HT], ALU.mult).then_inc(s["tn_done"], 1)
                    if n == AT["du1"] and S.scan:
                        make_du(m, 1, p)
                    if n == AT["edge"] and S.front:
                        taken(pool, S, "conv01", "conv11")
                        v = xc[f][:].rearrange("p k (w t) -> p k w t", t=WT)[:, :, :, 0:K - 1]
                        pool.tensor_tensor(v, v, wt["edge"][:].unsqueeze(2).to_broadcast([P, 2, NW, K - 1]),
                                           ALU.add).then_inc(s["edge_done"], 1)

            slots(pool, body, blocks)


def spectral(nc, wt, y_dram, phi_dram, t_dram):
    with ExitStack() as ctx:
        def sb(name, shape, dt=F32):
            return ctx.enter_context(nc.sbuf_tensor(name, shape, dt))

        def psum(name, shape):
            return ctx.enter_context(nc.psum_tensor(name, shape, F32))

        def sem(name):
            return ctx.enter_context(nc.semaphore(name))

        N = B * P
        ND, NPL = len(BY_DVE), len(BY_POOL)
        OPS = 4
        STEPS = 2 * NPL - 1
        th_high = sb("th_high", [P, L, C], F32R)
        th_low = sb("th_low", [P, L, C], F32R)
        ys = [sb(f"ys{i}", [P, 2, B, C]) for i in range(2)]
        filt = [sb(f"filt{i}", [P, 3, L]) for i in range(2)]
        x_full = sb("x_full", [P, 2, B, P])
        x_high = [sb(f"x_high{i}", [P, 2, B, P], F32R) for i in range(2)]
        x_low = [sb(f"x_low{i}", [P, 2, B, P], F32R) for i in range(2)]
        scaled = [sb(f"scaled{i}", [P, 2, 2, N]) for i in range(2)]
        sum_d = [sb(f"sum_d{i}", [P, 2, B, C]) for i in range(2)]
        sum_p = [sb(f"sum_p{i}", [P, 2, N]) for i in range(2)]
        mixed = sb("mixed", [P, 2, N])
        tt = [sb(f"tt{i}", [P, 2, N]) for i in range(2)]

        bank_d = [psum(f"bank_d{i}", [P, B, 2, C]) for i in range(2)]
        bank_p = psum("bank_p", [P, B, 2, C])
        x_bank = psum("x_bank", [P, 2, 2, P])
        way = psum("way", [P, N])

        names = """th_high_done th_low_done cols_done x_done dc_done x_high_done x_low_done unit_d_full
            unit_p_full summed_d scaled_done summed_p mixed_done inv_done tt_done""".split()
        s = {n: sem(n) for n in names}
        ys_ready, filt_ready, tt_stored = ([sem(f"{n}{i}") for i in range(2)] for n in
                                           ("ys_ready", "filt_ready", "tt_stored"))

        def rounds(eng, body):
            body(-1, -1, 1, True, False, False)
            body(0, 0, 0, True, True, False)
            body(1, 0, 1, True, True, True)
            with eng.Fori(1, (KY - 1) // 2) as j:
                for i in range(2):
                    body(j * 2 + i, j, i, True, True, True)
            body(KY - 1, (KY - 1) // 2, 0, False, True, True)
            body(KY, KY // 2, 1, False, False, True)

        def terms(part):
            return ((0, 0), (1, 2)) if part == 0 else ((0, 1), (1, 0))

        block = ctx.enter_context(nc.Block())

        @block.sync
        def _(sp):
            def load_ys(k, half, p, im_row=None):
                need(sp, s["cols_done"], (k - 1) * 2)
                for i, row in enumerate((k, k + KY - 1 if im_row is None else im_row)):
                    sp.dma_start(ys[p][:, i].rearrange("x b d -> x (b d)"),
                                 y_dram[bass.ds(row, 1)].rearrange("o x b d -> (o x) (b d)")).then_inc(ys_ready[p], 16)

            def load_filt(k, p):
                need(sp, s["mixed_done"], k - 1)
                sp.dma_start(filt[p][:].rearrange("p t l -> p (t l)"),
                             phi_dram[bass.ds(k, 1)].rearrange("o x n -> (o x) n")).then_inc(filt_ready[p], 16)

            def body(k, half, p, columns, products, back, more=True):
                if columns:
                    if more:
                        load_ys(k + 2, half + 1, p)
                    load_filt(k + 1, 1 - p)
                if back:
                    need(sp, s["tt_done"], k * 2)
                    for i, row in enumerate((k - 1, KY - 1 + (k - 1) if not (isinstance(k, int) and k == 1) else P)):
                        sp.dma_start(t_dram[bass.ds(row, 1)].rearrange("o x b d -> (o x) (b d)"),
                                     tt[1 - p][:, i]).then_inc(tt_stored[1 - p], 16)

            for i in range(2):
                sp.sem_inc(tt_stored[i], 32)
            load_ys(0, 0, 0, im_row=P)
            body(-1, -1, 1, True, False, False)
            body(0, 0, 0, True, True, False)
            body(1, 0, 1, True, True, True)
            with sp.Fori(1, (KY - 3) // 2) as j:
                for i in range(2):
                    body(j * 2 + i, j, i, True, True, True)
            body(KY - 3, (KY - 3) // 2, 0, True, True, True)
            body(KY - 2, (KY - 3) // 2, 1, True, True, True, more=False)
            body(KY - 1, 0, 0, False, True, True)
            body(KY, 0, 1, False, False, True)
            sp.wait_ge(tt_stored[0], 32 * ((KY + 1) // 2) + 32)
            sp.wait_ge(tt_stored[1], 32 * (KY // 2) + 32)

        @block.tensor
        def _(pe):
            def columns(k, half, p, pair):
                pe.wait_ge(ys_ready[p], (half + 1) * 32)
                need(pe, s["x_done"], k * 2 + pair)
                for b in range(2):
                    for i in range(2):
                        mm = pe.matmul(x_bank[:, b].rearrange("p c x -> p (c x)"), ys[p][:, i, 2 * pair + b, :],
                                       wt["fx"][:, 2 * i:2 * i + 2, :].rearrange("p c x -> p (c x)"),
                                       start=(b == 0 and i == 0), stop=(i == 1), skip_group_check=True)
                mm.then_inc(s["cols_done"], 1)

            def unit(k, p, u):
                pair, part = u // 2, u % 2
                if u == 0:
                    pe.wait_ge(s["th_low_done"], 1)
                    need(pe, s["x_low_done"], k + 1)
                if u in BY_POOL:
                    n = BY_POOL.index(u)
                    need(pe, s["scaled_done"], (k * NPL + n) * OPS)
                    dst, done = bank_p, s["unit_p_full"]
                else:
                    n = BY_DVE.index(u)
                    need(pe, s["summed_d"], (k * ND + n - 1) * OPS)
                    dst, done = bank_d[n % 2], s["unit_d_full"]
                for b in range(B):
                    o = dst[:, b].rearrange("p l h -> p (l h)")
                    for i, (x, th) in enumerate(((x_high, th_high), (x_high, th_low), (x_low, th_high))):
                        mm = pe.matmul(o, x[p][:, part, b, :],
                                       th[:, 2 * pair:2 * pair + 2, :].rearrange("p l h -> p (l h)"),
                                       start=(b % 2 == 0 and i == 0), stop=(i == 2), skip_group_check=True)
                mm.then_inc(done, 1)

            def inverse(k, part):
                need(pe, s["mixed_done"], k + 1)
                need(pe, s["tt_done"], k * 2 + part)
                pe.matmul(way[:], wt["ix"][:, part, :], mixed[:, 0, :], start=True, stop=False)
                pe.matmul(way[:], wt["ix"][:, 2 if part == 0 else 0, :], mixed[:, 1, :],
                          start=False, stop=True).then_inc(s["inv_done"], 1)

            def body(k, half, p, col, products, back):
                for u in range(UNITS):
                    if col and u in COLUMNS:
                        columns(k + 1, half + p, 1 - p, COLUMNS[u])
                    if back and u in BACK:
                        inverse(k - 1, BACK[u])
                    if products:
                        unit(k, p, u)

            rounds(pe, body)

        @block.scalar
        def _(act):
            def take_x(k, p, pair):
                need(act, s["cols_done"], k * 2 + pair + 1)
                need(act, s["x_low_done"], k)
                b = slice(2 * pair, 2 * pair + 2)
                act.activation(x_full[:, :, b, :], x_bank[:].rearrange("p b c x -> p c b x"), ACT.Copy,
                               scale=wt["gamma"][:, 0:1]).then_inc(s["x_done"], 1)
                need(act, s["unit_d_full"], (k - 1) * ND)
                if isinstance(k, int) and k == 0:
                    act.wait_ge(s["dc_done"], pair + 1)
                else:
                    need(act, s["x_done"], k * 2 + pair + 1)
                act.activation(x_high[p][:, :, b, :], x_full[:, :, b, :], ACT.Copy).then_inc(s["x_high_done"], 1)

            def scale(k, p, n):
                u = BY_POOL[n]
                need(act, s["unit_p_full"], k * NPL + n + 1)
                need(act, s["summed_p"], k * STEPS + (2 * n - 3 if n >= 2 else 2 * n - 2))
                for i in range(2):
                    for out, kind in terms(u % 2):
                        act.activation(scaled[n % 2][:, i, out, :].rearrange("p (b h) -> p b h", b=B),
                                       bank_p[:, :, i, :], ACT.Copy,
                                       scale=filt[p][:, kind, 2 * (u // 2) + i:2 * (u // 2) + i + 1]
                                       ).then_inc(s["scaled_done"], 1)

            def take_way(k, half, p, part):
                need(act, s["inv_done"], k * 2 + part + 1)
                if part == 0:
                    need(act, tt_stored[p], half * 32)
                act.activation(tt[p][:, part, :], way[:], ACT.Copy).then_inc(s["tt_done"], 1)

            def body(k, half, p, columns, products, back):
                if products:
                    act.wait_ge(filt_ready[p], (half + 1) * 16)
                for u in range(UNITS):
                    if columns and u in COLUMNS:
                        take_x(k + 1, 1 - p, COLUMNS[u])
                    if back and u in BACK:
                        take_way(k - 1, half + p, 1 - p, BACK[u])
                    if products and u in BY_POOL:
                        scale(k, p, BY_POOL.index(u))

            act.activation(th_high[:], wt["theta"][:], ACT.Copy).then_inc(s["th_high_done"], 1)
            rounds(act, body)

        @block.vector
        def _(dve):
            def sum_unit(k, p, n):
                u = BY_DVE[n]
                need(dve, s["unit_d_full"], k * ND + n + 1)
                for i in range(2):
                    for out, kind in terms(u % 2):
                        step = (k * ND + n) * OPS + 2 * i + out
                        factor = filt[p][:, kind, 2 * (u // 2) + i:2 * (u // 2) + i + 1]
                        acc, src = sum_d[p][:, out], bank_d[n % 2][:, :, i, :]
                        if n == 0 and i == 0:
                            need(dve, s["mixed_done"], k - 1)
                            dve.tensor_scalar(acc, src, factor, None, ALU.mult).then_inc(s["summed_d"], 1)
                        else:
                            need(dve, s["summed_d"], step - 1)
                            dve.scalar_tensor_tensor(acc, src, factor, acc, ALU.mult,
                                                     ALU.add).then_inc(s["summed_d"], 1)

            def split_x(k, p):
                if isinstance(k, int) and k == 0:
                    for pair in range(2):
                        dve.wait_ge(s["x_done"], pair + 1)
                        dc = x_full[:, 0, 2 * pair:2 * pair + 2, 0]
                        dve.tensor_scalar(dc, dc, wt["dc"][:, 0:1], None, ALU.add).then_inc(s["dc_done"], 1)
                need(dve, s["x_high_done"], k * 2 + 2)
                need(dve, s["unit_d_full"], (k - 1) * ND)
                dve.tensor_tensor(x_low[p][:], x_full[:], x_high[p][:].bitcast(F32),
                                  ALU.subtract).then_inc(s["x_low_done"], 1)

            def mix(k, p):
                need(dve, s["summed_p"], (k + 1) * STEPS)
                need(dve, s["summed_d"], (k + 1) * ND * OPS)
                need(dve, s["inv_done"], k * 2)
                dve.tensor_tensor(mixed[:], sum_d[p][:].rearrange("p c b h -> p c (b h)"), sum_p[p][:],
                                  ALU.add).then_inc(s["mixed_done"], 1)

            def body(k, half, p, columns, products, back):
                if products:
                    dve.wait_ge(filt_ready[p], (half + 1) * 16)
                for n in range(ND):
                    if products:
                        sum_unit(k, p, n)
                    if back and n == MIX_AFTER:
                        mix(k - 1, 1 - p)
                    if columns and n == SPLIT_AFTER:
                        split_x(k + 1, 1 - p)

            dve.wait_ge(s["th_high_done"], 1)
            dve.tensor_tensor(th_low[:], wt["theta"][:], th_high[:].bitcast(F32),
                              ALU.subtract).then_inc(s["th_low_done"], 1)
            rounds(dve, body)

        @block.gpsimd
        def _(pool):
            def sum_unit(k, p, n):
                acc = sum_p[p][:]
                if n == 0:
                    need(pool, s["scaled_done"], (k * NPL + 1) * OPS)
                    need(pool, s["mixed_done"], k - 1)
                    pool.tensor_tensor(acc, scaled[0][:, 0], scaled[0][:, 1], ALU.add).then_inc(s["summed_p"], 1)
                    return
                for i in range(2):
                    need(pool, s["scaled_done"], (k * NPL + n) * OPS + 2 * i + 2)
                    need(pool, s["summed_p"], k * STEPS + 2 * n - 1 + i)
                    pool.tensor_tensor(acc, acc, scaled[n % 2][:, i], ALU.add).then_inc(s["summed_p"], 1)

            def body(k, half, p, columns, products, back):
                if products:
                    for n in range(NPL):
                        sum_unit(k, p, n)

            rounds(pool, body)


def mlp(nc, wt, t_dram, x1_dram, out):
    with ExitStack() as ctx:
        def sb(name, shape, dt=F32):
            return ctx.enter_context(nc.sbuf_tensor(name, shape, dt))

        def psum(name, shape):
            return ctx.enter_context(nc.psum_tensor(name, shape, F32))

        def sem(name):
            return ctx.enter_context(nc.semaphore(name))

        R = 4
        T = R * W
        NGR = H // R
        tk = [sb(f"tk{i}", [P, R, B, C]) for i in range(2)]
        x1t = [sb(f"x1t{i}", [P, B, R, C]) for i in range(2)]
        w1_high, w1_low, w2_high, w2_low = (sb(f"{n}", [P, 2, P], F32R) for n in
                                            ("w1_high", "w1_low", "w2_high", "w2_low"))
        mix_high, mix_low = ([sb(f"{n}{i}", [P, T], F32R) for i in range(2)] for n in
                             ("mix_high", "mix_low"))
        hid = [sb(f"hid{i}", [P, 2, T]) for i in range(2)]
        hid_high, hid_low = ([sb(f"{n}{i}", [P, 2, T], F32R) for i in range(2)] for n in
                             ("hid_high", "hid_low"))
        res = [sb(f"res{i}", [P, T]) for i in range(2)]
        mix_bank = [psum(f"mix_bank{i}", [P, T]) for i in range(2)]
        hid_bank = [psum(f"hid_bank{i}", [P, 2, T]) for i in range(2)]
        res_bank = [psum(f"res_bank{i}", [P, T]) for i in range(2)]

        names = """w_high_done w_low_done rows_done mix_high_done mix_low_done up_done hid_done hid_high_done
            hid_low_done down_done res_done""".split()
        s = {n: sem(n) for n in names}
        tk_ready, x1_ready, res_stored = ([sem(f"{n}{i}") for i in range(2)] for n in
                                          ("tk_ready", "x1_ready", "res_stored"))

        def steps(eng, body):
            body(-2, -1, 6, True, False, False)
            body(-1, -1, 7, True, True, False)
            for i in range(2 * B):
                body(i, 0, i, True, True, True)
            with eng.Fori(1, NGR // 2 - 1) as j:
                for i in range(2 * B):
                    body(j * (2 * B) + i, j, i, True, True, True)
            last = NGR // 2 - 1
            for i in range(2 * B):
                body(last * 2 * B + i, last, i, i < 2 * B - 2, i < 2 * B - 1, True)

        block = ctx.enter_context(nc.Block())
        x1v = x1_dram.rearrange("(b x) y c -> b y x c", b=B)
        ov = out.rearrange("b d x y -> b d (x y)")

        @block.sync
        def _(sp):
            def load(g, p):
                need(sp, s["rows_done"], (g - 1) * B)
                sp.dma_start(tk[p][:].rearrange("p x b h -> p (x b h)"),
                             t_dram[0:P, bass.ds(g * R, R)].rearrange("f x b h -> f (x b h)")).then_inc(tk_ready[p], 16)
                need(sp, s["down_done"], (g - 1) * B)
                for b in range(B):
                    sp.dma_start(x1t[p][:, b], x1v[b, :, bass.ds(g * R, R), :]).then_inc(x1_ready[p], 16)

            def body(g, p, more):
                if more:
                    load(g + 1, 1 - p)
                for b in range(B):
                    need(sp, s["res_done"], g * B + b + 1)
                    sp.dma_start(ov[b, :, bass.ds(g * T, T)], res[b % 2][:]).then_inc(res_stored[b % 2], 16)

            load(0, 0)
            body(0, 0, True)
            body(1, 1, True)
            with sp.Fori(1, NGR // 2 - 1) as j:
                for i in range(2):
                    body(j * 2 + i, i, True)
            body(NGR - 2, 0, True)
            body(NGR - 1, 1, False)
            for i in range(2):
                sp.wait_ge(res_stored[i], 16 * NGR * B // 2)

        @block.tensor
        def _(pe):
            def rows(u, j, i):
                p, b = i // B, i % B
                pe.wait_ge(tk_ready[p], (j + 1) * 16)
                need(pe, s["mix_low_done"], u - 1)
                for r in range(R):
                    mm = pe.matmul(mix_bank[i % 2][:, r * W:(r + 1) * W], tk[p][:, r, b, :], wt["iy"][:],
                                   start=True, stop=True)
                mm.then_inc(s["rows_done"], 1)

            def up(u, i):
                if isinstance(u, int) and u == 0:
                    pe.wait_ge(s["w_low_done"], 2)
                need(pe, s["mix_low_done"], u + 1)
                need(pe, s["hid_done"], (u - 1) * 2)
                for k in range(2):
                    for n, (w, v) in enumerate(((w1_high, mix_high), (w1_low, mix_high), (w1_high, mix_low))):
                        mm = pe.matmul(hid_bank[i % 2][:, k, :], w[:, k, :], v[i % 2][:], start=(n == 0),
                                       stop=(n == 2))
                mm.then_inc(s["up_done"], 1)

            def down(u, j, i):
                p, b = i // B, i % B
                need(pe, s["res_done"], u - 1)
                pe.wait_ge(x1_ready[p], (j + 1) * 16 * B)
                for k in range(2):
                    need(pe, s["hid_low_done"], u * 2 + k + 1)
                    for n, (w, v) in enumerate(((w2_high, hid_high), (w2_low, hid_high), (w2_high, hid_low))):
                        pe.matmul(res_bank[i % 2][:], w[:, k, :], v[i % 2][:, k, :], start=(k == 0 and n == 0),
                                  stop=False, skip_group_check=True)
                for r in range(R):
                    mm = pe.matmul(res_bank[i % 2][:, r * W:(r + 1) * W], x1t[p][:, b, r, :], wt["ident"][:],
                                   start=False, stop=(r == R - 1), is_transpose=True, skip_group_check=True)
                mm.then_inc(s["down_done"], 1)

            def body(u, j, i, has_rows, has_up, has_down):
                if has_rows:
                    rows(u + 2, j + (i + 2) // (2 * B), (i + 2) % (2 * B))
                if has_up:
                    up(u + 1, (i + 1) % (2 * B))
                if has_down:
                    down(u, j, i)

            steps(pe, body)

        @block.scalar
        def _(act):
            def body(u, j, i, has_rows, has_up, has_down):
                if has_rows:
                    v, iv = u + 2, (i + 2) % 2
                    need(act, s["rows_done"], v + 1)
                    need(act, s["up_done"], v - 1)
                    act.activation(mix_high[iv][:], mix_bank[iv][:], ACT.Copy).then_inc(s["mix_high_done"], 1)
                if has_up:
                    v, i = u + 1, (i + 1) % (2 * B)
                    need(act, s["up_done"], v + 1)
                    need(act, s["down_done"], v - 1)
                    for k in range(2):
                        act.activation(hid[i % 2][:, k, :], hid_bank[i % 2][:, k, :], ACT.Gelu,
                                       bias=wt["b1"][:, k:k + 1]).then_inc(s["hid_done"], 1)
                        need(act, s["hid_done"], v * 2 + k + 1)
                        act.activation(hid_high[i % 2][:, k, :], hid[i % 2][:, k, :],
                                       ACT.Copy).then_inc(s["hid_high_done"], 1)

            act.activation(w1_high[:], wt["w1"][:], ACT.Copy)
            act.activation(w2_high[:], wt["w2"][:], ACT.Copy).then_inc(s["w_high_done"], 1)
            steps(act, body)

        @block.vector
        def _(dve):
            def body(u, j, i, has_rows, has_up, has_down):
                if has_rows:
                    v, iv = u + 2, (i + 2) % (2 * B)
                    need(dve, s["mix_high_done"], v + 1)
                    dve.tensor_tensor(mix_low[iv % 2][:], mix_bank[iv % 2][:], mix_high[iv % 2][:].bitcast(F32),
                                      ALU.subtract).then_inc(s["mix_low_done"], 1)
                if has_up:
                    v, iv = u + 1, (i + 1) % 2
                    for k in range(2):
                        need(dve, s["hid_high_done"], v * 2 + k + 1)
                        dve.tensor_tensor(hid_low[iv][:, k, :], hid[iv][:, k, :], hid_high[iv][:, k, :].bitcast(F32),
                                          ALU.subtract).then_inc(s["hid_low_done"], 1)
                if has_down:
                    need(dve, s["down_done"], u + 1)
                    need(dve, res_stored[i % 2], (j * B + i // 2) * 16)
                    dve.tensor_scalar(res[i % 2][:], res_bank[i % 2][:], wt["b2"][:, 0:1], None,
                                      ALU.add).then_inc(s["res_done"], 1)

            dve.wait_ge(s["w_high_done"], 1)
            for low, high, w in ((w1_low, w1_high, "w1"), (w2_low, w2_high, "w2")):
                dve.tensor_tensor(low[:], wt[w][:], high[:].bitcast(F32), ALU.subtract).then_inc(s["w_low_done"], 1)
            steps(dve, body)


_INS = {
    "x": "x", "ln_g": "L0_conv_ln_g", "ln_b": "L0_conv_ln_b", "W_in": "L0_conv_W_in", "b_in": "L0_conv_b_in",
    "conv_w": "L0_conv_conv_w", "conv_b": "L0_conv_conv_b", "W_x": "L0_conv_W_x", "dt_w": "L0_conv_dt_w",
    "dt_b": "L0_conv_dt_b", "A_log": "L0_conv_A_log", "D": "L0_conv_D", "W_out": "L0_conv_W_out",
    "b_out": "L0_conv_b_out", "Phi_f_real": "L1_conv_Phi_f_real", "Phi_f_imag": "L1_conv_Phi_f_imag",
    "Theta": "L1_conv_Theta", "ln_gamma": "L1_conv_ln_gamma", "ln_beta": "L1_conv_ln_beta",
    "W1": "L1_conv_W1", "b1": "L1_conv_b1", "W2": "L1_conv_W2", "b2": "L1_conv_b2",
}


def transforms():
    n = np.arange(P)
    angle = 2 * np.pi * (np.outer(n, n) % P) / P
    c, s = np.cos(angle), np.sin(angle)
    fy = np.concatenate([c[:, :KY], -s[:, 1:KY - 1]], axis=1)
    fx = np.stack([c, -s, s, c], axis=1)
    ix = np.stack([c, s, -s], axis=1)
    once = np.where((n[:KY] == 0) | (n[:KY] == KY - 1), 1.0, 2.0)[:, None]
    iy = np.concatenate([once * c[:KY], -2 * s[1:KY - 1]], axis=0) / (H * W)
    return {k: np.ascontiguousarray(v, dtype=np.float32) for k, v in dict(fy=fy, fx=fx, ix=ix, iy=iy).items()}


def kernel(**inputs):
    import concourse.bacc as _bacc
    from concourse.bass_utils import run_bass_kernel_spmd as _run

    nc = _bacc.Bacc("TRN2", target_bir_lowering=False, num_devices=1)
    arrays, args = {}, {}
    given = {k: np.ascontiguousarray(inputs[v]) for k, v in _INS.items()}
    for name, v in {**given, **transforms()}.items():
        arrays[f"in_{name}_dram"] = v
        args[name] = nc.dram_tensor(f"in_{name}_dram", v.shape, mybir.dt.from_np(v.dtype), kind="ExternalInput").ap()
    out = nc.dram_tensor("out_0_dram", (B, C, H, W), F32, kind="ExternalOutput").ap()
    conv_seq_program(nc, args, out)
    r = _run(nc, [arrays], core_ids=[0])
    return r.results[0]["out_0_dram"]
```
